# Optimizing a Trainium2 kernel written in Bass

```python
import numpy as np
import jax
import jax.numpy as jnp

def _softmax(x, axis=-1):
    return jax.nn.softmax(x, axis=axis)

def _gelu(x):
    return jax.nn.gelu(x, approximate=True)

def _silu(x):
    return jax.nn.silu(x)

def _sigmoid(x):
    return jax.nn.sigmoid(x)

def _layernorm(x, axis=-1, eps=1e-05):
    m = jnp.mean(x, axis=axis, keepdims=True)
    v = jnp.var(x, axis=axis, keepdims=True)
    return (x - m) / jnp.sqrt(v + eps)

def _scatter_add(tgt, idx, src, axis=0):
    return tgt.at[idx].add(src)

def _segment_sum(src, seg, n):
    return jax.ops.segment_sum(src, seg, n)
kernel_name = 'mk_gps_d1_gnn_r8_9958db'

def setup_inputs(seed: int=0):
    np.random.seed(seed)
    _w = jnp.asarray

    def _rec_inputs():
        import jax
        import jax.numpy as jnp
        _gk = jax.random.key(seed)
        x = -0.0001126 + 1 * jax.random.normal(jax.random.fold_in(_gk, 1), (1250, 768), jnp.float32)
        _s = jax.random.randint(jax.random.fold_in(_gk, 2), (10000,), 0, 1250, jnp.int32)
        _d = jax.random.randint(jax.random.fold_in(_gk, 3), (10000,), 0, 1250, jnp.int32)
        _loop = jnp.arange(1250, dtype=jnp.int32)
        src = jnp.concatenate([_s, _d, _loop])
        dst = jnp.concatenate([_d, _s, _loop])
        _o = jnp.argsort(dst, stable=True)
        src = src[_o]
        dst = dst[_o]
        edge_weight1 = -0.00472126 + 0.997171 * jax.random.normal(jax.random.fold_in(_gk, 13), (21250, 1), jnp.float32)
        return (x, src, dst, edge_weight1)
    x, src, dst, edge_weight1 = _rec_inputs()

    def _L0_gnn_setup():
        import jax, jax.numpy as jnp
        import numpy as np
        N, E, D, H, C = (1250, 12500, 768, 4, 192)
        NEG_SLOPE = 0.2

        def gat_conv(x, src, dst, W, a_src, a_dst, b):
            h = (x @ W).reshape(N, H, C)
            as_n = (h * a_src).sum(-1)
            ad_n = (h * a_dst).sum(-1)
            e = jax.nn.leaky_relu(as_n[src] + ad_n[dst], NEG_SLOPE)
            m = jax.ops.segment_max(e, dst, num_segments=N)
            p = jnp.exp(e - m[dst])
            s = jax.ops.segment_sum(p, dst, num_segments=N)
            alpha = p / (s[dst] + 1e-16)
            out = jax.ops.segment_sum(alpha[:, :, None] * h[src], dst, num_segments=N)
            return out.reshape(N, H * C) + b
        key = jax.random.key(seed)
        ks = jax.random.split(key, 16)
        w = lambda k, shape: jax.random.normal(k, shape, dtype=jnp.float32) * 0.02
        inp = {}
        inp['x'] = jax.random.normal(ks[0], (N, D), dtype=jnp.float32)
        inp['edge_index'] = jax.random.randint(ks[1], (2, E), 0, N, dtype=jnp.int32)
        inp['batch'] = jnp.zeros((N,), dtype=jnp.int32)
        inp['edge_attr'] = jax.random.normal(ks[2], (E, 1), dtype=jnp.float32)
        inp['W_ah'] = w(ks[3], (D, D))
        inp['b_ah'] = jnp.zeros((D,), jnp.float32)
        for i in range(3):
            inp[f'W{i}'] = w(ks[4 + 3 * i], (D, H * C))
            inp[f'a_src{i}'] = w(ks[5 + 3 * i], (H, C))
            inp[f'a_dst{i}'] = w(ks[6 + 3 * i], (H, C))
            inp[f'b{i}'] = jnp.zeros((H * C,), jnp.float32)
        inp['W_out'] = w(ks[13], (3 * D, D))
        inp['b_out'] = jnp.zeros((D,), jnp.float32)
        return inp
    _L0_gnn_all = _L0_gnn_setup()
    _L0_gnn_in = {k: v for k, v in _L0_gnn_all.items() if k in ('W_ah', 'b_ah', 'W0', 'a_src0', 'a_dst0', 'b0', 'W1', 'a_src1', 'a_dst1', 'b1', 'W2', 'a_src2', 'a_dst2', 'b2', 'W_out', 'b_out')}
    del _L0_gnn_all

    def _L0_mix_setup():
        import jax, jax.numpy as jnp
        import numpy as np
        NUM_HEADS = 12
        EPS = 0.0001

        def softmax_kernel(data, proj, is_query):
            d = data.shape[-1]
            data_normalizer = d ** (-0.25)
            ratio = proj.shape[0] ** (-0.5)
            data_dash = jnp.einsum('bhnd,md->bhnm', data_normalizer * data, proj)
            diag = jnp.sum(data * data, axis=-1, keepdims=True) * 0.5 * data_normalizer ** 2
            if is_query:
                m = jnp.max(data_dash, axis=-1, keepdims=True)
            else:
                m = jnp.max(data_dash, axis=(-3, -2, -1), keepdims=True)
            return ratio * (jnp.exp(data_dash - diag - m) + EPS)
        key = jax.random.key(seed)
        ks = jax.random.split(key, 5)
        B, N, C = (8, 512, 768)
        x = jax.random.normal(ks[0], (B, N, C), dtype=jnp.float32)
        w_qkv = jax.random.normal(ks[1], (3 * C, C), dtype=jnp.float32) * 0.02
        w_proj = jax.random.normal(ks[2], (C, C), dtype=jnp.float32) * 0.02
        b_proj = jnp.zeros((C,), dtype=jnp.float32)
        proj_mat = jax.random.normal(ks[3], (256, C // NUM_HEADS), dtype=jnp.float32)
        return {'x': x, 'w_qkv': w_qkv, 'w_proj': w_proj, 'b_proj': b_proj, 'proj_mat': proj_mat}
    _L0_mix_all = _L0_mix_setup()
    _L0_mix_in = {k: v for k, v in _L0_mix_all.items() if k in ('w_qkv', 'w_proj', 'b_proj', 'proj_mat')}
    del _L0_mix_all

    def _L0_ffn_setup():
        import jax, jax.numpy as jnp
        import numpy as np
        CAPACITY_FACTOR = 1.25
        key = jax.random.key(seed)
        ks = jax.random.split(key, 5)
        B, S, D, F, E = (8, 256, 768, 384, 8)
        return {'x': jax.random.normal(ks[0], (B, S, D), jnp.float32), 'switch_w': jax.random.normal(ks[1], (D, E), jnp.float32) * 0.02, 'switch_b': jnp.zeros((E,), jnp.float32), 'w1': jax.random.normal(ks[2], (E, D, F), jnp.float32) * 0.02, 'b1': jnp.zeros((E, F), jnp.float32), 'w2': jax.random.normal(ks[3], (E, F, D), jnp.float32) * 0.02, 'b2': jnp.zeros((E, D), jnp.float32)}
    _L0_ffn_all = _L0_ffn_setup()
    _L0_ffn_in = {k: v for k, v in _L0_ffn_all.items() if k in ('switch_w', 'switch_b', 'w1', 'b1', 'w2', 'b2')}
    del _L0_ffn_all
    return {'x': x, 'src': src, 'dst': dst, 'edge_weight1': edge_weight1, 'L0_gnn_W_ah': _L0_gnn_in['W_ah'], 'L0_gnn_b_ah': _L0_gnn_in['b_ah'], 'L0_gnn_W0': _L0_gnn_in['W0'], 'L0_gnn_a_src0': _L0_gnn_in['a_src0'], 'L0_gnn_a_dst0': _L0_gnn_in['a_dst0'], 'L0_gnn_b0': _L0_gnn_in['b0'], 'L0_gnn_W1': _L0_gnn_in['W1'], 'L0_gnn_a_src1': _L0_gnn_in['a_src1'], 'L0_gnn_a_dst1': _L0_gnn_in['a_dst1'], 'L0_gnn_b1': _L0_gnn_in['b1'], 'L0_gnn_W2': _L0_gnn_in['W2'], 'L0_gnn_a_src2': _L0_gnn_in['a_src2'], 'L0_gnn_a_dst2': _L0_gnn_in['a_dst2'], 'L0_gnn_b2': _L0_gnn_in['b2'], 'L0_gnn_W_out': _L0_gnn_in['W_out'], 'L0_gnn_b_out': _L0_gnn_in['b_out'], 'L0_mix_w_qkv': _L0_mix_in['w_qkv'], 'L0_mix_w_proj': _L0_mix_in['w_proj'], 'L0_mix_b_proj': _L0_mix_in['b_proj'], 'L0_mix_proj_mat': _L0_mix_in['proj_mat'], 'L0_ffn_switch_w': _L0_ffn_in['switch_w'], 'L0_ffn_switch_b': _L0_ffn_in['switch_b'], 'L0_ffn_w1': _L0_ffn_in['w1'], 'L0_ffn_b1': _L0_ffn_in['b1'], 'L0_ffn_w2': _L0_ffn_in['w2'], 'L0_ffn_b2': _L0_ffn_in['b2']}

def reference(x, src, dst, edge_weight1, L0_gnn_W_ah, L0_gnn_b_ah, L0_gnn_W0, L0_gnn_a_src0, L0_gnn_a_dst0, L0_gnn_b0, L0_gnn_W1, L0_gnn_a_src1, L0_gnn_a_dst1, L0_gnn_b1, L0_gnn_W2, L0_gnn_a_src2, L0_gnn_a_dst2, L0_gnn_b2, L0_gnn_W_out, L0_gnn_b_out, L0_mix_w_qkv, L0_mix_w_proj, L0_mix_b_proj, L0_mix_proj_mat, L0_ffn_switch_w, L0_ffn_switch_b, L0_ffn_w1, L0_ffn_b1, L0_ffn_w2, L0_ffn_b2):
    import jax
    import jax.numpy as jnp

    def _L0_gnn_ref(x, edge_index, batch, edge_attr, W_ah, b_ah, W0, a_src0, a_dst0, b0, W1, a_src1, a_dst1, b1, W2, a_src2, a_dst2, b2, W_out, b_out):
        import jax, jax.numpy as jnp
        import numpy as np
        N, E, D, H, C = (1250, 12500, 768, 4, 192)
        NEG_SLOPE = 0.2

        def gat_conv(x, src, dst, W, a_src, a_dst, b):
            h = (x @ W).reshape(N, H, C)
            as_n = (h * a_src).sum(-1)
            ad_n = (h * a_dst).sum(-1)
            e = jax.nn.leaky_relu(as_n[src] + ad_n[dst], NEG_SLOPE)
            m = jax.ops.segment_max(e, dst, num_segments=N)
            p = jnp.exp(e - m[dst])
            s = jax.ops.segment_sum(p, dst, num_segments=N)
            alpha = p / (s[dst] + 1e-16)
            out = jax.ops.segment_sum(alpha[:, :, None] * h[src], dst, num_segments=N)
            return out.reshape(N, H * C) + b
        loops = jnp.arange(N, dtype=edge_index.dtype)
        src = jnp.concatenate([edge_index[0], loops])
        dst = jnp.concatenate([edge_index[1], loops])
        x1 = jax.nn.relu(x @ W_ah + b_ah)
        xs = [jax.nn.relu(gat_conv(x1, src, dst, W, a_s, a_d, b)) for W, a_s, a_d, b in ((W0, a_src0, a_dst0, b0), (W1, a_src1, a_dst1, b1), (W2, a_src2, a_dst2, b2))]
        node_emb = jnp.concatenate(xs, axis=1)
        return jax.nn.relu(node_emb @ W_out + b_out)

    def _L0_mix_ref(x, w_qkv, w_proj, b_proj, proj_mat):
        import jax, jax.numpy as jnp
        import numpy as np
        NUM_HEADS = 12
        EPS = 0.0001

        def softmax_kernel(data, proj, is_query):
            d = data.shape[-1]
            data_normalizer = d ** (-0.25)
            ratio = proj.shape[0] ** (-0.5)
            data_dash = jnp.einsum('bhnd,md->bhnm', data_normalizer * data, proj)
            diag = jnp.sum(data * data, axis=-1, keepdims=True) * 0.5 * data_normalizer ** 2
            if is_query:
                m = jnp.max(data_dash, axis=-1, keepdims=True)
            else:
                m = jnp.max(data_dash, axis=(-3, -2, -1), keepdims=True)
            return ratio * (jnp.exp(data_dash - diag - m) + EPS)
        B, N, C = x.shape
        H = NUM_HEADS
        d = C // H
        qkv = (x @ w_qkv.T).reshape(B, N, 3, H, d).transpose(2, 0, 3, 1, 4)
        q, k, v = (qkv[0], qkv[1], qkv[2])
        q_prime = softmax_kernel(q, proj_mat, is_query=True)
        k_prime = softmax_kernel(k, proj_mat, is_query=False)
        k_sum = jnp.sum(k_prime, axis=-2)
        d_inv = 1.0 / jnp.einsum('bhnm,bhm->bhn', q_prime, k_sum)
        context = jnp.einsum('bhnm,bhnd->bhmd', k_prime, v)
        out = jnp.einsum('bhnm,bhmd,bhn->bhnd', q_prime, context, d_inv)
        out = out.transpose(0, 2, 1, 3).reshape(B, N, C)
        return out @ w_proj.T + b_proj

    def _L0_ffn_ref(x, switch_w, switch_b, w1, b1, w2, b2):
        import jax, jax.numpy as jnp
        import numpy as np
        CAPACITY_FACTOR = 1.25
        B, S, D = x.shape
        E = w1.shape[0]
        xf = x.reshape(-1, D)
        N = xf.shape[0]
        capacity = int(CAPACITY_FACTOR * N / E)
        probs = jax.nn.softmax(xf @ switch_w + switch_b, axis=-1)
        prob_max = jnp.max(probs, axis=-1)
        routes = jnp.argmax(probs, axis=-1)
        sort_idx = jnp.lexsort((-prob_max, routes))
        counts = jnp.bincount(routes, length=E)
        starts = jnp.concatenate([jnp.zeros((1,), counts.dtype), jnp.cumsum(counts)[:-1]])
        rank_sorted = jnp.arange(N) - starts[routes[sort_idx]]
        rank = jnp.zeros((N,), jnp.int32).at[sort_idx].set(rank_sorted.astype(jnp.int32))
        keep = rank < capacity
        dest_e = jnp.where(keep, routes, E)
        dest_c = jnp.where(keep, rank, 0)
        buf = jnp.zeros((E + 1, capacity, D), xf.dtype).at[dest_e, dest_c].set(xf)
        h = jax.nn.gelu(jnp.einsum('ecd,edf->ecf', buf[:E], w1) + b1[:, None, :], approximate=False)
        o = jnp.einsum('ecf,efd->ecd', h, w2) + b2[:, None, :]
        y_exp = o[routes, dest_c]
        y = jnp.where(keep[:, None], y_exp, xf)
        out = y * prob_max[:, None]
        return out.reshape(B, S, D)
    edge_index = jnp.stack([src, dst])
    batch0 = jnp.zeros((1250,), jnp.int32)
    xn = _layernorm(x, axis=-1)
    x = x + _L0_gnn_ref(xn, edge_index, batch0, edge_weight1, L0_gnn_W_ah, L0_gnn_b_ah, L0_gnn_W0, L0_gnn_a_src0, L0_gnn_a_dst0, L0_gnn_b0, L0_gnn_W1, L0_gnn_a_src1, L0_gnn_a_dst1, L0_gnn_b1, L0_gnn_W2, L0_gnn_a_src2, L0_gnn_a_dst2, L0_gnn_b2, L0_gnn_W_out, L0_gnn_b_out) + _L0_mix_ref(xn[None], L0_mix_w_qkv, L0_mix_w_proj, L0_mix_b_proj, L0_mix_proj_mat)[0]
    x = x + _L0_ffn_ref(_layernorm(x, axis=-1)[None], L0_ffn_switch_w, L0_ffn_switch_b, L0_ffn_w1, L0_ffn_b1, L0_ffn_w2, L0_ffn_b2)[0]
    return x

_drawn_inputs = setup_inputs


def setup_inputs(seed=0):
    import zlib

    import numpy as np

    out = dict(_drawn_inputs(seed))
    spreads = {'L0_gnn_b_ah': (0.0, 0.382),
     'L0_gnn_b0': (0.0, 0.1),
     'L0_gnn_b1': (0.0, 0.1),
     'L0_gnn_b2': (0.0, 0.274),
     'L0_gnn_b_out': (0.0, 0.1),
     'L0_mix_b_proj': (0.0, 0.1),
     'L0_ffn_switch_b': (0.0, 0.269),
     'L0_ffn_b1': (0.0, 0.8),
     'L0_ffn_b2': (0.0, 0.317)}
    factors = {'L0_gnn_a_src0': 35.457,
     'L0_gnn_a_dst0': 52.97,
     'L0_gnn_a_src1': 40.818,
     'L0_gnn_a_dst1': 64.0,
     'L0_gnn_a_src2': 34.138,
     'L0_gnn_a_dst2': 64.0,
     'L0_mix_w_qkv': 3.774,
     'L0_mix_w_proj': 4.498,
     'L0_mix_proj_mat': 64.0}
    for name, (base, spread) in spreads.items():
        noise = np.random.default_rng([zlib.crc32(name.encode()), seed]).standard_normal(out[name].shape)
        drawn = base * np.exp(spread * noise) if base else spread * noise
        out[name] = jnp.asarray(drawn.astype(out[name].dtype))
    for name, factor in factors.items():
        out[name] = (out[name] * factor).astype(out[name].dtype)
    return out
```

```python
from contextlib import ExitStack
from functools import partial

import numpy as np

import concourse.bass as bass
from concourse import mybir

ALU = mybir.AluOpType
ACT = mybir.ActivationFunctionType
AX = mybir.AxisListType
F32 = mybir.dt.float32
BF16 = mybir.dt.bfloat16
I32 = mybir.dt.int32
U32 = mybir.dt.uint32
U16 = mybir.dt.uint16

PE, DVE, SCAL, POOL, SYNC = "tensor", "vector", "scalar", "gpsimd", "sync"

BLOCKS = {PE: lambda b, f: b.tensor(f), DVE: lambda b, f: b.vector(f), SCAL: lambda b, f: b.scalar(f),
          POOL: lambda b, f: b.gpsimd(f), SYNC: lambda b, f: b.sync(f)}

N, D, E = 1250, 768, 21250
P = 125
NT = N // P
KD = D // 128
LAYERS, GH, GC = 3, 4, 192
LH = LAYERS * GH
SLOPE = 0.2
LN_EPS = 1e-5
SOFTMAX_EPS = 1e-16
HEADS, HD, FEATS = 12, 64, 256
PAIRS = HEADS // 2
MT = FEATS // 128
NORM = HD ** -0.25
RATIO = FEATS ** -0.5
EPS = 1e-4
EXPERTS, F = 8, 384
KF = F // 128
CAP = int(1.25 * N / EXPERTS)
SLOTS = EXPERTS * CAP
CHUNKS = E // P
TABLES = 2
PIECES = 10
CP = CHUNKS // PIECES
HW = 2 * (GC + 2)
BIG = 3e38
LATER = 1024.0
COLS = [(0, 500), (500, 1000), (1000, 1250)]


class Lanes:

    def __init__(self, nc, ctx):
        self.nc, self.ctx = nc, ctx
        self.dma = {SYNC: nc.sync.dma_start, SCAL: nc.scalar.dma_start, POOL: nc.gpsimd.dma_start}
        self.queues = {e: [] for e in (PE, DVE, SCAL, POOL, SYNC)}
        self.count, self.owner, self.sems = {}, {}, {}
        self.stores = {}

    def put(self, engine, issue, after=(), signal=None, by=1):
        self.queues[engine].append((tuple(t for t in after if t), issue, signal, by))
        if signal is None:
            return None
        if signal not in self.sems:
            self.sems[signal] = self.ctx.enter_context(self.nc.semaphore(signal))
            self.count[signal], self.owner[signal] = 0, engine
        assert self.owner[signal] == engine, signal
        self.count[signal] += by
        return signal, self.count[signal]

    def pe(self, issue, after=(), signal=None):
        return self.put(PE, issue, after, signal)

    def dve(self, issue, after=(), signal=None):
        return self.put(DVE, issue, after, signal)

    def act(self, issue, after=(), signal=None):
        return self.put(SCAL, issue, after, signal)

    def pool(self, issue, after=(), signal=None):
        return self.put(POOL, issue, after, signal)

    def load(self, dst, src, after=(), signal=None, engine=SYNC):
        return self.put(engine, partial(self.dma[engine], dst, src), after, signal, 16)

    def store(self, dst, src, after=(), signal=None, engine=SYNC):
        token = self.put(engine, partial(self.dma[engine], dst, src), after, signal, 16)
        self.stores[token[0]] = token
        return token

    def emit(self, block):
        for name, queue in self.queues.items():
            def instructions(eng, queue=queue):
                passed = {}
                for after, issue, signal, by in queue:
                    for sem, value in after:
                        if passed.get(sem, 0) < value:
                            eng.wait_ge(self.sems[sem], value)
                            passed[sem] = value
                    ins = issue() if issue else None
                    if signal:
                        ins.then_inc(self.sems[signal], by)
            BLOCKS[name](block, instructions)


class Ring:

    def __init__(self, buffers):
        self.buffers, self.free, self.n = buffers, [() for _ in buffers], 0
        self.held = [False] * len(buffers)

    def take(self):
        i = self.n % len(self.buffers)
        self.n += 1
        assert not self.held[i], "the ring is too short"
        self.held[i] = True
        return i, self.buffers[i], self.free[i]

    def give(self, i, *tokens):
        self.free[i], self.held[i] = tokens, False


def in_step(stages, n):
    for i in range(n + max(lag for lag, _ in stages)):
        for lag, step in stages:
            if 0 <= i - lag < n:
                step(i - lag)
        yield


def run(*tracks):
    live = [[g, w] for g, w in tracks]
    while live:
        for item in list(live):
            for _ in range(item[1]):
                try:
                    next(item[0])
                except StopIteration:
                    live.remove(item)
                    break


def program(nc, x, src_rows, dst_rows, src_cols, dst_cols, W_ah, b_ah, Wg, a_src, a_dst, bg, W_out, b_out,
            wT_qkv, wT_proj, b_proj, projT, switch_w, switch_b, w1, b1_cols, w2, b2, out):
    ctx = ExitStack()
    with ctx:
        L = Lanes(nc, ctx)
        T, V, A, G = nc.tensor, nc.vector, nc.scalar, nc.gpsimd

        def sb(stack, name, shape, dt=F32):
            return stack.enter_context(nc.sbuf_tensor(name, shape, dt))

        def dram(name, shape, dt=F32):
            return nc.dram_tensor(name, shape, dt).ap()

        bank = [ctx.enter_context(nc.psum_tensor(f"bank{i}", [128, 512], F32)) for i in range(8)]

        key_rows = dram("key_rows", (E,))
        tables = [dram(f"table{i}", (N * N + P, 1)) for i in range(TABLES)]
        h_rows = dram("h_rows", (LAYERS, N, GH, HW), BF16)
        as_rows = dram("as_rows", (8 * LAYERS, N))
        shift_rows = dram("shift_rows", (2 * LH, N))
        node_rows = dram("node_rows", (N, LAYERS * D))
        mixed_rows = dram("mixed_rows", (N, D))
        attn_rows = dram("attn_rows", (N, D))
        slot_rows = dram("slot_rows", (SLOTS + N, D))
        expert_rows = dram("expert_rows", (SLOTS, D))
        route_rows = dram("route_rows", (2, N))

        ident = sb(ctx, "ident", [128, 128])
        zero = sb(ctx, "zero", [128, 1250])
        ones = sb(ctx, "ones", [128, 128])
        halves = sb(ctx, "halves", [128, 2])
        t_zero = L.dve(partial(V.memset, zero[:, :], 0.0), (), "zero_set")
        t_ones = L.dve(partial(V.memset, ones[:, :], 1.0), (), "ones_set")
        t = L.pool(partial(G.memset, ident[:, :], 0.0), (), "consts")
        t = L.pool(partial(G.affine_select, out=ident[:, :], in_=ident[:, :], compare_op=ALU.not_equal, fill=1.0,
                                             base=0, pattern=[[-1, 128]], channel_multiplier=1), (t,), "consts")
        t_ident = t
        t = L.pool(partial(G.memset, halves[:, :], 1.0), (), "consts")
        t = L.pool(partial(G.affine_select, out=halves[:, 0:1], in_=halves[:, 0:1], compare_op=ALU.is_ge, fill=0.0,
                                             base=63, pattern=[[0, 1]], channel_multiplier=-1), (t,), "consts")
        t_halves = L.pool(partial(G.affine_select, out=halves[:, 1:2], in_=halves[:, 1:2], compare_op=ALU.is_ge,
                                                    fill=0.0, base=-64, pattern=[[0, 1]], channel_multiplier=1),
                          (t,), "consts")
        identP = ident[0:P, 0:P]

        def split(name, src, hi, lo, after, hi_after=()):
            a = L.act(partial(A.activation, hi, src, ACT.Copy), (*after, *hi_after), "high_part")
            return L.dve(partial(V.tensor_tensor, lo, src, hi, ALU.subtract), (a,), "low_part")

        def product(out_ap, lhs, rhs, first, last, after=(), signal=None, skip=False):
            terms = [(lhs[0], rhs[0]), (lhs[0], rhs[1]), (lhs[1], rhs[0])]
            token = None
            for n, (l, r) in enumerate(terms):
                token = L.pe(partial(T.matmul, out_ap, l, r, start=first and n == 0,
                                                               stop=last and n == 2, skip_group_check=skip),
                             after if n == 0 else (), signal if n == 2 else None)
            return token

        def load_split(name, stage, pieces, after=()):
            tokens = []
            for d, hi, lo in pieces:
                i, buf, free = stage.take()
                v = buf[0:d.shape[0], 0:d.shape[1]]
                got = L.load(v, d, free, f"w_in{i}")
                done = split(name, v, hi, lo, (got, *after))
                stage.give(i, done)
                tokens.append(done)
            return tokens

        def transposed(name, src, blocks, dst_hi, dst_lo, banks, after, relu=False):
            done, freed = None, None
            for g in range(blocks // 3):
                i, b, free = banks.take()
                for k in range(3):
                    kk = 3 * g + k
                    turned = L.pe(partial(T.transpose, b[:, k * P:(k + 1) * P],
                                                                         src[:, kk * 128:(kk + 1) * 128], identP),
                                  (*free, *after, t_ident) if k == 0 else (), "turned" if k == 2 else None)
                ps = b[:, 0:3 * P].rearrange("p (k n) -> p k n", k=3)
                hi, lo = dst_hi[:, 3 * g:3 * g + 3, :], dst_lo[:, 3 * g:3 * g + 3, :]
                fn = ACT.Relu if relu else ACT.Copy
                a = L.act(partial(A.activation, hi, ps, fn), (turned,), "turned_high")
                if relu:
                    done = L.dve(partial(V.scalar_tensor_tensor, lo, ps, 0.0, hi, ALU.max, ALU.subtract), (a,), "turned_low")
                else:
                    done = L.dve(partial(V.tensor_tensor, lo, ps, hi, ALU.subtract),
                                 (a,), "turned_low")
                banks.give(i, done)
            return done, turned

        def row_stats(xin, st, after):
            L.dve(partial(V.bn_stats, st[:, 0:6], xin[:, 0:D // 2]), after, "normed")
            a = L.dve(partial(V.bn_stats, st[:, 6:12], xin[:, D // 2:D]), (), "normed")
            return L.dve(partial(V.bn_aggr, st[:, 12:14], st[:, 0:12]), (a,), "normed")

        def inverse_root(st, after):
            v, r, u = st[:, :, 13], st[:, :, 14], st[:, :, 15]
            a = L.dve(partial(V.tensor_scalar, v, v, LN_EPS, None, ALU.add), after, "rstd")
            a = L.act(partial(A.activation, u, v, ACT.Sqrt), (a,), "root")
            a = L.dve(partial(V.reciprocal, r, u), (a,), "rstd")
            a = L.dve(partial(V.tensor_tensor, u, v, r, ALU.mult), (a,), "rstd")
            a = L.dve(partial(V.tensor_tensor, u, u, r, ALU.mult), (a,), "rstd")
            a = L.dve(partial(V.tensor_scalar, u, u, -0.5, 1.5, ALU.mult, ALU.add), (a,), "rstd")
            return L.dve(partial(V.tensor_tensor, r, r, u, ALU.mult), (a,), "rstd")

        def normalise(xin, xout, st, after):
            return L.dve(partial(V.tensor_scalar, xout, xin, st[:, 12:13], st[:, 14:15], ALU.subtract, ALU.mult),
                         after, "normed")

        def fence():
            return tuple((s, c) for s, c in L.count.items())

        asd = sb(ctx, "asd", [P, NT, 8 * LAYERS])
        as_low = sb(ctx, "as_low", [P, NT, LH])
        s0 = ExitStack()
        xnT = [sb(s0, f"xnT_{p}", [128, KD, N], BF16) for p in ("hi", "lo")]
        late = ExitStack()
        s1 = ExitStack()
        x1T = [sb(s1, f"x1T_{p}", [128, KD, N], BF16) for p in ("hi", "lo")]
        wide = D + 8
        w_ring = Ring([[sb(s1, f"w{i}_{p}", [128, KD, wide], BF16) for p in ("hi", "lo")] for i in range(2)])
        stage = Ring([sb(s1, f"stage{i}", [128, wide]) for i in range(3)])
        all_banks = Ring(bank[0:8])

        cols = [sb(s1, f"edge_cols{i}", [P, CHUNKS], I32) for i in range(2)]
        rows = [sb(s1, f"edge_rows{i}", [P, CHUNKS], I32) for i in range(2)]
        key_c, key_r = sb(s1, "key_c", [P, CHUNKS]), sb(s1, "key_r", [P, CHUNKS])
        spread = [sb(s1, f"spread{i}", [P, CP * P]) for i in range(2)]
        same = [sb(s1, f"same{i}", [P, P]) for i in range(2)]
        later = sb(s1, "later", [P, P])
        amount = sb(s1, "amount", [P, CHUNKS])
        spare_i = sb(s1, "spare_i", [P, 1], I32)
        spare = sb(s1, "spare", [P, 1])
        moved = sb(s1, "moved", [P, CHUNKS])
        place = sb(s1, "place", [P, CHUNKS], U32)

        def edges():
            got_r = [L.load(rows[i][:, :], d.rearrange("(a b) -> a b", a=P), (), "edge_rows_in")
                     for i, d in enumerate((src_rows, dst_rows))]
            got_c = [L.load(cols[i][:, :], d, (), "edge_cols_in") for i, d in enumerate((src_cols, dst_cols))]
            for i in range(TABLES):
                L.store(tables[i][0:N * N, :].rearrange("(t p n) o -> p t (n o)", p=P, t=NT),
                        zero[0:P, :].unsqueeze(1).broadcast_to([P, NT, N]), (t_zero,), "table_zero", SCAL)
                L.store(tables[i][N * N:, :], zero[0:P, 0:1], (), "table_zero", SCAL)
            kr = L.dve(partial(V.scalar_tensor_tensor, key_r[:, :], rows[0][:, :], float(N), rows[1][:, :],
                                                        ALU.mult, ALU.add), got_r[1:], "keys")
            kc = L.dve(partial(V.scalar_tensor_tensor, key_c[:, :], cols[0][:, :], float(N), cols[1][:, :],
                                                        ALU.mult, ALU.add), got_c[1:], "keys")
            kept = L.store(key_rows.rearrange("(a b) -> a b", a=P), key_r[:, :], (kr,), "key_rows_out")
            t = L.pool(partial(G.memset, later[:, :], 1.0), (), "edge_consts")
            t = L.pool(partial(G.affine_select, out=later[:, :], in_=later[:, :], compare_op=ALU.is_ge, fill=LATER,
                                                 base=0, pattern=[[1, P]], channel_multiplier=-1),
                       (t,), "edge_consts")
            t = L.pool(partial(G.iota, spare_i[:, :], pattern=[[0, 1]], base=N * N, channel_multiplier=1),
                       (t,), "edge_consts")
            t_sp = L.dve(partial(V.tensor_copy, spare[:, :], spare_i[:, :]), (t,), "keys")
            read = [(), ()]
            yield
            for q in range(PIECES):
                got = L.load(spread[q % 2][:, :],
                             key_rows[q * CP * P:(q + 1) * CP * P].partition_broadcast(P),
                             (kept, *read[q % 2]), f"spread_in{q % 2}")
                for j in range(CP):
                    c = q * CP + j
                    a = L.dve(partial(V.scalar_tensor_tensor, same[c % 2][:, :], spread[q % 2][:, j * P:(j + 1) * P], key_c[:, c:c + 1], later[:, :],
                        ALU.is_equal, ALU.mult, accum_out=amount[:, c:c + 1]),
                        (got, t_sp, ("same_key", c - 1) if c >= 2 else None), "same_key")
                read[q % 2] = (a,)
                cs = slice(q * CP, (q + 1) * CP)
                b = L.dve(partial(V.tensor_scalar, moved[:, cs], key_c[:, cs], spare[:, 0:1], None,
                                                           ALU.subtract), (a,), "keys")
                b = L.dve(partial(V.scalar_tensor_tensor, moved[:, cs], amount[:, cs], LATER, moved[:, cs],
                                                                  ALU.is_lt, ALU.mult), (b,), "keys")
                b = L.dve(partial(V.tensor_scalar, place[:, cs], moved[:, cs], spare[:, 0:1], None,
                                                           ALU.add), (b,), "keys")
                for c in range(q * CP, (q + 1) * CP):
                    i = c % TABLES
                    before = (f"scatter{i}", 16 * (c // TABLES)) if c >= TABLES else None
                    L.put(POOL, partial(G.indirect_dma_start, tables[i], bass.IndirectOffsetOnAxis(place[:, c:c + 1], axis=0), amount[:, c:c + 1], None,
                        compute_op=ALU.add), (b, L.stores["table_zero"], before), f"scatter{i}", 16)
                yield

        def nodes():
            xs = sb(s1, "xs", [P, NT, D])
            xn = [sb(s1, f"xn{i}", [P, D]) for i in range(2)]
            stats = sb(s1, "stats1", [P, NT, 16])
            b_col = sb(s1, "b_col", [128, KD])
            x1f = [sb(s1, f"x1f{i}", [128, 500]) for i in range(2)]
            b_got = L.load(b_col[:, :], b_ah, (), "bias_in")
            wi, w_ah, _ = w_ring.take()
            ln_done, turned, xn_done = {}, {}, {}
            BATCH = 5
            for t in range(NT):
                L.load(xs[:, t, :], x[t * P:(t + 1) * P, :], (), f"x_in{t // BATCH}")

            def statistics(t0):
                for t in range(t0, t0 + BATCH):
                    a = row_stats(xs[:, t, :], stats[:, t, :], ((f"x_in{t // BATCH}", 16 * BATCH),))
                ln_done[t0] = inverse_root(stats[:, t0:t0 + BATCH, :], (a,))

            def norm(t):
                ln_done["x", t] = normalise(xs[:, t, :], xn[t % 2][:, :], stats[:, t, :],
                                            (ln_done[t - t % BATCH], turned.get(t - 2)))

            def turn(t):
                ts = slice(t * P, (t + 1) * P)
                xn_done[t], turned[t] = transposed("xn", xn[t % 2], KD, xnT[0][:, :, ts], xnT[1][:, :, ts],
                                                   all_banks, (ln_done["x", t],))
            w_done = []
            for t in range(NT + 1):
                if t % BATCH == 0 and t < NT:
                    statistics(t)
                if t < NT:
                    norm(t)
                if t < KD:
                    w_done += load_split("w", stage, [(W_ah[t * 128:(t + 1) * 128, :], w_ah[0][:, t, 0:D],
                                                       w_ah[1][:, t, 0:D])])
                if t:
                    turn(t - 1)
                yield
            x1_done = []
            for m in range(KD):
                ms = slice(m * 128, (m + 1) * 128)
                for c, (c0, c1) in enumerate(COLS):
                    i, b, free = all_banks.take()
                    for k in range(KD):
                        mm = product(b[:, 0:c1 - c0], [w[:, k, ms] for w in w_ah], [v[:, k, c0:c1] for v in xnT],
                                     k == 0, k == KD - 1, (*free, w_done[k], xn_done[NT - 1]),
                                     "x1_mm" if k == KD - 1 else None)
                    n = 3 * m + c
                    f = x1f[n % 2][:, 0:c1 - c0]
                    a = L.act(partial(A.activation, f, b[:, 0:(c1 - c0)], ACT.Relu, bias=b_col[:, m:m + 1]),
                        (mm, b_got, x1_done[n - 2] if n >= 2 else None), "x1_relu")
                    all_banks.give(i, a)
                    x1_done.append(split("x1", f, x1T[0][:, m, c0:c1], x1T[1][:, m, c0:c1], (a,)))
                yield
            w_ring.give(wi, mm)

            a_row = [[sb(s1, f"a_row{i}{j}", [128, D]) for j in range(2)] for i in range(2)]
            wa_tmp = [sb(s1, f"wa_tmp{i}", [128, D]) for i in range(2)]
            h_out = Ring([sb(s1, f"h_out{i}", [P, GH, HW], BF16) for i in range(3)])
            for i, b in enumerate(h_out.buffers):
                t = L.dve(partial(V.memset, b[:, :, :], 0.0), (), "h_out_set")
                t = L.dve(partial(V.memset, b[:, :, GC:GC + 1], 1.0), (t,), "h_out_set")
                h_out.give(i, t)
            state = {"wa": 0}
            asd_done = {}
            h_mm_last = [None] * LAYERS

            def weights(l):
                i, w, w_free = w_ring.take()
                got = [L.load(a_row[l % 2][j][:, :], d[l].rearrange("h c -> (h c)").partition_broadcast(128),
                              (h_mm_last[l - 2],) if l >= 2 else (), f"a_in{l % 2}")
                       for j, d in enumerate((a_src, a_dst))]
                done = []
                for k in range(KD):
                    si, buf, free = stage.take()
                    g = L.load(buf[:, 0:D], Wg[l][k * 128:(k + 1) * 128, :], free, f"w_in{si}")
                    for j in range(2):
                        n = state["wa"]
                        state["wa"] += 1
                        m = L.dve(partial(V.tensor_tensor, wa_tmp[n % 2][:, :], buf[:, 0:D], a_row[l % 2][j][:, :], ALU.mult),
                            (g, got[1], ("wa_sum", n - 1) if n >= 2 else None), "wa_mul")
                        r = L.dve(partial(V.tensor_reduce, buf[:, D + 4 * j:D + 4 * j + 4], wa_tmp[n % 2][:, :].rearrange("p (h c) -> p h c", h=GH),
                            AX.X, ALU.add), (m, *free), "wa_sum")
                    d = split("w", buf[:, :], w[0][:, k, :], w[1][:, k, :], (g, r), w_free)
                    stage.give(si, d)
                    done.append(d)
                return i, w, done

            nxt = weights(0)
            yield
            for l in range(LAYERS):
                wi, w, w_done = nxt
                for t in range(NT):
                    if t == 2 and l + 1 < LAYERS:
                        nxt = weights(l + 1)
                    ts = slice(t * P, (t + 1) * P)
                    oi, o, o_free = h_out.take()
                    his, los = [], []
                    for half in range(2):
                        c0, width = half * (D // 2), D // 2 + 8 * half
                        bi, b, free = all_banks.take()
                        for k in range(KD):
                            mm = product(b[0:P, 0:width], [v[:, k, ts] for v in x1T],
                                         [v[:, k, c0:c0 + width] for v in w], k == 0, k == KD - 1,
                                         (*free, w_done[k], x1_done[-1]), "h_mm" if k == KD - 1 else None)
                        v = b[0:P, 0:D // 2].rearrange("p (h c) -> p h c", h=2)
                        hi, lo = (o[:, 2 * half:2 * half + 2, s:s + GC] for s in (0, HW // 2))
                        d = split("h", v, hi, lo, (mm, *o_free))
                        los.append(d)
                        if half:
                            d2 = L.dve(partial(V.tensor_copy, asd[:, t, 8 * l:8 * l + 8], b[0:P, D // 2:D // 2 + 8]), (mm,), "asd_copy")
                            asd_done[l, t] = d2
                            d = d2
                        all_banks.give(bi, d)
                    s = L.store(h_rows[l, ts, :, :], o[:, :, :], (los[0], los[1]), f"h_out{oi}")
                    h_out.give(oi, s)
                    yield
                h_mm_last[l] = mm
                w_ring.give(wi, mm)
            as_row_sb = xs[0:8 * LAYERS, :, :].rearrange("p t d -> p (t d)")[:, 0:N]
            last = None
            for t in range(NT):
                bi, b, free = all_banks.take()
                tt = L.pe(partial(T.transpose, b[0:8 * LAYERS, 0:P], asd[:, t, :], identP),
                          (*free, asd_done[LAYERS - 1, t]), "turned")
                last = L.dve(partial(V.tensor_copy, as_row_sb[:, t * P:(t + 1) * P],
                                                               b[0:8 * LAYERS, 0:P]),
                             (tt, ln_done["x", NT - 1]), "asd_row")
                all_banks.give(bi, last)
            L.store(as_rows, as_row_sb, (last,), "as_rows_out")
            for l in range(LAYERS):
                L.dve(partial(V.tensor_scalar, as_low[:, :, 4 * l:4 * l + 4], asd[:, :, 8 * l:8 * l + 4],
                                                     SLOPE, None, ALU.mult), (asd_done[LAYERS - 1, NT - 1],),
                      "as_low")
            yield

        of_nodes = nodes()
        for _ in range(NT + 1):
            next(of_nodes)
        run((edges(), 1), (of_nodes, 4))
        s1.close()
        t_as_rows, t_as_low = L.stores["as_rows_out"], ("as_low", LAYERS)
        end1 = fence()

        s2 = ExitStack()
        kT = [sb(s2, f"kT_{p}", [128, PAIRS, N], BF16) for p in ("hi", "lo")]
        v_sb = [sb(s2, f"v_{p}", [P, NT, HEADS, HD + 1], BF16) for p in ("hi", "lo")]

        def linear_attention(banks, cb, sp, end):
            st = Ring([sb(sp, f"qkv_stage{i}", [128, D]) for i in range(3)])
            for i in range(3):
                st.give(i, *end)
            pf = sb(sp, "pf", [128, 2 * FEATS])
            pb = [sb(sp, f"pb_{p}", [128, 2 * FEATS], BF16) for p in ("hi", "lo")]
            z = L.dve(partial(V.memset, pf[:, :], 0.0), end, "proj_zero")
            g0 = L.load(pf[0:HD, 0:FEATS], projT, (z,), "proj_in")
            g1 = L.load(pf[HD:128, FEATS:2 * FEATS], projT, (z,), "proj_in")
            p_done = split("proj", pf[:, :], pb[0][:, :], pb[1][:, :], (g1,))
            wv = [sb(sp, f"wv_{p}", [128, KD, D], BF16) for p in ("hi", "lo")]
            wq = Ring([[sb(sp, f"wq{i}_{p}", [128, KD, 128], BF16) for p in ("hi", "lo")] for i in range(2)])
            sq = [sb(sp, f"sq{i}", [128, 500]) for i in range(2)]
            diag = sb(sp, "diag", [P, 2, NT, HEADS])
            state = {"sq": 0}
            sq_read = [None, None]

            for p in range(2):
                last = L.dve(partial(V.memset, v_sb[p][:, :, :, HD:HD + 1], 1.0 - p), end, "v_ones")
            vw = []
            for k in range(KD):
                vw += load_split("wqkv", st, [(wT_qkv[k * 128:(k + 1) * 128, 2 * D:3 * D], wv[0][:, k, :],
                                              wv[1][:, k, :])])
            yield
            for t in range(NT):
                ts = slice(t * P, (t + 1) * P)
                for half in range(2):
                    cs = slice(half * (D // 2), (half + 1) * (D // 2))
                    bi, b, free = banks.take()
                    for k in range(KD):
                        mm = product(b[0:P, 0:D // 2], [v[:, k, ts] for v in xnT], [w[:, k, cs] for w in wv],
                                     k == 0, k == KD - 1, (*free, vw[k]), "v_mm" if k == KD - 1 else None)
                    hs = slice(half * HEADS // 2, (half + 1) * HEADS // 2)
                    d = split("v", b[0:P, 0:D // 2].rearrange("p (h c) -> p h c", c=HD), v_sb[0][:, t, hs, 0:HD],
                              v_sb[1][:, t, hs, 0:HD], (mm,))
                    v_done = d
                    banks.give(bi, d)
                yield

            def heads_T(which, pair, dst, dst_free, after=()):
                wi, w, w_free = wq.take()
                c = which * D + pair * 128
                si, buf, free = st.take()
                bv = buf[:, :].rearrange("p (k c) -> p k c", k=KD)
                g = L.load(bv, wT_qkv[:, c:c + 128].rearrange("(k p) c -> p k c", p=128), free, f"w_in{si}")
                wd = split("wqkv", bv, w[0][:, :, :], w[1][:, :, :], (g,), w_free)
                st.give(si, wd)
                for (c0, c1) in COLS:
                    bi, b, free = banks.take()
                    for k in range(KD):
                        mm = product(b[:, 0:c1 - c0], [u[:, k, :] for u in w], [v[:, k, c0:c1] for v in xnT],
                                     k == 0, k == KD - 1, (*free, wd), "qk_mm" if k == KD - 1 else None)
                    bb = b[:, 0:c1 - c0]
                    s = state["sq"]
                    state["sq"] += 1
                    sqv = sq[s % 2][:, 0:c1 - c0]
                    a0 = L.act(partial(A.activation, sqv, bb, ACT.Square),
                               (mm, sq_read[s % 2]), "qk_square")
                    a1 = L.act(partial(A.activation, dst[0][:, c0:c1], bb, ACT.Copy,
                                                                           scale=NORM), (*dst_free,), "qk_hi")
                    d = L.dve(partial(V.scalar_tensor_tensor, dst[1][:, c0:c1], bb, NORM, dst[0][:, c0:c1], ALU.mult, ALU.subtract), (a1,), "qk_lo")
                    banks.give(bi, d)
                    bi, b, free = banks.take()
                    nt = (c1 - c0) // P
                    for j in range(nt):
                        mm = L.pe(partial(T.matmul, b[0:P, 2 * j:2 * j + 2], sqv[:, j * P:(j + 1) * P], halves[:, :], start=True, stop=True),
                            (*free, a0, t_halves), "norm_mm" if j == nt - 1 else None)
                    sq_read[s % 2] = mm
                    t0 = c0 // P
                    dd = L.dve(partial(V.tensor_scalar, diag[:, which, t0:t0 + nt, 2 * pair:2 * pair + 2],
                        b[0:P, 0:2 * nt].rearrange("p (t h) -> p t h", h=2), 0.5 * NORM * NORM, None, ALU.mult),
                        (mm,), "diag")
                    banks.give(bi, dd)
                wq.give(wi, ("qk_mm", L.count["qk_mm"]))
                return d, dd

            def dash(parts, ts, banks, after):
                bi, b, free = banks.take()
                mm = product(b[0:P, :], [v[:, ts] for v in parts], [v[:, :] for v in pb], True, True,
                             (*free, *after, p_done), "dash_mm")
                return bi, b[0:P, :].rearrange("p (h m) -> p h m", h=2), mm

            kmax = sb(sp, "kmax", [P, PAIRS * NT])
            top = sb(sp, "top", [128, 4])
            k_ready = {}
            for pair in range(PAIRS):
                kk = [v[:, pair, :] for v in kT]
                k_ready[pair], dd = heads_T(1, pair, kk, end)
                yield
                for t in range(NT):
                    bi, v, mm = dash(kk, slice(t * P, (t + 1) * P), banks, (k_ready[pair],))
                    n = pair * NT + t
                    m = L.dve(partial(V.tensor_reduce, kmax[:, n:n + 1], v, AX.XY, ALU.max),
                              (mm,), "k_max")
                    banks.give(bi, m)
                    if t % 2:
                        yield
            a = L.dve(partial(V.tensor_reduce, top[0:P, 0:1], kmax[:, :], AX.X, ALU.max), (m,), "k_top")
            bi, b, free = banks.take()
            mm = L.pe(partial(T.transpose, b[0:1, 0:P], top[0:P, 0:1], identP), (*free, a), "k_top_mm")
            a = L.dve(partial(V.tensor_reduce, top[0:1, 1:2], b[0:1, 0:P], AX.X, ALU.max), (mm,), "k_top")
            mm = L.pe(partial(T.matmul, b[0:P, 0:1], ones[0:1, 0:P], top[0:1, 1:2], start=True, stop=True),
                      (a, t_ones), "k_top_mm")
            a = L.dve(partial(V.tensor_copy, top[0:P, 2:3], b[0:P, 0:1]), (mm,), "k_top")
            banks.give(bi, a)
            k_shift = sb(sp, "k_shift", [P, NT, HEADS])
            ks = L.dve(partial(V.tensor_scalar, k_shift[:, :, :], diag[:, 1, :, :], top[0:P, 2:3], -1.0,
                                                 ALU.add, ALU.mult), (a,), "k_top")
            yield

            ek = Ring([sb(sp, f"ek{i}", [P, 2, FEATS]) for i in range(2)])
            kp = Ring([[sb(sp, f"kp{i}_{p}", [P, 2, FEATS], BF16) for p in ("hi", "lo")] for i in range(2)])
            eq = Ring([sb(sp, f"eq{i}", [P, 2, FEATS]) for i in range(3)])
            qp = Ring([[sb(sp, f"qp{i}_{p}", [128, 2 * MT, P], BF16) for p in ("hi", "lo")] for i in range(2)])
            cx = [sb(sp, f"cx_{p}", [128, MT, 2, HD + 1], BF16) for p in ("hi", "lo")]
            qT = Ring([[sb(sp, f"qT{i}_{p}", [128, N], BF16) for p in ("hi", "lo")] for i in range(2)])
            cxf = sb(sp, "cxf", [128, MT, 2, HD + 1])
            q_max, q_shift = sb(sp, "q_max", [P, NT, 2]), sb(sp, "q_shift", [P, NT, 2])
            inv = sb(sp, "inv", [P, NT, 2])
            att = Ring([sb(sp, f"att{i}", [P, NT, 128]) for i in range(2)])
            ctx_read, c_free = None, end
            qi, q, q_free = qT.take()
            q_ready, _ = heads_T(0, 0, q, q_free)
            for pair in range(PAIRS):
                hs = slice(2 * pair, 2 * pair + 2)
                cv = cb[:, 0:MT * 2 * (HD + 1)].rearrange("p (m h d) -> p m h d", m=MT, h=2)
                step = {}

                def k_feats(t):
                    kk = [v[:, pair, :] for v in kT]
                    bi, v, mm = dash(kk, slice(t * P, (t + 1) * P), banks, ())
                    ei, e_buf, e_free = ek.take()
                    for h in range(2):
                        a = L.act(partial(A.activation, e_buf[:, h, :], v[:, h, :], ACT.Exp,
                            bias=k_shift[:, t, 2 * pair + h:2 * pair + h + 1]), (mm, ks, *e_free), "k_exp")
                    banks.give(bi, a)
                    ki, k_buf, k_free = kp.take()
                    d0 = L.dve(partial(V.tensor_scalar, k_buf[0][:, :, :], e_buf[:, :, :], EPS, None, ALU.add),
                               (a, *k_free), "k_feat")
                    d1 = L.dve(partial(V.scalar_tensor_tensor, k_buf[1][:, :, :], e_buf[:, :, :], EPS,
                                                                k_buf[0][:, :, :], ALU.add, ALU.subtract),
                               (d0,), "k_feat")
                    ek.give(ei, d1)
                    step[t] = (ki, k_buf, d1)

                def k_ctx(t):
                    ki, k_buf, ready = step.pop(t)
                    for m in range(MT):
                        for h in range(2):
                            first = t == 0 and m == 0 and h == 0
                            mm = product(cv[:, m, h, :], [v[:, h, m * 128:(m + 1) * 128] for v in k_buf],
                                         [v[:, t, 2 * pair + h, :] for v in v_sb], first, t == NT - 1,
                                         (ready, v_done, *c_free), "ctx_mm", skip=True)
                    kp.give(ki, mm)
                    step["ctx"] = mm

                yield from in_step([(0, k_feats), (1, k_ctx)], NT)
                cc = cv.rearrange("p m h d -> p (m h d)")
                a = L.act(partial(A.activation, cxf[:, :, :, :].rearrange("p m h d -> p (m h d)"), cc, ACT.Copy,
                                                 scale=RATIO * RATIO), (step["ctx"], ctx_read), "ctx_copy")
                c_free = (a,)
                c_hi = L.dve(partial(V.tensor_copy, cx[0][:, :, :, :], cxf[:, :, :, :]), (a, ctx_read), "ctx_split")
                c_lo = L.dve(partial(V.tensor_tensor, cx[1][:, :, :, :].rearrange("p m h d -> p (m h d)"),
                    cxf[:, :, :, :].rearrange("p m h d -> p (m h d)"),
                    cx[0][:, :, :, :].rearrange("p m h d -> p (m h d)"), ALU.subtract), (c_hi,), "ctx_split")
                this_q, this_ready, this_i = q, q_ready, qi
                if pair + 1 < PAIRS:
                    qi, q, q_free = qT.take()
                    q_ready, _ = heads_T(0, pair + 1, q, q_free)
                    yield
                ai, att_buf, att_free = att.take()

                def q_feats(t):
                    bi, v, mm = dash(this_q, slice(t * P, (t + 1) * P), banks, (this_ready,))
                    m = L.dve(partial(V.tensor_reduce, q_max[:, t, :], v, AX.X, ALU.max), (mm,), "q_max")
                    m = L.dve(partial(V.scalar_tensor_tensor, q_shift[:, t, :], q_max[:, t, :], -1.0, diag[:, 0, t, hs], ALU.mult, ALU.subtract),
                        (m, step.get("q_exp")), "q_max")
                    ei, e_buf, e_free = eq.take()
                    for h in range(2):
                        a = L.act(partial(A.activation, e_buf[:, h, :], v[:, h, :], ACT.Exp, bias=q_shift[:, t, h:h + 1]),
                            (m, *e_free), "q_exp")
                    banks.give(bi, a)
                    step["e", t] = (ei, e_buf, a)

                def q_turn(t):
                    ei, e_buf, ready = step.pop(("e", t))
                    bi, b, free = banks.take()
                    for n in range(2 * MT):
                        h, m = divmod(n, MT)
                        tt = L.pe(partial(T.transpose, b[:, n * P:(n + 1) * P], e_buf[:, h, m * 128:(m + 1) * 128], identP),
                            (*free, ready), "turned" if n == 2 * MT - 1 else None)
                    eq.give(ei, tt)
                    pi, p_buf, p_free = qp.take()
                    bv = b[:, 0:2 * MT * P].rearrange("p (n c) -> p n c", n=2 * MT)
                    a = L.dve(partial(V.tensor_scalar, p_buf[0][:, :, :], bv, EPS, None, ALU.add),
                              (tt, *p_free), "q_feat")
                    a = L.dve(partial(V.scalar_tensor_tensor, p_buf[1][:, :, :], bv, EPS, p_buf[0][:, :, :],
                                                               ALU.add, ALU.subtract), (a,), "q_feat")
                    banks.give(bi, a)
                    step["p", t] = (pi, p_buf, a)

                def q_out(t):
                    pi, p_buf, ready = step.pop(("p", t))
                    bi, b, free = banks.take()
                    ov = b[0:P, 0:2 * (HD + 1)].rearrange("p (h d) -> p h d", h=2)
                    for h in range(2):
                        for m in range(MT):
                            mm = product(ov[:, h, :], [v[:, h * MT + m, :] for v in p_buf],
                                         [v[:, m, h, :] for v in cx], h == 0 and m == 0, m == MT - 1,
                                         (ready, c_lo, *free), "out_mm", skip=True)
                    qp.give(pi, mm)
                    r = L.dve(partial(V.reciprocal, inv[:, t, :], ov[:, :, HD:HD + 1].rearrange(
                        "p h o -> p (h o)")), (mm, step.get("att")), "att_inv")
                    for h in range(2):
                        a = L.act(partial(A.activation, att_buf[:, t, h * HD:(h + 1) * HD], ov[:, h, 0:HD], ACT.Copy,
                            scale=inv[:, t, h:h + 1]), (r, *att_free), "att_scaled")
                    banks.give(bi, a)
                    step["att"] = a
                    step["out"] = mm

                yield from in_step([(0, q_feats), (2, q_turn), (3, q_out)], NT)
                ctx_read = step["out"]
                qT.give(this_i, step["out"])
                o = L.store(attn_rows[:, pair * 128:(pair + 1) * 128].rearrange("(t p) c -> p t c", p=P),
                            att_buf[:, :, :], (step["att"],), f"att_out{ai}")
                att.give(ai, o)
                att_out = (L.stores.get("att_out0"), L.stores.get("att_out1"))

            wi_free = (("v_mm", L.count["v_mm"]),)
            pw = []
            for k in range(KD):
                pw += load_split("wqkv", st, [(wT_proj[k * 128:(k + 1) * 128, :], wv[0][:, k, :],
                                              wv[1][:, k, :])], wi_free)
            yield
            bp = sb(sp, "bp", [P, D])
            b_got = L.load(bp[:, :], b_proj.partition_broadcast(P), end, "bias_in")
            ar = Ring([sb(sp, f"ar{i}", [P, D]) for i in range(2)])
            aT = Ring([[sb(sp, f"aT{i}_{p}", [128, KD, P], BF16) for p in ("hi", "lo")] for i in range(2)])
            xr = Ring([sb(sp, f"xr{i}", [P, D]) for i in range(2)])
            step = {}

            def rows_in(t):
                ri, r, free = ar.take()
                got = L.load(r[:, :], attn_rows[t * P:(t + 1) * P, :], (*free, *att_out), f"rows_in{ri}")
                ti, a, t_free = aT.take()
                d, tt = transposed("attn", r, KD, a[0], a[1], banks, (got, *t_free))
                ar.give(ri, tt)
                xi, xb, x_free = xr.take()
                xg = L.load(xb[:, :], x[t * P:(t + 1) * P, :], (*x_free, *end), f"x_again{xi}")
                xg = L.dve(partial(V.tensor_tensor, xb[:, :], xb[:, :], bp[:, :], ALU.add), (xg, b_got),
                           "x_bias")
                step[t] = (ti, a, d, xi, xb, xg)

            def project(t):
                ti, a, d, xi, xb, xg = step.pop(t)
                for half in range(2):
                    cs = slice(half * (D // 2), (half + 1) * (D // 2))
                    bi, b, free = banks.take()
                    for k in range(KD):
                        mm = product(b[0:P, 0:D // 2], [v[:, k, :] for v in a], [w[:, k, cs] for w in wv],
                                     k == 0, k == KD - 1, (*free, pw[k], d), "proj_mm" if k == KD - 1 else None)
                    s = L.dve(partial(V.tensor_tensor, xb[:, cs], b[0:P, 0:D // 2], xb[:, cs],
                                                                          ALU.add), (mm, xg), "mixed")
                    banks.give(bi, s)
                aT.give(ti, mm)
                o = L.store(mixed_rows[t * P:(t + 1) * P, :], xb[:, :], (s,), f"mixed_out{xi}")
                xr.give(xi, o)

            yield from in_step([(0, rows_in), (1, project)], NT)

        sp = ExitStack()
        run((linear_attention(Ring(bank[0:7]), bank[7], sp, end1), 1))
        sp.close()
        s2.close()
        s0.close()
        end2 = fence()

        wacc = sb(ctx, "wacc", [P, NT, D])
        s3 = ExitStack()
        count = sb(s3, "count", [P, NT, N], U16)
        m_col = sb(s3, "m_col", [P, LH, NT])
        shift = sb(s3, "shift", [P, NT, 2 * LH])

        def counts(banks, sp, end):
            absent = sb(sp, "absent", [P, NT, N], BF16)
            tab = Ring([[sb(sp, f"tab{i}{j}", [P, N]) for j in range(TABLES)] for i in range(2)])
            for i in range(2):
                tab.give(i, *end)
            scattered = tuple((f"scatter{i}", L.count[f"scatter{i}"]) for i in range(TABLES))
            for t in range(NT):
                ti, tb, free = tab.take()
                got = [L.load(tb[j][:, :], tables[j][t * P * N:(t + 1) * P * N, :].rearrange(
                    "(p n) o -> p (n o)", p=P), (*free, *scattered), f"tab_in{ti}") for j in range(TABLES)]
                a = L.dve(partial(V.tensor_tensor, tb[0][:, :], tb[0][:, :], tb[1][:, :], ALU.add),
                          got[1:], "counted")
                a = L.dve(partial(V.tensor_tensor, tb[0][:, t * P:(t + 1) * P],
                                                                tb[0][:, t * P:(t + 1) * P], identP, ALU.add),
                          (a, t_ident), "counted")
                c = L.dve(partial(V.tensor_copy, count[:, t, :], tb[0][:, :]), (a,), "counted")
                for u0 in range(0, NT, 4):
                    nu = min(4, NT - u0)
                    bi, b, free = banks.take()
                    for j in range(nu):
                        mm = L.pe(partial(T.transpose, b[0:P, j * P:(j + 1) * P], tb[0][:, (u0 + j) * P:((u0 + j) + 1) * P], identP),
                            (*free, a), "turned" if j == nu - 1 else None)
                    d = L.dve(partial(V.tensor_scalar, absent[:, u0:u0 + nu, t * P:(t + 1) * P],
                        b[0:P, 0:nu * P].rearrange("p (u s) -> p u s", u=nu), 0.0, -BIG, ALU.is_equal, ALU.mult),
                        (mm,), "absent")
                    banks.give(bi, d)
                tab.give(ti, mm, c)
                yield
            ab = Ring([sb(sp, f"ab{i}", [P, N]) for i in range(2)])
            junk = [sb(sp, f"junk{i}", [P, N]) for i in range(2)]
            for i in range(2):
                ab.give(i, *end)
            n = 0
            for lh in range(LH):
                l, h = divmod(lh, GH)
                ai, a_buf, free = ab.take()
                got = L.load(a_buf[:, :], as_rows[8 * l + h, :].partition_broadcast(P), (*free, t_as_rows),
                             f"spread_in{ai}")
                for t in range(NT):
                    m = L.dve(partial(V.tensor_tensor_reduce, out=junk[n % 2][:, :], in0=a_buf[:, :], in1=absent[:, t, :], scale=1.0, scalar=-BIG,
                        op0=ALU.add, op1=ALU.max, accum_out=m_col[:, lh, t:t + 1]),
                        (got, d, ("edge_max", n - 1) if n >= 2 else None), "edge_max")
                    n += 1
                ab.give(ai, m)
                yield
            mz = sb(sp, "mz", [P, NT, LH])
            ms = sb(sp, "ms", [P, NT, LH])
            for l in range(LAYERS):
                ls = slice(4 * l, 4 * l + 4)
                ad = asd[:, :, 8 * l + 4:8 * l + 8]
                a = L.dve(partial(V.tensor_tensor, mz[:, :, ls], m_col[:, ls, :].rearrange("p h t -> p t h"), ad, ALU.add), (m, *end), "shifts")
                a = L.dve(partial(V.scalar_tensor_tensor, ms[:, :, ls], mz[:, :, ls], SLOPE, mz[:, :, ls],
                                                                  ALU.mult, ALU.max), (a,), "shifts")
                b0 = L.dve(partial(V.tensor_tensor, shift[:, :, 4 * l:4 * l + 4], ad,
                                                                        ms[:, :, ls], ALU.subtract), (a,), "shifts")
                b1 = L.dve(partial(V.scalar_tensor_tensor, shift[:, :, LH + 4 * l:LH + 4 * l + 4], ad, SLOPE, ms[:, :, ls], ALU.mult, ALU.subtract),
                    (a,), "shifts")
            srow = sb(sp, "srow", [2 * LH, N])
            for t in range(NT):
                bi, b, free = banks.take()
                tt = L.pe(partial(T.transpose, b[0:2 * LH, 0:P], shift[:, t, :], identP), (*free, b1),
                          "turned")
                last = L.dve(partial(V.tensor_copy, srow[:, t * P:(t + 1) * P], b[0:2 * LH, 0:P]),
                             (tt,), "shift_row")
                banks.give(bi, last)
            L.store(shift_rows, srow[:, :], (last,), "shift_rows_out")
            yield

        spc = ExitStack()
        run((counts(Ring(bank[0:8]), spc, end2), 1))
        spc.close()
        end3 = fence()

        def graph_attention(acc, sp, end):
            rb = Ring([[sb(sp, f"shift_b{i}{j}", [P, N]) for j in range(2)] for i in range(2)])
            hb = Ring([sb(sp, f"hb{i}", [P, NT, HW], BF16) for i in range(2)])
            eb = Ring([[sb(sp, f"eb{i}{j}", [P, N]) for j in range(2)] for i in range(2)])
            pb = Ring([[sb(sp, f"pp{i}_{p}", [P, N], BF16) for p in ("hi", "lo")] for i in range(3)])
            bgr = sb(sp, "bgr", [P, LAYERS * D])
            rinv = sb(sp, "rinv", [P, 2, NT])
            node = Ring([sb(sp, f"node{i}", [P, NT, GC]) for i in range(2)])
            for r in (rb, hb, eb, pb, node):
                for i in range(len(r.buffers)):
                    r.give(i, *end)
            b_got = [L.load(bgr[:, l * D:(l + 1) * D], bg[l].partition_broadcast(P), end, "bg_in")
                     for l in range(LAYERS)]
            heads, step = {}, {}
            acc_free = [()] * 5

            def head_in(lh):
                l, h = divmod(lh, GH)
                ri, r, free = rb.take()
                got = [L.load(r[j][:, :], shift_rows[j * LH + lh, :].partition_broadcast(P),
                              (*free, L.stores["shift_rows_out"]), f"shift_in{ri}") for j in range(2)]
                hi, hv, h_free = hb.take()
                got_h = L.load(hv[:, :, :], h_rows[l, :, h, :].rearrange("(t p) c -> p t c", p=P),
                               (*h_free, *[L.stores[f"h_out{i}"] for i in range(3)]), f"h_in{hi}")
                heads[lh] = (ri, r, got, hi, hv, got_h)

            def weigh(i):
                lh, t = divmod(i, NT)
                l, h = divmod(lh, GH)
                if t == 0 and lh == 0:
                    head_in(0)
                if t == 3 and lh + 1 < LH:
                    head_in(lh + 1)
                ri, r, got, *_ = heads[lh]
                ei, eb2, free = eb.take()
                a0 = L.act(partial(A.activation, eb2[0][:, :], r[0][:, :], ACT.Exp,
                                                  bias=asd[:, t, 8 * l + h:8 * l + h + 1]),
                           (got[1], *free), "edge_exp")
                a1 = L.act(partial(A.activation, eb2[1][:, :], r[1][:, :], ACT.Exp,
                                                  bias=as_low[:, t, lh:lh + 1]), (t_as_low,), "edge_exp")
                if t == NT - 1:
                    rb.give(ri, a1)
                d = L.dve(partial(V.tensor_tensor, eb2[0][:, :], eb2[0][:, :], eb2[1][:, :], ALU.max),
                          (a1,), "edge_w")
                d = L.dve(partial(V.scalar_tensor_tensor, eb2[0][:, :], eb2[0][:, :], 1.0, count[:, t, :],
                                                           ALU.min, ALU.mult), (d,), "edge_w")
                step["w", i] = (ei, eb2, d)

            def part(i):
                ei, eb2, d = step.pop(("w", i))
                pi, pp, p_free = pb.take()
                a = L.act(partial(A.activation, pp[0][:, :], eb2[0][:, :], ACT.Copy), (d, *p_free), "edge_w_hi")
                s = L.dve(partial(V.tensor_tensor, pp[1][:, :], eb2[0][:, :], pp[0][:, :], ALU.subtract),
                          (a,), "edge_w_lo")
                eb.give(ei, s)
                step["p", i] = (pi, pp, s)

            def gather(i):
                lh, t = divmod(i, NT)
                ri, r, got, hi_, hv, got_h = heads[lh]
                pi, pp, ready = step.pop(("p", i))
                for u in range(NT):
                    o = acc[u // 2][0:P, (u % 2) * (GC + 2):(u % 2) * (GC + 2) + GC + 1]
                    us = slice(u * P, (u + 1) * P)
                    after = (ready, got_h, *acc_free[u // 2]) if t == 0 else (ready,)
                    L.pe(partial(T.matmul, o, pp[0][:, us], hv[:, t, 0:GC + 1],
                                                             start=(t == 0 and u % 2 == 0), stop=False,
                                                             skip_group_check=True), after)
                    L.pe(partial(T.matmul, o[:, 0:GC], pp[0][:, us], hv[:, t, HW // 2:HW // 2 + GC],
                                                        start=False, stop=False, skip_group_check=True))
                    mm = L.pe(partial(T.matmul, o, pp[1][:, us], hv[:, t, 0:GC + 1], start=False,
                                                             stop=(t == NT - 1), skip_group_check=True),
                              (), "gather_mm" if (u == NT - 1 or (t == NT - 1 and u % 2)) else None)
                    if t == NT - 1 and u % 2:
                        step["acc", lh, u // 2] = mm
                pb.give(pi, mm)
                if t == NT - 1:
                    hb.give(hi_, mm)
                    finish(lh)

            def finish(lh):
                ni, nb, free = node.take()
                for j in range(5):
                    v = acc[j][0:P, 0:2 * (GC + 2)].rearrange("p (u c) -> p u c", u=2)
                    q = rinv[:, lh % 2, 2 * j:2 * j + 2]
                    a = L.dve(partial(V.tensor_scalar, q, v[:, :, GC:GC + 1].rearrange(
                        "p u o -> p (u o)"), SOFTMAX_EPS, None, ALU.add), (step.pop(("acc", lh, j)),), "node_inv")
                    a = L.dve(partial(V.reciprocal, q, q), (a,), "node_inv")
                    for u in range(2):
                        a = L.dve(partial(V.scalar_tensor_tensor, nb[:, 2 * j + u, :], v[:, u, 0:GC], rinv[:, lh % 2, 2 * j + u:2 * j + u + 1],
                            bgr[:, lh * GC:(lh + 1) * GC], ALU.mult, ALU.add),
                            (a, *free, b_got[-1]) if u == 0 else (), "node_out")
                    acc_free[j] = (a,)
                o = L.store(node_rows[:, lh * GC:(lh + 1) * GC].rearrange("(t p) c -> p t c", p=P), nb[:, :, :],
                            (a,), f"node_out{ni}")
                node.give(ni, o)

            yield from in_step([(0, weigh), (1, part), (2, gather)], LH * NT)

        def node_out(banks, sp, end):
            wo = Ring([[sb(sp, f"wo{i}_{p}", [128, KD, D], BF16) for p in ("hi", "lo")] for i in range(1)])
            st = Ring([sb(sp, f"wo_stage{i}", [128, D]) for i in range(3)])
            nr = Ring([sb(sp, f"nr{i}", [P, D]) for i in range(2)])
            nT = Ring([[sb(sp, f"nT{i}_{p}", [128, KD, P], BF16) for p in ("hi", "lo")] for i in range(2)])
            for r in (wo, st, nr, nT):
                for i in range(len(r.buffers)):
                    r.give(i, *end)
            for l in range(LAYERS):
                stored = (L.stores["node_out0"], L.stores["node_out1"])
                wi, w, w_free = wo.take()
                wd = []
                for k in range(KD):
                    r0 = l * D + k * 128
                    wd += load_split("wout", st, [(W_out[r0:r0 + 128, :], w[0][:, k, :], w[1][:, k, :])], w_free)
                step = {}

                def rows_in(t):
                    ri, r, free = nr.take()
                    got = L.load(r[:, :], node_rows[t * P:(t + 1) * P, l * D:(l + 1) * D], (*free, *stored),
                                 f"rows_in{ri}")
                    ti, a, t_free = nT.take()
                    d, tt = transposed("node", r, KD, a[0], a[1], banks, (got, *t_free), relu=True)
                    nr.give(ri, tt)
                    step[t] = (ti, a, d)

                def times(t):
                    ti, a, d = step.pop(t)
                    for half in range(2):
                        cs = slice(half * (D // 2), (half + 1) * (D // 2))
                        bi, b, free = banks.take()
                        for k in range(KD):
                            mm = product(b[0:P, 0:D // 2], [v[:, k, :] for v in a], [v[:, k, cs] for v in w],
                                         k == 0, k == KD - 1, (*free, wd[k], d), "wout_mm" if k == KD - 1 else None)
                        if l == 0:
                            s = L.dve(partial(V.tensor_copy, wacc[:, t, cs], b[0:P, 0:D // 2]),
                                      (mm, *end), "wacc")
                        else:
                            s = L.dve(partial(V.tensor_tensor, wacc[:, t, cs], b[0:P, 0:D // 2], wacc[:, t, cs], ALU.add),
                                (mm, ("wacc", 2 * NT * l)), "wacc")
                        banks.give(bi, s)
                    nT.give(ti, mm)

                yield from in_step([(0, rows_in), (1, times)], NT)
                wo.give(wi, ("wout_mm", L.count["wout_mm"]))

        spg = ExitStack()
        run((graph_attention(bank[0:5], spg, end3), 1))
        spg.close()
        end4 = fence()
        spw = ExitStack()
        run((node_out(Ring(bank[0:8]), spw, end4), 1))
        spw.close()
        end5 = fence()

        s3.close()
        x2 = wacc
        xf = sb(ctx, "xf", [P, NT, D])
        pm = sb(ctx, "pm", [P, 8, NT])
        slot = sb(ctx, "slot", [P, 2, NT], U32)

        def experts(banks, sp, end):
            b1c = sb(sp, "b1c", [128, EXPERTS, KF])
            g_b1 = L.load(b1c[:, :, :], b1_cols, end, "b1_in")
            st1 = Ring([sb(sp, f"w1_stage{i}", [128, KD, F]) for i in range(2)])
            st2 = Ring([sb(sp, f"w2_stage{i}", [128, KF, D]) for i in range(2)])
            w1b = Ring([[sb(sp, f"w1b{i}_{p}", [128, KD, F], BF16) for p in ("hi", "lo")] for i in range(2)])
            w2b = Ring([[sb(sp, f"w2b{i}_{p}", [128, KF, D], BF16) for p in ("hi", "lo")] for i in range(2)])
            b2r = Ring([sb(sp, f"b2r{i}", [128, D]) for i in range(2)])
            hf = Ring([sb(sp, f"hf{i}", [128, CAP]) for i in range(2)])
            hT = Ring([[sb(sp, f"hT{i}_{p}", [128, KF, CAP], BF16) for p in ("hi", "lo")] for i in range(2)])
            orow = Ring([sb(sp, f"orow{i}", [128, D]) for i in range(2)])
            for r in (st1, st2, w1b, w2b, b2r, hf, hT, orow):
                for i in range(len(r.buffers)):
                    r.give(i, *end)
            rt = ExitStack()
            bo = sb(rt, "bo", [P, D])
            mi = [sb(rt, f"mi{i}", [P, D]) for i in range(2)]
            stats = sb(rt, "stats3", [P, NT, 16])
            sw = sb(rt, "sw", [128, KD, EXPERTS])
            sws = [sb(rt, f"sw_{p}", [128, KD, EXPERTS], BF16) for p in ("hi", "lo")]
            sbias = sb(rt, "sbias", [P, EXPERTS])
            fT = Ring([[sb(rt, f"fT{i}_{p}", [128, KD, P], BF16) for p in ("hi", "lo")] for i in range(2)])
            iota8i, iota8 = sb(rt, "iota8i", [P, EXPERTS], I32), sb(rt, "iota8", [P, EXPERTS])
            idx_i, idx = sb(rt, "idx_i", [P, NT], I32), sb(rt, "idx", [P, NT])
            lg = sb(rt, "lg", [P, NT, EXPERTS])
            ex = sb(rt, "ex", [P, NT, EXPERTS])
            z = L.store(slot_rows[0:SLOTS, :].rearrange("(t p) c -> p t c", p=120),
                        zero[0:120, 0:D].unsqueeze(1).broadcast_to([120, SLOTS // 120, D]), (), "slot_zero")
            b_got = L.load(bo[:, :], b_out.partition_broadcast(P), end, "bias_in")
            g = L.load(sw[:, :, :], switch_w.rearrange("(k p) e -> p k e", p=128), end, "switch_in")
            sw_done = split("switch", sw[:, :, :], sws[0][:, :, :], sws[1][:, :, :], (g,))
            g_bias = L.load(sbias[:, :], switch_b.partition_broadcast(P), end, "switch_b_in")
            t = L.pool(partial(G.iota, iota8i[:, :], pattern=[[1, EXPERTS]], base=0, channel_multiplier=0),
                       end, "late_iota")
            t = L.pool(partial(G.iota, idx_i[:, :], pattern=[[P, NT]], base=SLOTS, channel_multiplier=1),
                       (), "late_iota")
            i8 = L.dve(partial(V.tensor_copy, iota8[:, :], iota8i[:, :]), (t, *end), "late_consts")
            i8 = L.dve(partial(V.tensor_copy, idx[:, :], idx_i[:, :]), (t,), "late_consts")
            done = {}

            def new_x(t):
                got = L.load(mi[t % 2][:, :], mixed_rows[t * P:(t + 1) * P, :],
                             (*end, done.get(("x2", t - 2)), L.stores["mixed_out0"], L.stores["mixed_out1"]),
                             f"rows_in{t % 2}")
                a = L.dve(partial(V.tensor_tensor, x2[:, t, :], wacc[:, t, :], bo[:, :], ALU.add),
                          (b_got, *end), "x2")
                a = L.dve(partial(V.scalar_tensor_tensor, x2[:, t, :], x2[:, t, :], 0.0, mi[t % 2][:, :],
                                                                ALU.max, ALU.add), (a, got), "x2")
                done["x2", t] = a
                a = row_stats(x2[:, t, :], stats[:, t, :], (a,))
                if t % 5 == 4:
                    a = inverse_root(stats[:, t - 4:t + 1, :], (a,))
                    for u in range(t - 4, t + 1):
                        done["xf", u] = normalise(x2[:, u, :], xf[:, u, :], stats[:, u, :], (a,))

            def logits(t):
                ti, f, free = fT.take()
                d, tt = transposed("xf", xf[:, t, :], KD, f[0], f[1], banks, (done["xf", t], *free))
                bi, b, free = banks.take()
                for k in range(KD):
                    mm = product(b[0:P, 0:EXPERTS], [v[:, k, :] for v in f], [v[:, k, :] for v in sws],
                                 k == 0, k == KD - 1, (*free, d, sw_done), "logit_mm" if k == KD - 1 else None)
                fT.give(ti, mm)
                a = L.dve(partial(V.tensor_tensor, lg[:, t, :], b[0:P, 0:EXPERTS], sbias[:, :], ALU.add),
                          (mm, g_bias), "route")
                banks.give(bi, a)
                a = L.dve(partial(V.tensor_reduce, pm[:, 0, t:t + 1], lg[:, t, :], AX.X, ALU.max), (a,), "route")
                a = L.dve(partial(V.tensor_scalar, lg[:, t, :], lg[:, t, :], pm[:, 0, t:t + 1], None,
                                                         ALU.subtract), (a,), "route")
                a2 = L.act(partial(A.activation, ex[:, t, :], lg[:, t, :], ACT.Exp,
                                                       accum_out=pm[:, 7, t:t + 1]), (a,), "route_exp")
                a3 = L.dve(partial(V.reciprocal, pm[:, 1, t:t + 1], pm[:, 7, t:t + 1]), (a2,), "route")
                a = L.dve(partial(V.tensor_scalar, lg[:, t, :], lg[:, t, :], 0.0, float(EXPERTS), ALU.is_lt,
                                                         ALU.mult), (a2,), "route")
                a = L.dve(partial(V.tensor_tensor, lg[:, t, :], lg[:, t, :], iota8[:, :], ALU.add),
                          (a, i8), "route")
                a = L.dve(partial(V.tensor_reduce, pm[:, 2, t:t + 1], lg[:, t, :], AX.X, ALU.min), (a,), "route")
                done["route"] = a

            yield from in_step([(0, new_x), (5, logits)], NT)
            rr = sb(rt, "rr", [2 * NT, P])
            bi, b, free = banks.take()
            tt = L.pe(partial(T.transpose, b[0:2 * NT, 0:P], pm[:, 1:3, :].rearrange("p a t -> p (a t)"), identP),
                      (*free, done["route"]), "turned")
            a = L.dve(partial(V.tensor_copy, rr[:, :], b[0:2 * NT, 0:P]), (tt, *end), "route_row")
            banks.give(bi, a)
            s = L.store(route_rows.rearrange("a (t p) -> (a t) p", p=P), rr[:, :], (a,), "route_rows_out")
            pr, ro = sb(rt, "pr", [P, N]), sb(rt, "ro", [P, N])
            g0 = L.load(pr[:, :], route_rows[0, :].partition_broadcast(P), (s, *end), "route_in")
            g1 = L.load(ro[:, :], route_rows[1, :].partition_broadcast(P), (s, *end), "route_in")
            earlier = sb(rt, "earlier", [P, P])
            t = L.pool(partial(G.memset, earlier[:, :], 1.0), end, "late_iota")
            t_e = L.pool(partial(G.affine_select, out=earlier[:, :], in_=earlier[:, :], compare_op=ALU.is_gt,
                                                   fill=0.0, base=0, pattern=[[-1, P]], channel_multiplier=1),
                         (t,), "late_iota")
            mates = [sb(rt, f"mates{i}", [P, N]) for i in range(2)]
            won = sb(rt, "won", [P, N])
            cnt = sb(rt, "cnt", [P, 4, NT])
            c = L.dve(partial(V.memset, cnt[:, :, :], 0.0), end, "ranks")
            for t in range(NT):
                mt = mates[t % 2]
                lo, hi = t * P, (t + 1) * P
                prob, route = pm[:, 1, t:t + 1], pm[:, 2, t:t + 1]
                a = L.dve(partial(V.tensor_scalar, mt[:, :], ro[:, :], route, None,
                                                                        ALU.is_equal), (g1, c), "ranks")
                parts = [(0, lo, ALU.is_ge, 0), (lo, hi, ALU.is_gt, 1), (hi, N, ALU.is_gt, 2)]
                for p0, p1, op, j in parts:
                    if p1 > p0:
                        c = L.dve(partial(V.scalar_tensor_tensor, won[:, p0:p1], pr[:, p0:p1], prob, mt[:, p0:p1], op, ALU.mult,
                            accum_out=cnt[:, j, t:t + 1]), (a, c), "ranks")
                c = L.dve(partial(V.scalar_tensor_tensor, mt[:, lo:hi], pr[:, lo:hi], prob, mt[:, lo:hi], ALU.is_equal, ALU.mult), (c,), "ranks")
                c = L.dve(partial(V.scalar_tensor_tensor, won[:, lo:hi], mt[:, lo:hi], 1.0, earlier[:, :], ALU.mult, ALU.mult,
                    accum_out=cnt[:, 3, t:t + 1]), (c, t_e), "ranks")
            c = L.dve(partial(V.tensor_reduce, pm[:, 3, :], cnt[:, :, :].rearrange("p a t -> p t a"), AX.X,
                                                ALU.add), (c,), "ranks")
            keep = L.dve(partial(V.tensor_scalar, pm[:, 4, :], pm[:, 3, :], float(CAP), None, ALU.is_lt),
                         (c,), "ranks")
            a = L.dve(partial(V.scalar_tensor_tensor, pm[:, 5, :], pm[:, 2, :], float(CAP), pm[:, 3, :], ALU.mult,
                                                       ALU.add), (keep,), "ranks")
            a = L.dve(partial(V.tensor_tensor, pm[:, 6, :], pm[:, 5, :], idx[:, :], ALU.subtract), (a,), "ranks")
            a = L.dve(partial(V.tensor_tensor, pm[:, 6, :], pm[:, 6, :], pm[:, 4, :], ALU.mult), (a,), "ranks")
            a = L.dve(partial(V.tensor_tensor, slot[:, 0, :], pm[:, 6, :], idx[:, :], ALU.add), (a,), "ranks")
            a = L.dve(partial(V.tensor_tensor, slot[:, 1, :], pm[:, 5, :], pm[:, 4, :], ALU.mult), (a,), "ranks")
            a = L.dve(partial(V.tensor_tensor, pm[:, 5, :], pm[:, 4, :], pm[:, 1, :], ALU.mult), (a,), "ranks")
            ranked = L.dve(partial(V.tensor_tensor, pm[:, 6, :], pm[:, 1, :], pm[:, 5, :], ALU.subtract), (a,),
                           "ranks")
            yield
            for t in range(NT):
                L.put(POOL, partial(G.indirect_dma_start, slot_rows, bass.IndirectOffsetOnAxis(slot[:, 0, t:t + 1], axis=0), xf[:, t, :], None),
                    (ranked, z), "to_slots", 16)
                own = L.dve(partial(V.scalar_tensor_tensor, x2[:, t, :], xf[:, t, :], pm[:, 6, t:t + 1],
                                                                  x2[:, t, :], ALU.mult, ALU.add), (ranked,), "own")
            placed = ("to_slots", L.count["to_slots"])
            SP, ST = 120, SLOTS // 120
            rt.close()
            routed = fence()
            sT = [sb(sp, f"sT_{p}", [128, KD, SLOTS], BF16) for p in ("hi", "lo")]
            sr = Ring([sb(sp, f"sr{i}", [P, D]) for i in range(2)])
            for i in range(2):
                sr.give(i, *routed)
            sT_done = {}
            for t in range(ST):
                ri, r, free = sr.take()
                got = L.load(r[0:SP, :], slot_rows[t * SP:(t + 1) * SP, :], (*free, placed), f"rows_in{ri}")
                for g in range(KD // 3):
                    bi, b, free = banks.take()
                    for k in range(3):
                        kk = 3 * g + k
                        tt = L.pe(partial(T.transpose, b[:, k * SP:(k + 1) * SP], r[0:SP, kk * 128:(kk + 1) * 128], ident[0:SP, 0:SP]),
                            (*free, got), "turned" if k == 2 else None)
                    bv = b[:, 0:3 * SP].rearrange("p (k n) -> p k n", k=3)
                    sT_done[t] = d = split("slot", bv, *[v[:, 3 * g:3 * g + 3, t * SP:(t + 1) * SP] for v in sT],
                                           (tt, *routed))
                    banks.give(bi, d)
                sr.give(ri, tt)
                if t % 2:
                    yield
            ws, hs = {}, {}

            def weights(x_):
                i1, s1_, f1 = st1.take()
                g1_ = L.load(s1_[:, :, :], w1[x_].rearrange("(k p) f -> p k f", p=128), f1, f"w1_in{i1}")
                j1, wb1, fb1 = w1b.take()
                d1 = split("w1", s1_[:, :, :].rearrange("p k f -> p (k f)"),
                           *[v[:, :, :].rearrange("p k f -> p (k f)") for v in wb1], (g1_, *fb1))
                st1.give(i1, d1)
                i2, s2_, f2 = st2.take()
                g2_ = L.load(s2_[:, :, :], w2[x_].rearrange("(k p) d -> p k d", p=128), f2, f"w2_in{i2}")
                j2, wb2, fb2 = w2b.take()
                d2 = split("w2", s2_[:, :, :].rearrange("p k f -> p (k f)"),
                           *[v[:, :, :].rearrange("p k f -> p (k f)") for v in wb2], (g2_, *fb2))
                st2.give(i2, d2)
                i3, br, f3 = b2r.take()
                g3 = L.load(br[:, :], b2[x_].partition_broadcast(128), f3, f"b2_in{i3}")
                ws[x_] = (j1, wb1, d1, j2, wb2, d2, i3, br, g3)

            def first(x_):
                j1, wb1, d1, *_ = ws[x_]
                hi_, h, h_free = hT.take()
                for f in range(KF):
                    bi, b, free = banks.take()
                    for k in range(KD):
                        mm = product(b[:, 0:CAP], [v[:, k, f * 128:(f + 1) * 128] for v in wb1],
                                     [v[:, k, x_ * CAP:(x_ + 1) * CAP] for v in sT], k == 0, k == KD - 1,
                                     (*free, d1, sT_done[ST - 1]), "w1_mm" if k == KD - 1 else None)
                    fi, hff, f_free = hf.take()
                    a = L.act(partial(A.activation, hff[:, :], b[:, 0:CAP], ACT.Gelu, bias=b1c[:, x_, f:f + 1]), (mm, g_b1, *f_free), "gelu")
                    banks.give(bi, a)
                    d = split("hid", hff[:, :], h[0][:, f, :], h[1][:, f, :], (a, *h_free))
                    hf.give(fi, d)
                w1b.give(j1, mm)
                hs[x_] = (hi_, h, d)

            def second(x_):
                j1, wb1, d1, j2, wb2, d2, i3, br, g3 = ws.pop(x_)
                hi_, h, ready = hs.pop(x_)
                for r0, r1 in ((0, 98), (98, CAP)):
                    oi, ob, o_free = orow.take()
                    for half in range(2):
                        cs = slice(half * (D // 2), (half + 1) * (D // 2))
                        bi, b, free = banks.take()
                        for f in range(KF):
                            mm = product(b[0:r1 - r0, 0:D // 2], [v[:, f, r0:r1] for v in h],
                                         [v[:, f, cs] for v in wb2], f == 0, f == KF - 1,
                                         (*free, ready, d2), "w2_mm" if f == KF - 1 else None)
                        a = L.dve(partial(V.tensor_tensor, ob[0:(r1 - r0), cs], b[0:(r1 - r0), 0:D // 2], br[0:(r1 - r0), cs], ALU.add), (mm, g3, *o_free), "expert_row")
                        banks.give(bi, a)
                    o = L.store(expert_rows[x_ * CAP + r0:x_ * CAP + r1, :], ob[0:r1 - r0, :], (a,),
                                f"expert_out{oi}")
                    orow.give(oi, o)
                hT.give(hi_, mm)
                w2b.give(j2, mm)
                b2r.give(i3, a)

            yield from in_step([(2, second), (0, weights), (1, first)], EXPERTS)
            stored = (L.stores["expert_out0"], L.stores["expert_out1"])
            for t in range(NT):
                fi, f, free = sr.take()
                got = L.put(POOL, partial(G.indirect_dma_start, f[:, :], None, expert_rows, bass.IndirectOffsetOnAxis(slot[:, 1, t:t + 1], axis=0)),
                    (*free, *stored, ranked), f"fetch{fi}", 16)
                a = L.dve(partial(V.scalar_tensor_tensor, f[:, :], f[:, :], pm[:, 5, t:t + 1],
                                                                    x2[:, t, :], ALU.mult, ALU.add),
                          (got, own), "result")
                o = L.store(out[t * P:(t + 1) * P, :], f[:, :], (a,), f"result_out{fi}")
                sr.give(fi, o)
                yield

        spe = ExitStack()
        run((experts(Ring(bank[0:8]), spe, end5), 1))
        spe.close()
        for token in L.stores.values():
            L.put(SYNC, None, (token,))
        block = ctx.enter_context(nc.Block())
        L.emit(block)


_SHAPE = (N, D)


def kernel(**inputs):
    import numpy as _np
    import concourse.bacc as _bacc
    from concourse import mybir as _mybir
    from concourse.bass_utils import run_bass_kernel_spmd as _run

    g = {k: _np.asarray(v) for k, v in inputs.items()}
    laid = {
        "x": g["x"], "src_rows": g["src"], "dst_rows": g["dst"],
        "src_cols": g["src"].reshape(CHUNKS, P).T, "dst_cols": g["dst"].reshape(CHUNKS, P).T,
        "W_ah": g["L0_gnn_W_ah"], "b_ah": g["L0_gnn_b_ah"].reshape(KD, 128).T,
        "W0": g["L0_gnn_W0"], "W1": g["L0_gnn_W1"], "W2": g["L0_gnn_W2"],
        "a_src": _np.stack([g[f"L0_gnn_a_src{i}"] for i in range(LAYERS)]),
        "a_dst": _np.stack([g[f"L0_gnn_a_dst{i}"] for i in range(LAYERS)]),
        "bg": _np.stack([g[f"L0_gnn_b{i}"] for i in range(LAYERS)]),
        "W_out": g["L0_gnn_W_out"], "b_out": g["L0_gnn_b_out"],
        "wT_qkv": g["L0_mix_w_qkv"].T, "wT_proj": g["L0_mix_w_proj"].T, "b_proj": g["L0_mix_b_proj"],
        "projT": g["L0_mix_proj_mat"].T, "switch_w": g["L0_ffn_switch_w"], "switch_b": g["L0_ffn_switch_b"],
        "w1": g["L0_ffn_w1"], "b1_cols": g["L0_ffn_b1"].reshape(EXPERTS, KF, 128).transpose(2, 0, 1),
        "w2": g["L0_ffn_w2"], "b2": g["L0_ffn_b2"],
    }
    nc = _bacc.Bacc("TRN2", target_bir_lowering=False, num_devices=1)
    arrays, ap = {}, {}
    for name, a in laid.items():
        a = _np.ascontiguousarray(a)
        arrays[f"in_{name}"] = a
        ap[name] = nc.dram_tensor(f"in_{name}", a.shape, _mybir.dt.from_np(a.dtype), kind="ExternalInput").ap()
    out = nc.dram_tensor("out_x", _SHAPE, _mybir.dt.float32, kind="ExternalOutput").ap()
    program(nc, ap["x"], ap["src_rows"], ap["dst_rows"], ap["src_cols"], ap["dst_cols"], ap["W_ah"], ap["b_ah"],
            [ap["W0"], ap["W1"], ap["W2"]], ap["a_src"], ap["a_dst"], ap["bg"], ap["W_out"], ap["b_out"],
            ap["wT_qkv"], ap["wT_proj"], ap["b_proj"], ap["projT"], ap["switch_w"], ap["switch_b"], ap["w1"],
            ap["b1_cols"], ap["w2"], ap["b2"], out)
    r = _run(nc, [arrays], core_ids=[0])
    return r.results[0]["out_x"]
```

```python
from contextlib import ExitStack
from functools import partial

import numpy as np

import concourse.bass as bass
from concourse import mybir

ALU = mybir.AluOpType
ACT = mybir.ActivationFunctionType
AX = mybir.AxisListType
F32 = mybir.dt.float32
BF16 = mybir.dt.bfloat16
I32 = mybir.dt.int32
U32 = mybir.dt.uint32
U16 = mybir.dt.uint16

PE, DVE, SCAL, POOL, SYNC = "tensor", "vector", "scalar", "gpsimd", "sync"

BLOCKS = {PE: lambda b, f: b.tensor(f), DVE: lambda b, f: b.vector(f), SCAL: lambda b, f: b.scalar(f),
          POOL: lambda b, f: b.gpsimd(f), SYNC: lambda b, f: b.sync(f)}

N, D, E = 1250, 768, 21250
P = 125
NT = N // P
KD = D // 128
LAYERS, GH, GC = 3, 4, 192
LH = LAYERS * GH
SLOPE = 0.2
LN_EPS = 1e-5
SOFTMAX_EPS = 1e-16
HEADS, HD, FEATS = 12, 64, 256
PAIRS = HEADS // 2
MT = FEATS // 128
NORM = HD ** -0.25
RATIO = FEATS ** -0.5
EPS = 1e-4
EXPERTS, F = 8, 384
KF = F // 128
EDGE_RATE = 2
RATE = 1.0
AREA = 67968
CAP = int(1.25 * N / EXPERTS)
SLOTS = EXPERTS * CAP
CHUNKS = E // P
TABLES = 2
PIECES = 10
CP = CHUNKS // PIECES
HW = 2 * (GC + 2)
BIG = 3e38
LATER = 1024.0
COLS = [(0, 500), (500, 1000), (1000, 1250)]


class Lanes:

    def __init__(self, nc, ctx):
        self.nc, self.ctx = nc, ctx
        self.dma = {SYNC: nc.sync.dma_start, SCAL: nc.scalar.dma_start, POOL: nc.gpsimd.dma_start}
        self.queues = {e: [] for e in (PE, DVE, SCAL, POOL, SYNC)}
        self.count, self.owner, self.sems = {}, {}, {}
        self.stores = {}

    def put(self, engine, issue, after=(), signal=None, by=1):
        self.queues[engine].append((tuple(t for t in after if t), issue, signal, by))
        if signal is None:
            return None
        if signal not in self.sems:
            self.sems[signal] = self.ctx.enter_context(self.nc.semaphore(signal))
            self.count[signal], self.owner[signal] = 0, engine
        assert self.owner[signal] == engine, signal
        self.count[signal] += by
        return signal, self.count[signal]

    def pe(self, issue, after=(), signal=None):
        return self.put(PE, issue, after, signal)

    def dve(self, issue, after=(), signal=None):
        return self.put(DVE, issue, after, signal)

    def act(self, issue, after=(), signal=None):
        return self.put(SCAL, issue, after, signal)

    def pool(self, issue, after=(), signal=None):
        return self.put(POOL, issue, after, signal)

    def load(self, dst, src, after=(), signal=None, engine=SYNC):
        return self.put(engine, partial(self.dma[engine], dst, src), after, signal, 16)

    def store(self, dst, src, after=(), signal=None, engine=SYNC):
        token = self.put(engine, partial(self.dma[engine], dst, src), after, signal, 16)
        self.stores[token[0]] = token
        return token

    def emit(self, block):
        for name, queue in self.queues.items():
            def instructions(eng, queue=queue):
                passed = {}
                for after, issue, signal, by in queue:
                    for sem, value in after:
                        if passed.get(sem, 0) < value:
                            eng.wait_ge(self.sems[sem], value)
                            passed[sem] = value
                    ins = issue() if issue else None
                    if signal:
                        ins.then_inc(self.sems[signal], by)
            BLOCKS[name](block, instructions)


class Ring:

    def __init__(self, buffers, free=()):
        self.buffers, self.free, self.n = buffers, [free for _ in buffers], 0
        self.held = [False] * len(buffers)

    def take(self):
        i = self.n % len(self.buffers)
        self.n += 1
        assert not self.held[i], "the ring is too short"
        self.held[i] = True
        return i, self.buffers[i], self.free[i]

    def give(self, i, *tokens):
        self.free[i], self.held[i] = tokens, False


def in_step(stages, n):
    for i in range(n + max(lag for lag, _ in stages)):
        for lag, step in stages:
            if 0 <= i - lag < n:
                yield from step(i - lag) or ()
        yield


def run(*tracks):
    live = [[steps, rate, 0.0] for steps, rate in tracks]
    while live:
        for track in list(live):
            track[2] += track[1]
            while track[2] >= 1:
                track[2] -= 1
                if next(track[0], "over") == "over":
                    live.remove(track)
                    break


class Area:

    def __init__(self, memory):
        self.memory, self.used = memory, 0

    def take(self, shape, dt=F32):
        words = (int(np.prod(shape[1:])) * (2 if dt == BF16 else 4) + 3) // 4
        view = self.memory[0:shape[0], self.used:self.used + words]
        self.used += words
        assert self.used <= self.memory.shape[1], "the area is too small"
        view = view if dt == F32 else view.bitcast(dt)
        names = "abcdefg"[:len(shape) - 1]
        sizes = {n: size for n, size in zip(names, shape[1:])}
        return view.rearrange(f"p ({' '.join(names)}) -> p {' '.join(names)}", **sizes)

    def clear(self, used=0):
        self.used = used


def program(nc, x, src_rows, dst_rows, src_cols, dst_cols, W_ah, b_ah, Wg, a_src, a_dst, bg, W_out, b_out,
            wT_qkv, wT_proj, b_proj, projT, switch_w, switch_b, w1, b1_cols, w2, b2, out):
    ctx = ExitStack()
    with ctx:
        L = Lanes(nc, ctx)
        T, V, A, G = nc.tensor, nc.vector, nc.scalar, nc.gpsimd

        def sb(stack, name, shape, dt=F32):
            return stack.enter_context(nc.sbuf_tensor(name, shape, dt))

        def dram(name, shape, dt=F32):
            return nc.dram_tensor(name, shape, dt).ap()

        bank = [ctx.enter_context(nc.psum_tensor(f"bank{i}", [128, 512], F32)) for i in range(8)]

        key_rows = dram("key_rows", (E,))
        tables = [dram(f"table{i}", (N * N + P, 1)) for i in range(TABLES)]
        h_rows = dram("h_rows", (LAYERS, N, GH, HW), BF16)
        as_rows = dram("as_rows", (8 * LAYERS, N))
        shift_rows = dram("shift_rows", (2 * LH, N))
        qk_rows = dram("qk_rows", (2, PAIRS, 128, 2, N), BF16)
        v_rows = dram("v_rows", (PAIRS, N, 2 * (HD + 1)))
        node_rows = dram("node_rows", (N, LAYERS * D))
        mixed_rows = dram("mixed_rows", (N, D))
        attn_rows = dram("attn_rows", (N, D))
        slot_rows = dram("slot_rows", (SLOTS + N, D))
        expert_rows = dram("expert_rows", (SLOTS, D))
        route_rows = dram("route_rows", (2, N))

        ident = sb(ctx, "ident", [128, 128])
        zero = sb(ctx, "zero", [128, D])
        ones = sb(ctx, "ones", [128, 128])
        halves = sb(ctx, "halves", [128, 2])
        t_zero = L.dve(partial(V.memset, zero[:, :], 0.0), (), "zero_set")
        t_ones = L.dve(partial(V.memset, ones[:, :], 1.0), (), "ones_set")
        t = L.pool(partial(G.memset, ident[:, :], 0.0), (), "consts")
        t = L.pool(partial(G.affine_select, out=ident[:, :], in_=ident[:, :], compare_op=ALU.not_equal, fill=1.0,
                                             base=0, pattern=[[-1, 128]], channel_multiplier=1), (t,), "consts")
        t_ident = t
        t = L.pool(partial(G.memset, halves[:, :], 1.0), (), "consts")
        t = L.pool(partial(G.affine_select, out=halves[:, 0:1], in_=halves[:, 0:1], compare_op=ALU.is_ge, fill=0.0,
                                             base=63, pattern=[[0, 1]], channel_multiplier=-1), (t,), "consts")
        t_halves = L.pool(partial(G.affine_select, out=halves[:, 1:2], in_=halves[:, 1:2], compare_op=ALU.is_ge,
                                                    fill=0.0, base=-64, pattern=[[0, 1]], channel_multiplier=1),
                          (t,), "consts")
        identP = ident[0:P, 0:P]

        def split(src, hi, lo, after, hi_after=()):
            a = L.act(partial(A.activation, hi, src, ACT.Copy), (*after, *hi_after), "high_part")
            return L.dve(partial(V.tensor_tensor, lo, src, hi, ALU.subtract), (a,), "low_part")

        def product(out_ap, lhs, rhs, first, last, after=(), signal=None, skip=False):
            terms = [(lhs[0], rhs[0]), (lhs[0], rhs[1]), (lhs[1], rhs[0])]
            token = None
            for n, (l, r) in enumerate(terms):
                token = L.pe(partial(T.matmul, out_ap, l, r, start=first and n == 0,
                                                               stop=last and n == 2, skip_group_check=skip),
                             after if n == 0 else (), signal if n == 2 else None)
            return token

        def load_split(stage, pieces, after=()):
            tokens = []
            for d, hi, lo in pieces:
                i, buf, free = stage.take()
                v = buf[0:d.shape[0], 0:d.shape[1]]
                got = L.load(v, d, free, f"w_in{i}")
                done = split(v, hi, lo, (got, *after))
                stage.give(i, done)
                tokens.append(done)
            return tokens

        def transposed(src, blocks, dst_hi, dst_lo, banks, after, relu=False):
            done, freed = None, None
            for g in range(blocks // 3):
                i, b, free = banks.take()
                for k in range(3):
                    kk = 3 * g + k
                    turned = L.pe(partial(T.transpose, b[:, k * P:(k + 1) * P],
                                                                         src[:, kk * 128:(kk + 1) * 128], identP),
                                  (*free, *after, t_ident) if k == 0 else (), "turned" if k == 2 else None)
                ps = b[:, 0:3 * P].rearrange("p (k n) -> p k n", k=3)
                hi, lo = dst_hi[:, 3 * g:3 * g + 3, :], dst_lo[:, 3 * g:3 * g + 3, :]
                fn = ACT.Relu if relu else ACT.Copy
                a = L.act(partial(A.activation, hi, ps, fn), (turned,), "turned_high")
                if relu:
                    done = L.dve(partial(V.scalar_tensor_tensor, lo, ps, 0.0, hi, ALU.max, ALU.subtract), (a,), "turned_low")
                else:
                    done = L.dve(partial(V.tensor_tensor, lo, ps, hi, ALU.subtract),
                                 (a,), "turned_low")
                banks.give(i, done)
            return done, turned

        def dash(parts, ts, banks, after):
            bi, b, free = banks.take()
            mm = product(b[0:P, :], [parts[:, p, ts] for p in range(2)], [v[:, :] for v in feats], True, True,
                         (*free, *after), "dash_mm")
            return bi, b[0:P, :].rearrange("p (h m) -> p h m", h=2), mm

        def row_stats(xin, st, after):
            L.dve(partial(V.bn_stats, st[:, 0:6], xin[:, 0:D // 2]), after, "normed")
            a = L.dve(partial(V.bn_stats, st[:, 6:12], xin[:, D // 2:D]), (), "normed")
            return L.dve(partial(V.bn_aggr, st[:, 12:14], st[:, 0:12]), (a,), "normed")

        def inverse_root(st, after):
            v, r, u = st[:, :, 13], st[:, :, 14], st[:, :, 15]
            a = L.dve(partial(V.tensor_scalar, v, v, LN_EPS, None, ALU.add), after, "rstd")
            a = L.act(partial(A.activation, u, v, ACT.Sqrt), (a,), "root")
            a = L.dve(partial(V.reciprocal, r, u), (a,), "rstd")
            a = L.dve(partial(V.tensor_tensor, u, v, r, ALU.mult), (a,), "rstd")
            a = L.dve(partial(V.tensor_tensor, u, u, r, ALU.mult), (a,), "rstd")
            a = L.dve(partial(V.tensor_scalar, u, u, -0.5, 1.5, ALU.mult, ALU.add), (a,), "rstd")
            return L.dve(partial(V.tensor_tensor, r, r, u, ALU.mult), (a,), "rstd")

        def normalise(xin, xout, st, after):
            return L.dve(partial(V.tensor_scalar, xout, xin, st[:, 12:13], st[:, 14:15], ALU.subtract, ALU.mult),
                         after, "normed")

        def fence(besides=()):
            return tuple((s, c) for s, c in L.count.items() if s not in besides)

        asd = sb(ctx, "asd", [P, NT, 8 * LAYERS])
        as_low = sb(ctx, "as_low", [P, NT, LH])
        diag = sb(ctx, "diag", [P, 2, NT, HEADS])
        k_shift = sb(ctx, "k_shift", [P, NT, HEADS])
        feats = [sb(ctx, f"feats_{p}", [128, 2 * FEATS], BF16) for p in ("hi", "lo")]
        area = Area(sb(ctx, "area", [128, AREA // 4]))
        s_edges = ExitStack()
        m_col = sb(s_edges, "m_col", [P, LH, NT])
        shift = sb(s_edges, "shift", [P, NT, 2 * LH])
        count = sb(s_edges, "count", [P, NT, N], U16)
        s0 = ExitStack()
        xnT = [sb(s0, f"xnT_{p}", [128, KD, N], BF16) for p in ("hi", "lo")]
        s1 = ExitStack()
        xs = area.take([P, NT, D])
        area.clear()
        x1T = [area.take([128, KD, N], BF16) for p in range(2)]
        area.clear(NT * D)
        wide = D + 8
        w_ring = Ring([[area.take([128, KD, wide], BF16) for p in range(2)] for i in range(2)])
        stage = Ring([sb(s1, f"stage{i}", [128, wide]) for i in range(3)])
        all_banks = Ring(bank[0:8])

        cols = [sb(s1, f"edge_cols{i}", [P, CHUNKS], I32) for i in range(2)]
        rows = [sb(s1, f"edge_rows{i}", [P, CHUNKS], I32) for i in range(2)]
        key_c, key_r = sb(s1, "key_c", [P, CHUNKS]), sb(s1, "key_r", [P, CHUNKS])
        spread = [sb(s1, f"spread{i}", [P, CP * P]) for i in range(2)]
        same = [sb(s1, f"same{i}", [P, P]) for i in range(2)]
        later = sb(s1, "later", [P, P])
        amount = sb(s1, "amount", [P, CHUNKS])
        spare_i = sb(s1, "spare_i", [P, 1], I32)
        spare = sb(s1, "spare", [P, 1])
        moved = sb(s1, "moved", [P, CHUNKS])
        place = sb(s1, "place", [P, CHUNKS], U32)

        def edges():
            got_r = [L.load(rows[i][:, :], d.rearrange("(a b) -> a b", a=P), (), "edge_rows_in")
                     for i, d in enumerate((src_rows, dst_rows))]
            got_c = [L.load(cols[i][:, :], d, (), "edge_cols_in") for i, d in enumerate((src_cols, dst_cols))]
            kr = L.dve(partial(V.scalar_tensor_tensor, key_r[:, :], rows[0][:, :], float(N), rows[1][:, :],
                                                        ALU.mult, ALU.add), got_r[1:], "keys")
            kc = L.dve(partial(V.scalar_tensor_tensor, key_c[:, :], cols[0][:, :], float(N), cols[1][:, :],
                                                        ALU.mult, ALU.add), got_c[1:], "keys")
            kept = L.store(key_rows.rearrange("(a b) -> a b", a=P), key_r[:, :], (kr,), "key_rows_out")
            t = L.pool(partial(G.memset, later[:, :], 1.0), (), "edge_consts")
            t = L.pool(partial(G.affine_select, out=later[:, :], in_=later[:, :], compare_op=ALU.is_ge, fill=LATER,
                                                 base=0, pattern=[[1, P]], channel_multiplier=-1),
                       (t,), "edge_consts")
            t = L.pool(partial(G.iota, spare_i[:, :], pattern=[[0, 1]], base=N * N, channel_multiplier=1),
                       (t,), "edge_consts")
            t_sp = L.dve(partial(V.tensor_copy, spare[:, :], spare_i[:, :]), (t,), "keys")
            read = [(), ()]

            def spread_in(q):
                return L.load(spread[q % 2][:, :], key_rows[q * CP * P:(q + 1) * CP * P].partition_broadcast(P),
                              (kept, *read[q % 2]), f"spread_in{q % 2}")

            following = spread_in(0)
            yield
            for q in range(PIECES):
                got = following
                if q + 1 < PIECES:
                    following = spread_in(q + 1)
                for j in range(CP):
                    c = q * CP + j
                    a = L.dve(partial(V.scalar_tensor_tensor, same[c % 2][:, :], spread[q % 2][:, j * P:(j + 1) * P], key_c[:, c:c + 1], later[:, :],
                        ALU.is_equal, ALU.mult, accum_out=amount[:, c:c + 1]),
                        (got, t_sp, ("same_key", c - 1) if c >= 2 else None), "same_key")
                read[q % 2] = (a,)
                cs = slice(q * CP, (q + 1) * CP)
                b = L.dve(partial(V.tensor_scalar, moved[:, cs], key_c[:, cs], spare[:, 0:1], None,
                                                           ALU.subtract), (a,), "keys")
                b = L.dve(partial(V.scalar_tensor_tensor, moved[:, cs], amount[:, cs], LATER, moved[:, cs],
                                                                  ALU.is_lt, ALU.mult), (b,), "keys")
                b = L.dve(partial(V.tensor_scalar, place[:, cs], moved[:, cs], spare[:, 0:1], None,
                                                           ALU.add), (b,), "keys")
                for c in range(q * CP, (q + 1) * CP):
                    i = c % TABLES
                    before = (f"scatter{i}", 16 * (c // TABLES)) if c >= TABLES else None
                    L.put(POOL, partial(G.indirect_dma_start, tables[i], bass.IndirectOffsetOnAxis(place[:, c:c + 1], axis=0), amount[:, c:c + 1], None,
                        compute_op=ALU.add), (b, L.stores["table_zero"], before), f"scatter{i}", 16)
                yield

        def nodes():
            xn = [sb(s1, f"xn{i}", [P, D]) for i in range(2)]
            stats = sb(s1, "stats1", [P, NT, 16])
            b_col = sb(s1, "b_col", [128, KD])
            x1f = [sb(s1, f"x1f{i}", [128, 500]) for i in range(2)]
            b_got = L.load(b_col[:, :], b_ah, (), "bias_in")
            wi, w_ah, _ = w_ring.take()
            ln_done, turned, xn_done = {}, {}, {}
            BATCH = 5
            for t in range(NT):
                L.load(xs[:, t, :], x[t * P:(t + 1) * P, :], (), f"x_in{t // BATCH}")

            def clear_table(t):
                table, part = tables[t % TABLES], t // TABLES
                n = N * N // (NT // TABLES)
                rows = part * n
                L.store(table[rows:rows + n, :].rearrange("(t p n) o -> p t (n o)", p=P, n=N // 2),
                        zero[0:P, 0:N // 2].unsqueeze(1).broadcast_to([P, n // (P * (N // 2)), N // 2]),
                        (t_zero,), "table_zero", SCAL)
                if part == 0:
                    L.store(table[N * N:, :], zero[0:P, 0:1], (t_zero,), "table_zero", SCAL)

            def statistics(t0):
                for t in range(t0, t0 + BATCH):
                    a = row_stats(xs[:, t, :], stats[:, t, :], ((f"x_in{t // BATCH}", 16 * BATCH),))
                ln_done[t0] = inverse_root(stats[:, t0:t0 + BATCH, :], (a,))

            def norm(t):
                ln_done["x", t] = normalise(xs[:, t, :], xn[t % 2][:, :], stats[:, t, :],
                                            (ln_done[t - t % BATCH], turned.get(t - 2)))

            def turn(t):
                ts = slice(t * P, (t + 1) * P)
                xn_done[t], turned[t] = transposed(xn[t % 2], KD, xnT[0][:, :, ts], xnT[1][:, :, ts],
                                                   all_banks, (ln_done["x", t],))
            w_done = []
            for t in range(NT + 1):
                if t % BATCH == 0 and t < NT:
                    statistics(t)
                if t < NT:
                    norm(t)
                    clear_table(t)
                if t < KD:
                    w_done += load_split(stage, [(W_ah[t * 128:(t + 1) * 128, :], w_ah[0][:, t, 0:D],
                                                       w_ah[1][:, t, 0:D])])
                if t:
                    turn(t - 1)
                yield
            x1_done = []
            for m in range(KD):
                ms = slice(m * 128, (m + 1) * 128)
                for c, (c0, c1) in enumerate(COLS):
                    i, b, free = all_banks.take()
                    for k in range(KD):
                        mm = product(b[:, 0:c1 - c0], [w[:, k, ms] for w in w_ah], [v[:, k, c0:c1] for v in xnT],
                                     k == 0, k == KD - 1, (*free, w_done[k], xn_done[NT - 1]),
                                     "x1_mm" if k == KD - 1 else None)
                    n = 3 * m + c
                    f = x1f[n % 2][:, 0:c1 - c0]
                    a = L.act(partial(A.activation, f, b[:, 0:(c1 - c0)], ACT.Relu, bias=b_col[:, m:m + 1]),
                        (mm, b_got, x1_done[n - 2] if n >= 2 else None), "x1_relu")
                    all_banks.give(i, a)
                    x1_done.append(split(f, x1T[0][:, m, c0:c1], x1T[1][:, m, c0:c1], (a,)))
                yield
            w_ring.give(wi, mm)

            a_row = [[sb(s1, f"a_row{i}{j}", [128, D]) for j in range(2)] for i in range(2)]
            wa_tmp = [sb(s1, f"wa_tmp{i}", [128, D]) for i in range(2)]
            h_out = Ring([sb(s1, f"h_out{i}", [P, GH, HW], BF16) for i in range(3)])
            for i, b in enumerate(h_out.buffers):
                t = L.dve(partial(V.memset, b[:, :, :], 0.0), (), "h_out_set")
                t = L.dve(partial(V.memset, b[:, :, GC:GC + 1], 1.0), (t,), "h_out_set")
                h_out.give(i, t)
            state = {"wa": 0}
            asd_done = {}
            h_mm_last = [None] * LAYERS

            def weights(l):
                i, w, w_free = w_ring.take()
                got = [L.load(a_row[l % 2][j][:, :], d[l].rearrange("h c -> (h c)").partition_broadcast(128),
                              (h_mm_last[l - 2],) if l >= 2 else (), f"a_in{l % 2}")
                       for j, d in enumerate((a_src, a_dst))]
                done = []
                for k in range(KD):
                    si, buf, free = stage.take()
                    g = L.load(buf[:, 0:D], Wg[l][k * 128:(k + 1) * 128, :], free, f"w_in{si}")
                    for j in range(2):
                        n = state["wa"]
                        state["wa"] += 1
                        m = L.dve(partial(V.tensor_tensor, wa_tmp[n % 2][:, :], buf[:, 0:D], a_row[l % 2][j][:, :], ALU.mult),
                            (g, got[1], ("wa_sum", n - 1) if n >= 2 else None), "wa_mul")
                        r = L.dve(partial(V.tensor_reduce, buf[:, D + 4 * j:D + 4 * j + 4], wa_tmp[n % 2][:, :].rearrange("p (h c) -> p h c", h=GH),
                            AX.X, ALU.add), (m, *free), "wa_sum")
                    d = split(buf[:, :], w[0][:, k, :], w[1][:, k, :], (g, r), w_free)
                    stage.give(si, d)
                    done.append(d)
                return i, w, done

            nxt = weights(0)
            yield
            for l in range(LAYERS):
                wi, w, w_done = nxt
                for t in range(NT):
                    if t == 2 and l + 1 < LAYERS:
                        nxt = weights(l + 1)
                    ts = slice(t * P, (t + 1) * P)
                    oi, o, o_free = h_out.take()
                    his, los = [], []
                    for half in range(2):
                        c0, width = half * (D // 2), D // 2 + 8 * half
                        bi, b, free = all_banks.take()
                        for k in range(KD):
                            mm = product(b[0:P, 0:width], [v[:, k, ts] for v in x1T],
                                         [v[:, k, c0:c0 + width] for v in w], k == 0, k == KD - 1,
                                         (*free, w_done[k], x1_done[-1]), "h_mm" if k == KD - 1 else None)
                        v = b[0:P, 0:D // 2].rearrange("p (h c) -> p h c", h=2)
                        hi, lo = (o[:, 2 * half:2 * half + 2, s:s + GC] for s in (0, HW // 2))
                        d = split(v, hi, lo, (mm, *o_free))
                        los.append(d)
                        if half:
                            d2 = L.dve(partial(V.tensor_copy, asd[:, t, 8 * l:8 * l + 8], b[0:P, D // 2:D // 2 + 8]), (mm,), "asd_copy")
                            asd_done[l, t] = d2
                            d = d2
                        all_banks.give(bi, d)
                    s = L.store(h_rows[l, ts, :, :], o[:, :, :], (los[0], los[1]), f"h_out{oi}")
                    h_out.give(oi, s)
                    yield
                h_mm_last[l] = mm
                w_ring.give(wi, mm)
            as_row_sb = count[0:8 * LAYERS, :, :].rearrange("p t n -> p (t n)").bitcast(F32)[:, 0:N]
            last = None
            for t in range(NT):
                bi, b, free = all_banks.take()
                tt = L.pe(partial(T.transpose, b[0:8 * LAYERS, 0:P], asd[:, t, :], identP),
                          (*free, asd_done[LAYERS - 1, t]), "turned")
                last = L.dve(partial(V.tensor_copy, as_row_sb[:, t * P:(t + 1) * P],
                                                               b[0:8 * LAYERS, 0:P]),
                             (tt, ln_done["x", NT - 1]), "asd_row")
                all_banks.give(bi, last)
            L.store(as_rows, as_row_sb, (last,), "as_rows_out")
            for l in range(LAYERS):
                L.dve(partial(V.tensor_scalar, as_low[:, :, 4 * l:4 * l + 4], asd[:, :, 8 * l:8 * l + 4],
                                                     SLOPE, None, ALU.mult), (asd_done[LAYERS - 1, NT - 1],),
                      "as_low")
            yield

        of_nodes = nodes()
        of_edges = edges()
        next(of_edges)
        for _ in range(NT + 1):
            next(of_nodes)
        run((of_nodes, EDGE_RATE), (of_edges, 1))
        s1.close()
        t_as_rows, t_as_low = L.stores["as_rows_out"], ("as_low", LAYERS)
        end1 = fence()
        nodes_end = fence([f"scatter{i}" for i in range(TABLES)])

        def projections(banks, end):
            st = Ring([area.take([128, D]) for i in range(3)], end)
            pf = area.take([128, 2 * FEATS])
            z = L.dve(partial(V.memset, pf[:, :], 0.0), end, "proj_zero")
            L.load(pf[0:HD, 0:FEATS], projT, (z,), "proj_in")
            g1 = L.load(pf[HD:128, FEATS:2 * FEATS], projT, (z,), "proj_in")
            p_done = split(pf[:, :], feats[0][:, :], feats[1][:, :], (g1,))
            wv = [area.take([128, KD, D], BF16) for p in range(2)]
            wq = Ring([[area.take([128, KD, 128], BF16) for p in range(2)] for i in range(2)], end)
            sq = Ring([area.take([128, 500]) for i in range(2)], end)
            v_out = Ring([area.take([P, PAIRS, 2, HD + 1]) for i in range(2)])
            qk_out = Ring([area.take([128, 2, N], BF16) for i in range(2)], end)
            kmax = area.take([P, PAIRS * NT])
            top = area.take([128, 4])
            for i, b in enumerate(v_out.buffers):
                v_out.free[i] = (L.dve(partial(V.memset, b[:, :, :, HD:HD + 1], 1.0), end, "v_ones"),)
            order = [(which, pair) for pair in range(PAIRS) for which in (1, 0)]
            loaded, parted = {}, {}

            def weights_in(n):
                if n < len(order):
                    which, pair = order[n]
                    c = which * D + pair * 128
                    si, buf, free = st.take()
                    bv = buf[:, :].rearrange("p (k c) -> p k c", k=KD)
                    g = L.load(bv, wT_qkv[:, c:c + 128].rearrange("(k p) c -> p k c", p=128), free, f"w_in{si}")
                    loaded[n] = si, bv, g

            def weights_split(n):
                if n < len(order):
                    si, bv, g = loaded.pop(n)
                    wi, w, w_free = wq.take()
                    wd = split(bv, w[0][:, :, :], w[1][:, :, :], (g,), w_free)
                    st.give(si, wd)
                    parted[n] = wi, w, wd

            def heads_T(n, dst, dst_free):
                which, pair = order[n]
                wi, w, wd = parted.pop(n)
                weights_in(n + 2)
                for (c0, c1) in COLS:
                    bi, b, free = banks.take()
                    for k in range(KD):
                        mm = product(b[:, 0:c1 - c0], [u[:, k, :] for u in w], [v[:, k, c0:c1] for v in xnT],
                                     k == 0, k == KD - 1, (*free, wd), "qk_mm" if k == KD - 1 else None)
                    bb = b[:, 0:c1 - c0]
                    qi, sq_buf, sq_free = sq.take()
                    sqv = sq_buf[:, 0:c1 - c0]
                    a0 = L.act(partial(A.activation, sqv, bb, ACT.Square), (mm, *sq_free), "qk_square")
                    a1 = L.act(partial(A.activation, dst[:, 0, c0:c1], bb, ACT.Copy, scale=NORM), dst_free, "qk_hi")
                    d = L.dve(partial(V.scalar_tensor_tensor, dst[:, 1, c0:c1], bb, NORM, dst[:, 0, c0:c1],
                                      ALU.mult, ALU.subtract), (a1,), "qk_lo")
                    banks.give(bi, d)
                    bi, b, free = banks.take()
                    nt = (c1 - c0) // P
                    for j in range(nt):
                        nm = L.pe(partial(T.matmul, b[0:P, 2 * j:2 * j + 2], sqv[:, j * P:(j + 1) * P], halves[:, :],
                                          start=True, stop=True),
                                  (*free, a0, t_halves), "norm_mm" if j == nt - 1 else None)
                    sq.give(qi, nm)
                    t0 = c0 // P
                    dd = L.dve(partial(V.tensor_scalar, diag[:, which, t0:t0 + nt, 2 * pair:2 * pair + 2],
                                       b[0:P, 0:2 * nt].rearrange("p (t h) -> p t h", h=2), 0.5 * NORM * NORM, None,
                                       ALU.mult), (nm,), "diag")
                    banks.give(bi, dd)
                    yield
                    if c0 == 0:
                        weights_split(n + 1)
                wq.give(wi, mm)
                ready[which, pair] = d

            vw = []
            for k in range(KD):
                vw += load_split(st, [(wT_qkv[k * 128:(k + 1) * 128, 2 * D:3 * D], wv[0][:, k, :], wv[1][:, k, :])])
            yield
            for t in range(NT):
                ts = slice(t * P, (t + 1) * P)
                oi, o, o_free = v_out.take()
                for half in range(2):
                    cs = slice(half * (D // 2), (half + 1) * (D // 2))
                    bi, b, free = banks.take()
                    for k in range(KD):
                        mm = product(b[0:P, 0:D // 2], [v[:, k, ts] for v in xnT], [w[:, k, cs] for w in wv],
                                     k == 0, k == KD - 1, (*free, vw[k]), "v_mm" if k == KD - 1 else None)
                    ps = slice(half * PAIRS // 2, (half + 1) * PAIRS // 2)
                    d = L.act(partial(A.activation, o[:, ps, :, 0:HD],
                                      b[0:P, 0:D // 2].rearrange("p (a h c) -> p a h c", h=2, c=HD), ACT.Copy),
                              (mm, *o_free), "v_copy")
                    banks.give(bi, d)
                    yield
                if t >= NT - 2:
                    weights_in(t - NT + 2)
                s = L.store(v_rows[:, ts, :].rearrange("a p c -> p a c"),
                            o[:, :, :, :].rearrange("p a h c -> p a (h c)"), (d,), f"v_out{oi}")
                v_out.give(oi, s)

            ready = {}
            weights_split(0)
            for n, (which, pair) in enumerate(order):
                    oi, o, o_free = qk_out.take()
                    yield from heads_T(n, o, o_free)
                    done = ready[which, pair]
                    s = L.store(qk_rows[which, pair], o[:, :, :], (done,), f"qk_out{oi}")
                    if which:
                        for t in range(NT):
                            bi, v, mm = dash(o, slice(t * P, (t + 1) * P), banks, (done, p_done))
                            c = pair * NT + t
                            m = L.dve(partial(V.tensor_reduce, kmax[:, c:c + 1], v, AX.XY, ALU.max), (mm,), "k_max")
                            banks.give(bi, m)
                            if t % 2:
                                yield
                        s = (s, mm)
                    else:
                        s = (s,)
                    qk_out.give(oi, *s)
            a = L.dve(partial(V.tensor_reduce, top[0:P, 0:1], kmax[:, :], AX.X, ALU.max), (m,), "k_top")
            bi, b, free = banks.take()
            mm = L.pe(partial(T.transpose, b[0:1, 0:P], top[0:P, 0:1], identP), (*free, a), "k_top_mm")
            a = L.dve(partial(V.tensor_reduce, top[0:1, 1:2], b[0:1, 0:P], AX.X, ALU.max), (mm,), "k_top")
            mm = L.pe(partial(T.matmul, b[0:P, 0:1], ones[0:1, 0:P], top[0:1, 1:2], start=True, stop=True),
                      (a, t_ones), "k_top_mm")
            a = L.dve(partial(V.tensor_copy, top[0:P, 2:3], b[0:P, 0:1]), (mm,), "k_top")
            banks.give(bi, a)
            L.dve(partial(V.tensor_scalar, k_shift[:, :, :], diag[:, 1, :, :], top[0:P, 2:3], -1.0,
                          ALU.add, ALU.mult), (a,), "k_top")
            yield

        def linear_attention(banks, cb, end):
            STEPS, DRAIN = NT // 2, 3
            ef = Ring([area.take([P, 2, FEATS]) for i in range(4)], end)
            qf = Ring([area.take([128, 2 * MT, P]) for i in range(4)], end)
            context = area.take([128, MT, 2, HD + 1])
            kT = Ring([area.take([128, 2, N], BF16) for i in range(2)], end)
            qT = Ring([area.take([128, 2, N], BF16) for i in range(2)], end)
            vs = Ring([area.take([P, NT, 2, HD + 1]) for i in range(2)], end)
            q_max, q_shift = area.take([P, NT, 2]), area.take([P, NT, 2])
            inv = area.take([P, 2, 2])
            att = Ring([area.take([P, NT, 128]) for i in range(2)], end)
            spilled = [L.stores[f"{what}_out{i}"] for what in ("qk", "v") for i in range(2)]
            order = [(pair, kind, b) for pair in range(PAIRS)
                     for kind, n in (("k", STEPS), ("q", STEPS), (None, DRAIN)) for b in range(n)]
            cv = cb[:, 0:MT * 2 * (HD + 1)].rearrange("p (m h d) -> p m h d", m=MT, h=2)
            ov = cb[0:P, 0:4 * (HD + 1)].rearrange("p (u h d) -> p u h d", u=2, h=2)
            loaded, step = {}, {"cb": end}

            def pair_in(pair):
                ki, kb, k_free = kT.take()
                k_got = L.load(kb[:, :, :], qk_rows[1, pair], (*k_free, *spilled), f"k_in{ki}")
                vi, vb, v_free = vs.take()
                v_got = L.load(vb[:, :, :, :].rearrange("p t h c -> p t (h c)"),
                               v_rows[pair].rearrange("(t p) c -> p t c", p=P), (*v_free, *spilled), f"v_in{vi}")
                qi, qb, q_free = qT.take()
                q_got = L.load(qb[:, :, :], qk_rows[0, pair], (*q_free, *spilled), f"q_in{qi}")
                loaded[pair] = {"k": (ki, kb, k_got), "v": (vi, vb, v_got), "q": (qi, qb, q_got)}

            def features(n):
                pair, kind, b = order[n]
                if kind is None:
                    return
                if kind == "k" and b == 0:
                    if pair == 0:
                        pair_in(0)
                    if pair + 1 < PAIRS:
                        pair_in(pair + 1)
                i, buf, got = loaded[pair][kind]
                step["dash", n] = [dash(buf, slice(t * P, (t + 1) * P), banks, (got,)) for t in (2 * b, 2 * b + 1)]
                if b == STEPS - 1:
                    (kT if kind == "k" else qT).give(i, step["dash", n][1][2])

            def exponentials(n):
                pair, kind, b = order[n]
                if kind is None:
                    return
                hs = slice(2 * pair, 2 * pair + 2)
                tiles = step.pop(("dash", n))
                done = []
                if kind == "q":
                    for u, (bi, v, mm) in enumerate(tiles):
                        m = L.dve(partial(V.tensor_reduce, q_max[:, 2 * b + u, :], v, AX.X, ALU.max), (mm,), "q_max")
                    ts = slice(2 * b, 2 * b + 2)
                    m = L.dve(partial(V.scalar_tensor_tensor, q_shift[:, ts, :], q_max[:, ts, :], -1.0,
                                      diag[:, 0, ts, hs], ALU.mult, ALU.subtract), (m, step.get("q_exp")), "q_max")
                for u, (bi, v, mm) in enumerate(tiles):
                    t = 2 * b + u
                    ei, e, e_free = ef.take()
                    for h in range(2):
                        bias = k_shift[:, t, 2 * pair + h:2 * pair + h + 1] if kind == "k" else q_shift[:, t, h:h + 1]
                        a = L.act(partial(A.activation, e[:, h, :], v[:, h, :], ACT.Exp, bias=bias),
                                  (mm if kind == "k" else m, *e_free), kind + "_exp")
                    banks.give(bi, a)
                    if kind == "k":
                        a = L.dve(partial(V.tensor_scalar, e[:, :, :], e[:, :, :], EPS, None, ALU.add), (a,),
                                   "k_feat")
                    else:
                        step["q_exp"] = a
                    done.append((ei, e, a))
                step["exp", n] = done

            def sum_or_turn(n):
                pair, kind, b = order[n]
                if kind is None:
                    return
                tiles = step.pop(("exp", n))
                turned = []
                for u, (ei, e, ready) in enumerate(tiles):
                    t = 2 * b + u
                    if kind == "k":
                        vi, vb, v_got = loaded[pair]["v"]
                        for m in range(MT):
                            for h in range(2):
                                mm = L.pe(partial(T.matmul, cv[:, m, h, :], e[:, h, m * 128:(m + 1) * 128],
                                                  vb[:, t, h, :], start=t == 0 and m == 0 and h == 0,
                                                  stop=t == NT - 1, skip_group_check=True),
                                          (ready, v_got, *step["cb"]), "ctx_mm" if m == MT - 1 and h else None)
                        step["ctx"] = mm
                    else:
                        bi, bk, free = banks.take()
                        for k in range(2 * MT):
                            h, m = divmod(k, MT)
                            mm = L.pe(partial(T.transpose, bk[:, k * P:(k + 1) * P], e[:, h, m * 128:(m + 1) * 128],
                                              identP), (*free, ready), "turned" if k == 2 * MT - 1 else None)
                        turned.append((bi, bk, mm))
                    ef.give(ei, mm)
                if kind == "k" and b == STEPS - 1:
                    vs.give(vi, mm)
                step["turn", n] = turned

            def turned_features(n):
                pair, kind, b = order[n]
                if kind is None:
                    return
                tiles = step.pop(("turn", n))
                if kind == "k" and b == STEPS - 1:
                    a = L.act(partial(A.activation, context[:, :, :, :], cv, ACT.Copy, scale=RATIO * RATIO),
                              (step["ctx"], step.get("out"), *end), "ctx_copy")
                    step["cb"], step["context"] = (a,), a
                step["qf", n] = done = []
                for bi, bk, mm in tiles:
                    qi, q, q_free = qf.take()
                    a = L.dve(partial(V.tensor_scalar, q[:, :, :],
                                      bk[:, 0:2 * MT * P].rearrange("p (n c) -> p n c", n=2 * MT), EPS, None,
                                      ALU.add), (mm, *q_free), "q_feat")
                    banks.give(bi, a)
                    done.append((qi, q, a))

            def outputs(n):
                pair, kind, b = order[n]
                if kind is None:
                    return
                for u, (qi, q, ready) in enumerate(step.pop(("qf", n))):
                    for h in range(2):
                        for m in range(MT):
                            mm = L.pe(partial(T.matmul, ov[:, u, h, :], q[:, h * MT + m, :], context[:, m, h, :],
                                              start=u == 0 and h == 0 and m == 0, stop=m == MT - 1,
                                              skip_group_check=True),
                                      (ready, step["context"], *step["cb"]), "out_mm" if h and m == MT - 1 else None)
                    qf.give(qi, mm)
                    step["out"] = mm

            def divided(n):
                pair, kind, b = order[n]
                if kind != "q":
                    return
                if b == 0:
                    step["att"] = att.take()
                ai, att_buf, att_free = step["att"]
                r = L.dve(partial(V.reciprocal, inv[:, :, :], ov[:, :, :, HD:HD + 1].rearrange(
                    "p u h o -> p u (h o)")), (step["out"], step.get("att_done")), "att_inv")
                for u in range(2):
                    for h in range(2):
                        a = L.act(partial(A.activation, att_buf[:, 2 * b + u, h * HD:(h + 1) * HD],
                                          ov[:, u, h, 0:HD], ACT.Copy, scale=inv[:, u, h:h + 1]),
                                  (r, *att_free), "att_scaled")
                step["cb"], step["att_done"] = (a,), a
                if b == STEPS - 1:
                    o = L.store(attn_rows[:, pair * 128:(pair + 1) * 128].rearrange("(t p) c -> p t c", p=P),
                                att_buf[:, :, :], (a,), f"att_out{ai}")
                    att.give(ai, o)

            yield from in_step([(5, divided), (1, exponentials), (3, turned_features),
                                (2, sum_or_turn), (0, features), (4, outputs)], len(order))

        def mix_projection(banks, end):
            st = Ring([area.take([128, D]) for i in range(3)], end)
            wp = [area.take([128, KD, D], BF16) for p in range(2)]
            bp = area.take([P, D])
            ar = Ring([area.take([P, D]) for i in range(2)], end)
            aT = Ring([[area.take([128, KD, P], BF16) for p in range(2)] for i in range(2)], end)
            xr = Ring([area.take([P, D]) for i in range(2)], end)
            att_out = (L.stores["att_out0"], L.stores["att_out1"])
            b_got = L.load(bp[:, :], b_proj.partition_broadcast(P), end, "bias_in")
            pw = []
            for k in range(KD):
                pw += load_split(st, [(wT_proj[k * 128:(k + 1) * 128, :], wp[0][:, k, :], wp[1][:, k, :])], end)
            yield
            step = {}

            def rows_in(t):
                ri, r, free = ar.take()
                got = L.load(r[:, :], attn_rows[t * P:(t + 1) * P, :], (*free, *att_out), f"rows_in{ri}")
                ti, a, t_free = aT.take()
                d, tt = transposed(r, KD, a[0], a[1], banks, (got, *t_free))
                ar.give(ri, tt)
                xi, xb, x_free = xr.take()
                xg = L.load(xb[:, :], x[t * P:(t + 1) * P, :], x_free, f"x_again{xi}")
                xg = L.dve(partial(V.tensor_tensor, xb[:, :], xb[:, :], bp[:, :], ALU.add), (xg, b_got),
                           "x_bias")
                step[t] = (ti, a, d, xi, xb, xg)

            def project(t):
                ti, a, d, xi, xb, xg = step.pop(t)
                for half in range(2):
                    cs = slice(half * (D // 2), (half + 1) * (D // 2))
                    bi, b, free = banks.take()
                    for k in range(KD):
                        mm = product(b[0:P, 0:D // 2], [v[:, k, :] for v in a], [w[:, k, cs] for w in wp],
                                     k == 0, k == KD - 1, (*free, pw[k], d), "proj_mm" if k == KD - 1 else None)
                    s = L.dve(partial(V.tensor_tensor, xb[:, cs], b[0:P, 0:D // 2], xb[:, cs],
                                                                          ALU.add), (mm, xg), "mixed")
                    banks.give(bi, s)
                    yield
                aT.give(ti, mm)
                o = L.store(mixed_rows[t * P:(t + 1) * P, :], xb[:, :], (s,), f"mixed_out{xi}")
                xr.give(xi, o)

            yield from in_step([(0, rows_in), (1, project)], NT)

        def counts(banks, sp, end):
            absent = sb(sp, "absent", [P, NT, N], BF16)
            tab = Ring([[sb(sp, f"tab{i}{j}", [P, N]) for j in range(TABLES)] for i in range(2)])
            for i in range(2):
                tab.give(i, *end)
            scattered = tuple((f"scatter{i}", L.count[f"scatter{i}"]) for i in range(TABLES))
            for t in range(NT):
                ti, tb, free = tab.take()
                got = [L.load(tb[j][:, :], tables[j][t * P * N:(t + 1) * P * N, :].rearrange(
                    "(p n) o -> p (n o)", p=P), (*free, *scattered), f"tab_in{ti}") for j in range(TABLES)]
                a = L.dve(partial(V.tensor_tensor, tb[0][:, :], tb[0][:, :], tb[1][:, :], ALU.add),
                          got[1:], "counted")
                a = L.dve(partial(V.tensor_tensor, tb[0][:, t * P:(t + 1) * P],
                                                                tb[0][:, t * P:(t + 1) * P], identP, ALU.add),
                          (a, t_ident), "counted")
                c = L.dve(partial(V.tensor_copy, count[:, t, :], tb[0][:, :]), (a,), "counted")
                for u0 in range(0, NT, 4):
                    nu = min(4, NT - u0)
                    bi, b, free = banks.take()
                    for j in range(nu):
                        mm = L.pe(partial(T.transpose, b[0:P, j * P:(j + 1) * P], tb[0][:, (u0 + j) * P:((u0 + j) + 1) * P], identP),
                            (*free, a), "turned" if j == nu - 1 else None)
                    d = L.dve(partial(V.tensor_scalar, absent[:, u0:u0 + nu, t * P:(t + 1) * P],
                        b[0:P, 0:nu * P].rearrange("p (u s) -> p u s", u=nu), 0.0, -BIG, ALU.is_equal, ALU.mult),
                        (mm,), "absent")
                    banks.give(bi, d)
                tab.give(ti, mm, c)
                yield
            ab = Ring([sb(sp, f"ab{i}", [P, N]) for i in range(2)])
            junk = [sb(sp, f"junk{i}", [P, N]) for i in range(2)]
            for i in range(2):
                ab.give(i, *end)
            n = 0
            for lh in range(LH):
                l, h = divmod(lh, GH)
                ai, a_buf, free = ab.take()
                got = L.load(a_buf[:, :], as_rows[8 * l + h, :].partition_broadcast(P), (*free, t_as_rows),
                             f"spread_in{ai}")
                for t in range(NT):
                    m = L.dve(partial(V.tensor_tensor_reduce, out=junk[n % 2][:, :], in0=a_buf[:, :], in1=absent[:, t, :], scale=1.0, scalar=-BIG,
                        op0=ALU.add, op1=ALU.max, accum_out=m_col[:, lh, t:t + 1]),
                        (got, d, ("edge_max", n - 1) if n >= 2 else None), "edge_max")
                    n += 1
                    yield
                ab.give(ai, m)
            mz = sb(sp, "mz", [P, NT, LH])
            ms = sb(sp, "ms", [P, NT, LH])
            for l in range(LAYERS):
                ls = slice(4 * l, 4 * l + 4)
                ad = asd[:, :, 8 * l + 4:8 * l + 8]
                a = L.dve(partial(V.tensor_tensor, mz[:, :, ls], m_col[:, ls, :].rearrange("p h t -> p t h"), ad, ALU.add), (m, *end), "shifts")
                a = L.dve(partial(V.scalar_tensor_tensor, ms[:, :, ls], mz[:, :, ls], SLOPE, mz[:, :, ls],
                                                                  ALU.mult, ALU.max), (a,), "shifts")
                b0 = L.dve(partial(V.tensor_tensor, shift[:, :, 4 * l:4 * l + 4], ad,
                                                                        ms[:, :, ls], ALU.subtract), (a,), "shifts")
                b1 = L.dve(partial(V.scalar_tensor_tensor, shift[:, :, LH + 4 * l:LH + 4 * l + 4], ad, SLOPE, ms[:, :, ls], ALU.mult, ALU.subtract),
                    (a,), "shifts")
            srow = sb(sp, "srow", [2 * LH, N])
            for t in range(NT):
                bi, b, free = banks.take()
                tt = L.pe(partial(T.transpose, b[0:2 * LH, 0:P], shift[:, t, :], identP), (*free, b1),
                          "turned")
                last = L.dve(partial(V.tensor_copy, srow[:, t * P:(t + 1) * P], b[0:2 * LH, 0:P]),
                             (tt,), "shift_row")
                banks.give(bi, last)
            L.store(shift_rows, srow[:, :], (last,), "shift_rows_out")
            yield

        sc = ExitStack()
        area.clear()
        run((projections(Ring(bank[0:6]), nodes_end), 1), (counts(Ring(bank[6:8]), sc, end1), 1.6))
        sc.close()
        s0.close()
        end2 = fence()

        HALF = NT // 2
        HN = HALF * P
        layers_queued = [0]

        def graph_attention(acc, sp, end):
            rb = Ring([[sb(sp, f"shift_b{i}{j}", [P, N]) for j in range(2)] for i in range(2)], end)
            hb = Ring([sb(sp, f"hb{i}", [P, NT, HW], BF16) for i in range(2)], end)
            eb = Ring([[sb(sp, f"eb{i}{j}", [P, 2, HN]) for j in range(2)] for i in range(4)], end)
            pb = Ring([[sb(sp, f"pp{i}_{p}", [P, 2, HN], BF16) for p in ("hi", "lo")] for i in range(3)], end)
            bgr = sb(sp, "bgr", [P, LAYERS * D])
            rinv = sb(sp, "rinv", [P, 2, HALF])
            node = Ring([sb(sp, f"node{i}", [P, HALF, GC]) for i in range(2)], end)
            b_got = [L.load(bgr[:, l * D:(l + 1) * D], bg[l].partition_broadcast(P), end, "bg_in")
                     for l in range(LAYERS)]
            heads, step = {}, {}
            acc_free = [end] * len(acc)
            SPLITS = NT // 2
            ITEMS = 2 * SPLITS

            def head_in(lh):
                l, h = divmod(lh, GH)
                ri, r, free = rb.take()
                got = [L.load(r[j][:, :], shift_rows[j * LH + lh, :].partition_broadcast(P),
                              (*free, L.stores["shift_rows_out"]), f"shift_in{ri}") for j in range(2)]
                hi, hv, h_free = hb.take()
                got_h = L.load(hv[:, :, :], h_rows[l, :, h, :].rearrange("(t p) c -> p t c", p=P),
                               (*h_free, *[L.stores[f"h_out{i}"] for i in range(3)]), f"h_in{hi}")
                heads[lh] = (ri, r, got, hi, hv, got_h)

            def edge_exp(i):
                lh, j = divmod(i, ITEMS)
                half, pair = divmod(j, SPLITS)
                l, h = divmod(lh, GH)
                ns = slice(half * HN, (half + 1) * HN)
                if j == 0 and lh == 0:
                    head_in(0)
                if j == 3 and lh + 1 < LH:
                    head_in(lh + 1)
                ri, r, got, *_ = heads[lh]
                ei, eb2, free = eb.take()
                for u in range(2):
                    t = 2 * pair + u
                    L.act(partial(A.activation, eb2[0][:, u, :], r[0][:, ns], ACT.Exp,
                                  bias=asd[:, t, 8 * l + h:8 * l + h + 1]), (got[1], *free))
                    a1 = L.act(partial(A.activation, eb2[1][:, u, :], r[1][:, ns], ACT.Exp,
                                       bias=as_low[:, t, lh:lh + 1]), (), "edge_exp" if u else None)
                if j == ITEMS - 1:
                    rb.give(ri, a1)
                step["e", i] = (ei, eb2, a1)

            def weigh(i):
                j = i % ITEMS
                half, pair = divmod(j, SPLITS)
                ns = slice(half * HN, (half + 1) * HN)
                ei, eb2, a1 = step.pop(("e", i))
                d = L.dve(partial(V.tensor_tensor, eb2[0][:, :, :], eb2[0][:, :, :], eb2[1][:, :, :], ALU.max),
                          (a1,), "edge_w")
                d = L.dve(partial(V.scalar_tensor_tensor, eb2[0][:, :, :], eb2[0][:, :, :], 1.0,
                                  count[:, 2 * pair:2 * pair + 2, ns], ALU.min, ALU.mult), (d,), "edge_w")
                pi, pp, p_free = pb.take()
                a = L.dve(partial(V.tensor_copy, pp[0][:, :, :], eb2[0][:, :, :]), (d, *p_free), "edge_w_hi")
                s = L.pool(partial(G.tensor_tensor, pp[1][:, :, :], eb2[0][:, :, :], pp[0][:, :, :],
                                   ALU.subtract), (a,), "edge_w_lo")
                eb.give(ei, s)
                step["p", i] = (pi, pp, s)

            def gather(i):
                lh, j = divmod(i, ITEMS)
                half, pair = divmod(j, SPLITS)
                ri, r, got, hi_, hv, got_h = heads[lh]
                pi, pp, ready = step.pop(("p", i))
                for u in range(2):
                    t = 2 * pair + u
                    first, last = pair == 0 and u == 0, pair == SPLITS - 1 and u == 1
                    for v in range(HALF):
                        c0 = (v % 2) * (GC + 2)
                        o = acc[v // 2][0:P, c0:c0 + GC + 1]
                        vs = slice(v * P, (v + 1) * P)
                        after = (ready, got_h, *acc_free[v // 2]) if first else (ready,)
                        L.pe(partial(T.matmul, o, pp[0][:, u, vs], hv[:, t, 0:GC + 1], start=first and v % 2 == 0,
                                     stop=False, skip_group_check=True), after)
                        L.pe(partial(T.matmul, o[:, 0:GC], pp[0][:, u, vs], hv[:, t, HW // 2:HW // 2 + GC],
                                     start=False, stop=False, skip_group_check=True))
                        ends = v % 2 == 1 or v == HALF - 1
                        mm = L.pe(partial(T.matmul, o, pp[1][:, u, vs], hv[:, t, 0:GC + 1], start=False,
                                          stop=last, skip_group_check=True),
                                  (), "gather_mm" if (last and ends) or (u == 1 and v == HALF - 1) else None)
                        if last and ends:
                            step["acc", v // 2] = mm
                pb.give(pi, mm)
                if j == ITEMS - 1:
                    hb.give(hi_, mm)

            def finish(i):
                lh, j = divmod(i, ITEMS)
                half, pair = divmod(j, SPLITS)
                if pair < SPLITS - 1:
                    return
                ni, nb, free = node.take()
                for k, b in enumerate(acc):
                    n = min(2, HALF - 2 * k)
                    v = b[0:P, 0:n * (GC + 2)].rearrange("p (u c) -> p u c", u=n)
                    q = rinv[:, half, 2 * k:2 * k + n]
                    a = L.dve(partial(V.tensor_scalar, q, v[:, :, GC:GC + 1].rearrange("p u o -> p (u o)"),
                                      SOFTMAX_EPS, None, ALU.add), (step.pop(("acc", k)),), "node_inv")
                    a = L.dve(partial(V.reciprocal, q, q), (a,), "node_inv")
                    for u in range(n):
                        a = L.dve(partial(V.scalar_tensor_tensor, nb[:, 2 * k + u, :], v[:, u, 0:GC],
                                          rinv[:, half, 2 * k + u:2 * k + u + 1],
                                          bgr[:, lh * GC:(lh + 1) * GC], ALU.mult, ALU.add),
                                  (a, *free, b_got[-1]) if u == 0 else (), "node_out")
                    acc_free[k] = (a,)
                o = L.store(node_rows[half * HN:(half + 1) * HN, lh * GC:(lh + 1) * GC].rearrange(
                    "(t p) c -> p t c", p=P), nb[:, :, :], (a,), f"node_out{ni}")
                node.give(ni, o)
                if half and lh % GH == GH - 1:
                    layers_queued[0] += 1

            yield from in_step([(0, edge_exp), (1, weigh), (4, finish), (3, gather)], LH * ITEMS)

        def node_projection(banks, end, wacc):
            w = [area.take([128, KD, D], BF16) for p in range(2)]
            st = Ring([area.take([128, D]) for i in range(2)], end)
            nr = Ring([area.take([P, D]) for i in range(2)], end)
            nT = Ring([[area.take([128, KD, P], BF16) for p in range(2)] for i in range(2)], end)
            w_free, summed = end, end
            for l in range(LAYERS):
                wd = []
                for k in range(KD):
                    r0 = l * D + k * 128
                    wd += load_split(st, [(W_out[r0:r0 + 128, :], w[0][:, k, :], w[1][:, k, :])], w_free)
                while layers_queued[0] <= l:
                    yield
                stored = (L.stores["node_out0"], L.stores["node_out1"])
                step = {}

                def rows_in(t):
                    ri, r, free = nr.take()
                    got = L.load(r[:, :], node_rows[t * P:(t + 1) * P, l * D:(l + 1) * D], (*free, *stored),
                                 f"rows_in{ri}")
                    ti, a, t_free = nT.take()
                    d, tt = transposed(r, KD, a[0], a[1], banks, (got, *t_free), relu=True)
                    nr.give(ri, tt)
                    step[t] = (ti, a, d)

                def times(t):
                    ti, a, d = step.pop(t)
                    for half in range(2):
                        cs = slice(half * (D // 2), (half + 1) * (D // 2))
                        bi, b, free = banks.take()
                        for k in range(KD):
                            mm = product(b[0:P, 0:D // 2], [v[:, k, :] for v in a], [v[:, k, cs] for v in w],
                                         k == 0, k == KD - 1, (*free, wd[k], d), "wout_mm" if k == KD - 1 else None)
                        if l == 0:
                            s = L.dve(partial(V.tensor_copy, wacc[:, t, cs], b[0:P, 0:D // 2]), (mm, *end), "wacc")
                        else:
                            s = L.dve(partial(V.tensor_tensor, wacc[:, t, cs], b[0:P, 0:D // 2], wacc[:, t, cs],
                                              ALU.add), (mm, *summed), "wacc")
                        banks.give(bi, s)
                        step["sum"] = s
                        yield
                    nT.give(ti, mm)

                yield from in_step([(0, rows_in), (1, times)], NT)
                w_free, summed = (("wout_mm", L.count["wout_mm"]),), (step["sum"],)

        def mix_then_nodes(end):
            yield from linear_attention(Ring(bank[3:7], end), bank[7], end)
            area.clear()
            end = fence()
            yield from mix_projection(Ring(bank[3:8], end), end)
            area.clear(NT * D)
            end = fence()
            yield from node_projection(Ring(bank[3:8], end), end, wacc)

        area.clear()
        wacc = area.take([P, NT, D])
        area.clear()
        sg = ExitStack()
        run((graph_attention(bank[0:3], sg, end2), 1), (mix_then_nodes(end2), RATE))
        sg.close()
        s_edges.close()
        end5 = fence()

        x2 = wacc
        area.clear(NT * D)
        xf = area.take([P, NT, D])
        pm = sb(ctx, "pm", [P, 8, NT])
        slot = sb(ctx, "slot", [P, 2, NT], U32)

        def experts(banks, sp, end):
            b1c = sb(sp, "b1c", [128, EXPERTS, KF])
            g_b1 = L.load(b1c[:, :, :], b1_cols, end, "b1_in")
            st1 = Ring([sb(sp, f"w1_stage{i}", [128, KD, F]) for i in range(2)])
            st2 = Ring([sb(sp, f"w2_stage{i}", [128, KF, D]) for i in range(2)])
            w1b = Ring([[sb(sp, f"w1b{i}_{p}", [128, KD, F], BF16) for p in ("hi", "lo")] for i in range(2)])
            w2b = Ring([[sb(sp, f"w2b{i}_{p}", [128, KF, D], BF16) for p in ("hi", "lo")] for i in range(2)])
            b2r = Ring([sb(sp, f"b2r{i}", [128, D]) for i in range(2)])
            hf = Ring([sb(sp, f"hf{i}", [128, CAP]) for i in range(2)])
            hT = Ring([[sb(sp, f"hT{i}_{p}", [128, KF, CAP], BF16) for p in ("hi", "lo")] for i in range(2)])
            orow = Ring([sb(sp, f"orow{i}", [128, D]) for i in range(2)])
            for r in (st1, st2, w1b, w2b, b2r, hf, hT, orow):
                for i in range(len(r.buffers)):
                    r.give(i, *end)
            rt = ExitStack()
            bo = sb(rt, "bo", [P, D])
            mi = [sb(rt, f"mi{i}", [P, D]) for i in range(2)]
            stats = sb(rt, "stats3", [P, NT, 16])
            sw = sb(rt, "sw", [128, KD, EXPERTS])
            sws = [sb(rt, f"sw_{p}", [128, KD, EXPERTS], BF16) for p in ("hi", "lo")]
            sbias = sb(rt, "sbias", [P, EXPERTS])
            fT = Ring([[sb(rt, f"fT{i}_{p}", [128, KD, P], BF16) for p in ("hi", "lo")] for i in range(2)])
            iota8i, iota8 = sb(rt, "iota8i", [P, EXPERTS], I32), sb(rt, "iota8", [P, EXPERTS])
            idx_i, idx = sb(rt, "idx_i", [P, NT], I32), sb(rt, "idx", [P, NT])
            lg = sb(rt, "lg", [P, NT, EXPERTS])
            ex = sb(rt, "ex", [P, NT, EXPERTS])
            z = L.store(slot_rows[0:SLOTS, :].rearrange("(t p) c -> p t c", p=120),
                        zero[0:120, 0:D].unsqueeze(1).broadcast_to([120, SLOTS // 120, D]), (), "slot_zero")
            b_got = L.load(bo[:, :], b_out.partition_broadcast(P), end, "bias_in")
            g = L.load(sw[:, :, :], switch_w.rearrange("(k p) e -> p k e", p=128), end, "switch_in")
            sw_done = split(sw[:, :, :], sws[0][:, :, :], sws[1][:, :, :], (g,))
            g_bias = L.load(sbias[:, :], switch_b.partition_broadcast(P), end, "switch_b_in")
            t = L.pool(partial(G.iota, iota8i[:, :], pattern=[[1, EXPERTS]], base=0, channel_multiplier=0),
                       end, "late_iota")
            t = L.pool(partial(G.iota, idx_i[:, :], pattern=[[P, NT]], base=SLOTS, channel_multiplier=1),
                       (), "late_iota")
            i8 = L.dve(partial(V.tensor_copy, iota8[:, :], iota8i[:, :]), (t, *end), "late_consts")
            i8 = L.dve(partial(V.tensor_copy, idx[:, :], idx_i[:, :]), (t,), "late_consts")
            done = {}

            def new_x(t):
                got = L.load(mi[t % 2][:, :], mixed_rows[t * P:(t + 1) * P, :],
                             (*end, done.get(("x2", t - 2)), L.stores["mixed_out0"], L.stores["mixed_out1"]),
                             f"rows_in{t % 2}")
                a = L.dve(partial(V.tensor_tensor, x2[:, t, :], wacc[:, t, :], bo[:, :], ALU.add),
                          (b_got, *end), "x2")
                a = L.dve(partial(V.scalar_tensor_tensor, x2[:, t, :], x2[:, t, :], 0.0, mi[t % 2][:, :],
                                                                ALU.max, ALU.add), (a, got), "x2")
                done["x2", t] = a
                a = row_stats(x2[:, t, :], stats[:, t, :], (a,))
                if t % 5 == 4:
                    a = inverse_root(stats[:, t - 4:t + 1, :], (a,))
                    for u in range(t - 4, t + 1):
                        done["xf", u] = normalise(x2[:, u, :], xf[:, u, :], stats[:, u, :], (a,))

            def logits(t):
                ti, f, free = fT.take()
                d, tt = transposed(xf[:, t, :], KD, f[0], f[1], banks, (done["xf", t], *free))
                bi, b, free = banks.take()
                for k in range(KD):
                    mm = product(b[0:P, 0:EXPERTS], [v[:, k, :] for v in f], [v[:, k, :] for v in sws],
                                 k == 0, k == KD - 1, (*free, d, sw_done), "logit_mm" if k == KD - 1 else None)
                fT.give(ti, mm)
                a = L.dve(partial(V.tensor_tensor, lg[:, t, :], b[0:P, 0:EXPERTS], sbias[:, :], ALU.add),
                          (mm, g_bias), "route")
                banks.give(bi, a)
                a = L.dve(partial(V.tensor_reduce, pm[:, 0, t:t + 1], lg[:, t, :], AX.X, ALU.max), (a,), "route")
                a = L.dve(partial(V.tensor_scalar, lg[:, t, :], lg[:, t, :], pm[:, 0, t:t + 1], None,
                                                         ALU.subtract), (a,), "route")
                a2 = L.act(partial(A.activation, ex[:, t, :], lg[:, t, :], ACT.Exp,
                                                       accum_out=pm[:, 7, t:t + 1]), (a,), "route_exp")
                a3 = L.dve(partial(V.reciprocal, pm[:, 1, t:t + 1], pm[:, 7, t:t + 1]), (a2,), "route")
                a = L.dve(partial(V.tensor_scalar, lg[:, t, :], lg[:, t, :], 0.0, float(EXPERTS), ALU.is_lt,
                                                         ALU.mult), (a2,), "route")
                a = L.dve(partial(V.tensor_tensor, lg[:, t, :], lg[:, t, :], iota8[:, :], ALU.add),
                          (a, i8), "route")
                a = L.dve(partial(V.tensor_reduce, pm[:, 2, t:t + 1], lg[:, t, :], AX.X, ALU.min), (a,), "route")
                done["route"] = a

            yield from in_step([(0, new_x), (5, logits)], NT)
            rr = sb(rt, "rr", [2 * NT, P])
            bi, b, free = banks.take()
            tt = L.pe(partial(T.transpose, b[0:2 * NT, 0:P], pm[:, 1:3, :].rearrange("p a t -> p (a t)"), identP),
                      (*free, done["route"]), "turned")
            a = L.dve(partial(V.tensor_copy, rr[:, :], b[0:2 * NT, 0:P]), (tt, *end), "route_row")
            banks.give(bi, a)
            s = L.store(route_rows.rearrange("a (t p) -> (a t) p", p=P), rr[:, :], (a,), "route_rows_out")
            pr, ro = sb(rt, "pr", [P, N]), sb(rt, "ro", [P, N])
            g0 = L.load(pr[:, :], route_rows[0, :].partition_broadcast(P), (s, *end), "route_in")
            g1 = L.load(ro[:, :], route_rows[1, :].partition_broadcast(P), (s, *end), "route_in")
            earlier = sb(rt, "earlier", [P, P])
            t = L.pool(partial(G.memset, earlier[:, :], 1.0), end, "late_iota")
            t_e = L.pool(partial(G.affine_select, out=earlier[:, :], in_=earlier[:, :], compare_op=ALU.is_gt,
                                                   fill=0.0, base=0, pattern=[[-1, P]], channel_multiplier=1),
                         (t,), "late_iota")
            mates = [sb(rt, f"mates{i}", [P, N]) for i in range(2)]
            won = sb(rt, "won", [P, N], BF16)
            cnt = sb(rt, "cnt", [P, 4, NT])
            c = L.dve(partial(V.memset, cnt[:, :, :], 0.0), end, "ranks")
            for t in range(NT):
                mt = mates[t % 2]
                lo, hi = t * P, (t + 1) * P
                prob, route = pm[:, 1, t:t + 1], pm[:, 2, t:t + 1]
                a = L.dve(partial(V.tensor_scalar, mt[:, :], ro[:, :], route, None,
                                                                        ALU.is_equal), (g1, c), "ranks")
                parts = [(0, lo, ALU.is_ge, 0), (lo, hi, ALU.is_gt, 1), (hi, N, ALU.is_gt, 2)]
                for p0, p1, op, j in parts:
                    if p1 > p0:
                        c = L.dve(partial(V.scalar_tensor_tensor, won[:, p0:p1], pr[:, p0:p1], prob, mt[:, p0:p1], op, ALU.mult,
                            accum_out=cnt[:, j, t:t + 1]), (a, c), "ranks")
                c = L.dve(partial(V.scalar_tensor_tensor, mt[:, lo:hi], pr[:, lo:hi], prob, mt[:, lo:hi], ALU.is_equal, ALU.mult), (c,), "ranks")
                c = L.dve(partial(V.scalar_tensor_tensor, won[:, lo:hi], mt[:, lo:hi], 1.0, earlier[:, :], ALU.mult, ALU.mult,
                    accum_out=cnt[:, 3, t:t + 1]), (c, t_e), "ranks")
            c = L.dve(partial(V.tensor_reduce, pm[:, 3, :], cnt[:, :, :].rearrange("p a t -> p t a"), AX.X,
                                                ALU.add), (c,), "ranks")
            keep = L.dve(partial(V.tensor_scalar, pm[:, 4, :], pm[:, 3, :], float(CAP), None, ALU.is_lt),
                         (c,), "ranks")
            a = L.dve(partial(V.scalar_tensor_tensor, pm[:, 5, :], pm[:, 2, :], float(CAP), pm[:, 3, :], ALU.mult,
                                                       ALU.add), (keep,), "ranks")
            a = L.dve(partial(V.tensor_tensor, pm[:, 6, :], pm[:, 5, :], idx[:, :], ALU.subtract), (a,), "ranks")
            a = L.dve(partial(V.tensor_tensor, pm[:, 6, :], pm[:, 6, :], pm[:, 4, :], ALU.mult), (a,), "ranks")
            a = L.dve(partial(V.tensor_tensor, slot[:, 0, :], pm[:, 6, :], idx[:, :], ALU.add), (a,), "ranks")
            a = L.dve(partial(V.tensor_tensor, slot[:, 1, :], pm[:, 5, :], pm[:, 4, :], ALU.mult), (a,), "ranks")
            a = L.dve(partial(V.tensor_tensor, pm[:, 5, :], pm[:, 4, :], pm[:, 1, :], ALU.mult), (a,), "ranks")
            ranked = L.dve(partial(V.tensor_tensor, pm[:, 6, :], pm[:, 1, :], pm[:, 5, :], ALU.subtract), (a,),
                           "ranks")
            yield
            for t in range(NT):
                L.put(POOL, partial(G.indirect_dma_start, slot_rows, bass.IndirectOffsetOnAxis(slot[:, 0, t:t + 1], axis=0), xf[:, t, :], None),
                    (ranked, z), "to_slots", 16)
                own = L.dve(partial(V.scalar_tensor_tensor, x2[:, t, :], xf[:, t, :], pm[:, 6, t:t + 1],
                                                                  x2[:, t, :], ALU.mult, ALU.add), (ranked,), "own")
            placed = ("to_slots", L.count["to_slots"])
            SP, ST = 120, SLOTS // 120
            rt.close()
            routed = fence()
            sT = [sb(sp, f"sT_{p}", [128, KD, SLOTS], BF16) for p in ("hi", "lo")]
            sr = Ring([area.take([P, D]) for i in range(2)])
            for i in range(2):
                sr.give(i, *routed)
            sT_done = {}
            for t in range(ST):
                ri, r, free = sr.take()
                got = L.load(r[0:SP, :], slot_rows[t * SP:(t + 1) * SP, :], (*free, placed), f"rows_in{ri}")
                for g in range(KD // 3):
                    bi, b, free = banks.take()
                    for k in range(3):
                        kk = 3 * g + k
                        tt = L.pe(partial(T.transpose, b[:, k * SP:(k + 1) * SP], r[0:SP, kk * 128:(kk + 1) * 128], ident[0:SP, 0:SP]),
                            (*free, got), "turned" if k == 2 else None)
                    bv = b[:, 0:3 * SP].rearrange("p (k n) -> p k n", k=3)
                    sT_done[t] = d = split(bv, *[v[:, 3 * g:3 * g + 3, t * SP:(t + 1) * SP] for v in sT],
                                           (tt, *routed))
                    banks.give(bi, d)
                sr.give(ri, tt)
                if t % 2:
                    yield
            ws, hs = {}, {}

            def weights(x_):
                i1, s1_, f1 = st1.take()
                g1_ = L.load(s1_[:, :, :], w1[x_].rearrange("(k p) f -> p k f", p=128), f1, f"w1_in{i1}")
                j1, wb1, fb1 = w1b.take()
                d1 = split(s1_[:, :, :].rearrange("p k f -> p (k f)"),
                           *[v[:, :, :].rearrange("p k f -> p (k f)") for v in wb1], (g1_, *fb1))
                st1.give(i1, d1)
                i2, s2_, f2 = st2.take()
                g2_ = L.load(s2_[:, :, :], w2[x_].rearrange("(k p) d -> p k d", p=128), f2, f"w2_in{i2}")
                j2, wb2, fb2 = w2b.take()
                d2 = split(s2_[:, :, :].rearrange("p k f -> p (k f)"),
                           *[v[:, :, :].rearrange("p k f -> p (k f)") for v in wb2], (g2_, *fb2))
                st2.give(i2, d2)
                i3, br, f3 = b2r.take()
                g3 = L.load(br[:, :], b2[x_].partition_broadcast(128), f3, f"b2_in{i3}")
                ws[x_] = (j1, wb1, d1, j2, wb2, d2, i3, br, g3)

            def first(x_):
                j1, wb1, d1, *_ = ws[x_]
                hi_, h, h_free = hT.take()
                for f in range(KF):
                    bi, b, free = banks.take()
                    for k in range(KD):
                        mm = product(b[:, 0:CAP], [v[:, k, f * 128:(f + 1) * 128] for v in wb1],
                                     [v[:, k, x_ * CAP:(x_ + 1) * CAP] for v in sT], k == 0, k == KD - 1,
                                     (*free, d1, sT_done[ST - 1]), "w1_mm" if k == KD - 1 else None)
                    fi, hff, f_free = hf.take()
                    a = L.act(partial(A.activation, hff[:, :], b[:, 0:CAP], ACT.Gelu, bias=b1c[:, x_, f:f + 1]), (mm, g_b1, *f_free), "gelu")
                    banks.give(bi, a)
                    d = split(hff[:, :], h[0][:, f, :], h[1][:, f, :], (a, *h_free))
                    hf.give(fi, d)
                w1b.give(j1, mm)
                hs[x_] = (hi_, h, d)

            def second(x_):
                j1, wb1, d1, j2, wb2, d2, i3, br, g3 = ws.pop(x_)
                hi_, h, ready = hs.pop(x_)
                for r0, r1 in ((0, 98), (98, CAP)):
                    oi, ob, o_free = orow.take()
                    for half in range(2):
                        cs = slice(half * (D // 2), (half + 1) * (D // 2))
                        bi, b, free = banks.take()
                        for f in range(KF):
                            mm = product(b[0:r1 - r0, 0:D // 2], [v[:, f, r0:r1] for v in h],
                                         [v[:, f, cs] for v in wb2], f == 0, f == KF - 1,
                                         (*free, ready, d2), "w2_mm" if f == KF - 1 else None)
                        a = L.dve(partial(V.tensor_tensor, ob[0:(r1 - r0), cs], b[0:(r1 - r0), 0:D // 2], br[0:(r1 - r0), cs], ALU.add), (mm, g3, *o_free), "expert_row")
                        banks.give(bi, a)
                    o = L.store(expert_rows[x_ * CAP + r0:x_ * CAP + r1, :], ob[0:r1 - r0, :], (a,),
                                f"expert_out{oi}")
                    orow.give(oi, o)
                hT.give(hi_, mm)
                w2b.give(j2, mm)
                b2r.give(i3, a)

            yield from in_step([(2, second), (0, weights), (1, first)], EXPERTS)
            stored = (L.stores["expert_out0"], L.stores["expert_out1"])
            for t in range(NT):
                fi, f, free = sr.take()
                got = L.put(POOL, partial(G.indirect_dma_start, f[:, :], None, expert_rows, bass.IndirectOffsetOnAxis(slot[:, 1, t:t + 1], axis=0)),
                    (*free, *stored, ranked), f"fetch{fi}", 16)
                a = L.dve(partial(V.scalar_tensor_tensor, f[:, :], f[:, :], pm[:, 5, t:t + 1],
                                                                    x2[:, t, :], ALU.mult, ALU.add),
                          (got, own), "result")
                o = L.store(out[t * P:(t + 1) * P, :], f[:, :], (a,), f"result_out{fi}")
                sr.give(fi, o)
                yield

        spe = ExitStack()
        run((experts(Ring(bank[0:8]), spe, end5), 1))
        spe.close()
        for token in L.stores.values():
            L.put(SYNC, None, (token,))
        block = ctx.enter_context(nc.Block())
        L.emit(block)


_SHAPE = (N, D)


def kernel(**inputs):
    import numpy as _np
    import concourse.bacc as _bacc
    from concourse import mybir as _mybir
    from concourse.bass_utils import run_bass_kernel_spmd as _run

    g = {k: _np.asarray(v) for k, v in inputs.items()}
    laid = {
        "x": g["x"], "src_rows": g["src"], "dst_rows": g["dst"],
        "src_cols": g["src"].reshape(CHUNKS, P).T, "dst_cols": g["dst"].reshape(CHUNKS, P).T,
        "W_ah": g["L0_gnn_W_ah"], "b_ah": g["L0_gnn_b_ah"].reshape(KD, 128).T,
        "W0": g["L0_gnn_W0"], "W1": g["L0_gnn_W1"], "W2": g["L0_gnn_W2"],
        "a_src": _np.stack([g[f"L0_gnn_a_src{i}"] for i in range(LAYERS)]),
        "a_dst": _np.stack([g[f"L0_gnn_a_dst{i}"] for i in range(LAYERS)]),
        "bg": _np.stack([g[f"L0_gnn_b{i}"] for i in range(LAYERS)]),
        "W_out": g["L0_gnn_W_out"], "b_out": g["L0_gnn_b_out"],
        "wT_qkv": g["L0_mix_w_qkv"].T, "wT_proj": g["L0_mix_w_proj"].T, "b_proj": g["L0_mix_b_proj"],
        "projT": g["L0_mix_proj_mat"].T, "switch_w": g["L0_ffn_switch_w"], "switch_b": g["L0_ffn_switch_b"],
        "w1": g["L0_ffn_w1"], "b1_cols": g["L0_ffn_b1"].reshape(EXPERTS, KF, 128).transpose(2, 0, 1),
        "w2": g["L0_ffn_w2"], "b2": g["L0_ffn_b2"],
    }
    nc = _bacc.Bacc("TRN2", target_bir_lowering=False, num_devices=1)
    arrays, ap = {}, {}
    for name, a in laid.items():
        a = _np.ascontiguousarray(a)
        arrays[f"in_{name}"] = a
        ap[name] = nc.dram_tensor(f"in_{name}", a.shape, _mybir.dt.from_np(a.dtype), kind="ExternalInput").ap()
    out = nc.dram_tensor("out_x", _SHAPE, _mybir.dt.float32, kind="ExternalOutput").ap()
    program(nc, ap["x"], ap["src_rows"], ap["dst_rows"], ap["src_cols"], ap["dst_cols"], ap["W_ah"], ap["b_ah"],
            [ap["W0"], ap["W1"], ap["W2"]], ap["a_src"], ap["a_dst"], ap["bg"], ap["W_out"], ap["b_out"],
            ap["wT_qkv"], ap["wT_proj"], ap["b_proj"], ap["projT"], ap["switch_w"], ap["switch_b"], ap["w1"],
            ap["b1_cols"], ap["w2"], ap["b2"], out)
    r = _run(nc, [arrays], core_ids=[0])
    return r.results[0]["out_x"]
```

```python
from contextlib import ExitStack
from functools import partial

import numpy as np

import concourse.bass as bass
from concourse import mybir

ALU = mybir.AluOpType
ACT = mybir.ActivationFunctionType
AX = mybir.AxisListType
F32 = mybir.dt.float32
BF16 = mybir.dt.bfloat16
I32 = mybir.dt.int32
U32 = mybir.dt.uint32
U16 = mybir.dt.uint16

PE, DVE, SCAL, POOL, SYNC = "tensor", "vector", "scalar", "gpsimd", "sync"

BLOCKS = {PE: lambda b, f: b.tensor(f), DVE: lambda b, f: b.vector(f), SCAL: lambda b, f: b.scalar(f),
          POOL: lambda b, f: b.gpsimd(f), SYNC: lambda b, f: b.sync(f)}

N, D, E = 1250, 768, 21250
P = 125
NT = N // P
KD = D // 128
LAYERS, GH, GC = 3, 4, 192
LH = LAYERS * GH
SLOPE = 0.2
LN_EPS = 1e-5
SOFTMAX_EPS = 1e-16
HEADS, HD, FEATS = 12, 64, 256
PAIRS = HEADS // 2
MT = FEATS // 128
NORM = HD ** -0.25
RATIO = FEATS ** -0.5
EPS = 1e-4
EXPERTS, F = 8, 384
KF = F // 128
AREA = 68224
CAP = int(1.25 * N / EXPERTS)
SLOTS = EXPERTS * CAP
CHUNKS = E // P
TABLES = 2
PIECES = 10
CP = CHUNKS // PIECES
HW = 2 * (GC + 2)
BIG = 3e38
LATER = 1024.0
COLS = [(c, min(c + 4 * P, N)) for c in range(0, N, 4 * P)]
SP = 120
ST = SLOTS // SP
FETCHES = 4
NODE_RATE = 2
COUNT_RATE = 1.6
COUNT_DELAY = 20
MIX_RATE = 1.0
LOAD_DELAY = 12
MATE_TURN = 3


class Lanes:

    def __init__(self, nc, ctx):
        self.nc, self.ctx = nc, ctx
        self.dma = {SYNC: nc.sync.dma_start, SCAL: nc.scalar.dma_start, POOL: nc.gpsimd.dma_start}
        self.queues = {e: [] for e in (PE, DVE, SCAL, POOL, SYNC)}
        self.count, self.owner, self.sems = {}, {}, {}
        self.stores = {}

    def put(self, engine, issue, after=(), signal=None, by=1):
        self.queues[engine].append((tuple(t for t in after if t), issue, signal, by))
        if signal is None:
            return None
        if signal not in self.sems:
            self.sems[signal] = self.ctx.enter_context(self.nc.semaphore(signal))
            self.count[signal], self.owner[signal] = 0, engine
        assert self.owner[signal] == engine, signal
        self.count[signal] += by
        return signal, self.count[signal]

    def pe(self, issue, after=(), signal=None):
        return self.put(PE, issue, after, signal)

    def dve(self, issue, after=(), signal=None):
        return self.put(DVE, issue, after, signal)

    def act(self, issue, after=(), signal=None):
        return self.put(SCAL, issue, after, signal)

    def pool(self, issue, after=(), signal=None):
        return self.put(POOL, issue, after, signal)

    def load(self, dst, src, after=(), signal=None, engine=SYNC):
        return self.put(engine, partial(self.dma[engine], dst, src), after, signal, 16)

    def store(self, dst, src, after=(), signal=None, engine=SYNC):
        token = self.put(engine, partial(self.dma[engine], dst, src), after, signal, 16)
        self.stores[token[0]] = token
        return token

    def emit(self, block):
        for name, queue in self.queues.items():
            def instructions(eng, queue=queue):
                passed = {}
                for after, issue, signal, by in queue:
                    for sem, value in after:
                        if passed.get(sem, 0) < value:
                            eng.wait_ge(self.sems[sem], value)
                            passed[sem] = value
                    ins = issue() if issue else None
                    if signal:
                        ins.then_inc(self.sems[signal], by)
            BLOCKS[name](block, instructions)


class Ring:

    def __init__(self, buffers, free=()):
        self.buffers, self.free, self.n = buffers, [free for _ in buffers], 0
        self.held = [False] * len(buffers)

    def take(self):
        i = self.n % len(self.buffers)
        self.n += 1
        assert not self.held[i], "the ring is too short"
        self.held[i] = True
        return i, self.buffers[i], self.free[i]

    def give(self, i, *tokens):
        self.free[i], self.held[i] = tokens, False


def in_step(stages, n):
    for i in range(n + max(lag for lag, _ in stages)):
        for lag, step in stages:
            if 0 <= i - lag < n:
                yield from step(i - lag) or ()
        yield


def run(*tracks):
    live = [[steps, rate, 0.0] for steps, rate in tracks]
    while live:
        for track in list(live):
            track[2] += track[1]
            while track[2] >= 1:
                track[2] -= 1
                if next(track[0], "over") == "over":
                    live.remove(track)
                    break


class Area:

    def __init__(self, memory):
        self.memory, self.used = memory, 0

    def take(self, shape, dt=F32):
        words = (int(np.prod(shape[1:])) * (2 if dt == BF16 else 4) + 3) // 4
        view = self.memory[0:shape[0], self.used:self.used + words]
        self.used += words
        assert self.used <= self.memory.shape[1], "the area is too small"
        view = view if dt == F32 else view.bitcast(dt)
        names = "abcdefg"[:len(shape) - 1]
        sizes = {n: size for n, size in zip(names, shape[1:])}
        return view.rearrange(f"p ({' '.join(names)}) -> p {' '.join(names)}", **sizes)

    def clear(self, used=0):
        self.used = used


def program(nc, x, src_rows, dst_rows, src_cols, dst_cols, W_ah, b_ah, Wg, a_src, a_dst, bg, W_out, b_out,
            wT_qkv, wT_proj, b_proj, projT, switch_w, switch_b, w1, b1_cols, w2, b2, out):
    ctx = ExitStack()
    with ctx:
        L = Lanes(nc, ctx)
        T, V, A, G = nc.tensor, nc.vector, nc.scalar, nc.gpsimd

        def sb(stack, name, shape, dt=F32):
            return stack.enter_context(nc.sbuf_tensor(name, shape, dt))

        def dram(name, shape, dt=F32):
            return nc.dram_tensor(name, shape, dt).ap()

        bank = [ctx.enter_context(nc.psum_tensor(f"bank{i}", [128, 512], F32)) for i in range(8)]

        key_rows = dram("key_rows", (E,))
        tables = [dram(f"table{i}", (N * N + P, 1)) for i in range(TABLES)]
        h_rows = dram("h_rows", (LAYERS, N, GH, HW), BF16)
        as_rows = dram("as_rows", (8 * LAYERS, N))
        shift_rows = dram("shift_rows", (LAYERS, 2 * GH, N))
        qk_rows = dram("qk_rows", (2, PAIRS, 128, 2, N), BF16)
        v_rows = dram("v_rows", (PAIRS, N, 2 * (HD + 1)))
        node_rows = dram("node_rows", (N, LAYERS * D))
        mixed_rows = dram("mixed_rows", (N, D))
        attn_rows = dram("attn_rows", (N, D))
        slot_rows = dram("slot_rows", (SLOTS + N, D))
        expert_rows = dram("expert_rows", (SLOTS, D))
        route_rows = dram("route_rows", (2, N))

        ident = sb(ctx, "ident", [128, 128])
        zero = sb(ctx, "zero", [128, D])
        ones = sb(ctx, "ones", [128, 128])
        halves = sb(ctx, "halves", [128, 2])
        t_zero = L.dve(partial(V.memset, zero[:, :], 0.0), (), "consts_set")
        t_ones = L.dve(partial(V.memset, ones[:, :], 1.0), (), "consts_set")
        t = L.pool(partial(G.memset, ident[:, :], 0.0), (), "consts")
        t = L.pool(partial(G.affine_select, out=ident[:, :], in_=ident[:, :], compare_op=ALU.not_equal, fill=1.0,
                           base=0, pattern=[[-1, 128]], channel_multiplier=1), (t,), "consts")
        t_ident = t
        t = L.pool(partial(G.memset, halves[:, :], 1.0), (), "consts")
        t = L.pool(partial(G.affine_select, out=halves[:, 0:1], in_=halves[:, 0:1], compare_op=ALU.is_ge, fill=0.0,
                           base=63, pattern=[[0, 1]], channel_multiplier=-1), (t,), "consts")
        t_halves = L.pool(partial(G.affine_select, out=halves[:, 1:2], in_=halves[:, 1:2], compare_op=ALU.is_ge,
                                  fill=0.0, base=-64, pattern=[[0, 1]], channel_multiplier=1),
                          (t,), "consts")
        identP = ident[0:P, 0:P]

        def split(src, hi, lo, after, hi_after=()):
            a = L.act(partial(A.activation, hi, src, ACT.Copy), (*after, *hi_after), "high_part")
            return L.dve(partial(V.tensor_tensor, lo, src, hi, ALU.subtract), (a,), "low_part")

        def product(out_ap, lhs, rhs, first, last, after=(), signal=None, skip=False):
            terms = [(lhs[0], rhs[0]), (lhs[0], rhs[1]), (lhs[1], rhs[0])]
            token = None
            for n, (l, r) in enumerate(terms):
                token = L.pe(partial(T.matmul, out_ap, l, r, start=first and n == 0,
                                     stop=last and n == 2, skip_group_check=skip),
                             after if n == 0 else (), signal if n == 2 else None)
            return token

        def load_split(stage, pieces, after=()):
            tokens = []
            for d, hi, lo in pieces:
                i, buf, free = stage.take()
                v = buf[0:d.shape[0], 0:d.shape[1]]
                got = L.load(v, d, free, f"w_in{i}")
                done = split(v, hi, lo, (got, *after))
                stage.give(i, done)
                tokens.append(done)
            return tokens

        def load_split_spread(stage, pieces, after=(), signal="w_in"):
            waiting, tokens = [], []

            def part():
                i, v, hi, lo, got = waiting.pop(0)
                done = split(v, hi, lo, (got, *after))
                stage.give(i, done)
                tokens.append(done)

            for d, hi, lo in pieces:
                if len(waiting) == len(stage.buffers):
                    yield
                    part()
                i, buf, free = stage.take()
                v = buf[0:d.shape[0], 0:d.shape[1]]
                waiting.append((i, v, hi, lo, L.load(v, d, free, f"{signal}{i}")))
            while waiting:
                yield
                part()
            return tokens

        def transposed(src, blocks, dst_hi, dst_lo, banks, after, relu=False):
            done, freed = None, None
            for g in range(blocks // 3):
                i, b, free = banks.take()
                for k in range(3):
                    kk = 3 * g + k
                    turned = L.pe(partial(T.transpose, b[:, k * P:(k + 1) * P],
                                          src[:, kk * 128:(kk + 1) * 128], identP),
                                  (*free, *after, t_ident) if k == 0 else (), "turned" if k == 2 else None)
                ps = b[:, 0:3 * P].rearrange("p (k n) -> p k n", k=3)
                hi, lo = dst_hi[:, 3 * g:3 * g + 3, :], dst_lo[:, 3 * g:3 * g + 3, :]
                fn = ACT.Relu if relu else ACT.Copy
                a = L.act(partial(A.activation, hi, ps, fn), (turned,), "turned_high")
                if relu:
                    done = L.dve(partial(V.scalar_tensor_tensor, lo, ps, 0.0, hi, ALU.max, ALU.subtract),
                                 (a,), "turned_low")
                else:
                    done = L.dve(partial(V.tensor_tensor, lo, ps, hi, ALU.subtract),
                                 (a,), "turned_low")
                banks.give(i, done)
            return done, turned

        def dash(parts, ts, banks, after):
            bi, b, free = banks.take()
            mm = product(b[0:P, :], [parts[:, p, ts] for p in range(2)], [v[:, :] for v in feats], True, True,
                         (*free, *after), "dash_mm")
            return bi, b[0:P, :].rearrange("p (h m) -> p h m", h=2), mm

        def row_stats(xin, st, after):
            L.dve(partial(V.bn_stats, st[:, 0:6], xin[:, 0:D // 2]), after, "normed")
            a = L.dve(partial(V.bn_stats, st[:, 6:12], xin[:, D // 2:D]), (), "normed")
            return L.dve(partial(V.bn_aggr, st[:, 12:14], st[:, 0:12]), (a,), "normed")

        def inverse_root(st, after):
            v, r, u = st[:, :, 13], st[:, :, 14], st[:, :, 15]
            a = L.dve(partial(V.tensor_scalar, v, v, LN_EPS, None, ALU.add), after, "rstd")
            a = L.act(partial(A.activation, u, v, ACT.Sqrt), (a,), "root")
            a = L.dve(partial(V.reciprocal, r, u), (a,), "rstd")
            a = L.dve(partial(V.tensor_tensor, u, v, r, ALU.mult), (a,), "rstd")
            a = L.dve(partial(V.tensor_tensor, u, u, r, ALU.mult), (a,), "rstd")
            a = L.dve(partial(V.tensor_scalar, u, u, -0.5, 1.5, ALU.mult, ALU.add), (a,), "rstd")
            return L.dve(partial(V.tensor_tensor, r, r, u, ALU.mult), (a,), "rstd")

        def normalise(xin, xout, st, after):
            return L.dve(partial(V.tensor_scalar, xout, xin, st[:, 12:13], st[:, 14:15], ALU.subtract, ALU.mult),
                         after, "normed")

        def fence(besides=()):
            return tuple((s, c) for s, c in L.count.items() if s not in besides)

        asd = sb(ctx, "asd", [P, NT, 8 * LAYERS])
        as_low = sb(ctx, "as_low", [P, NT, LH])
        diag = sb(ctx, "diag", [P, 2, NT, HEADS])
        k_shift = sb(ctx, "k_shift", [P, NT, HEADS])
        feats = [sb(ctx, f"feats_{p}", [128, 2 * FEATS], BF16) for p in ("hi", "lo")]
        area = Area(sb(ctx, "area", [128, AREA // 4]))
        s_edges = ExitStack()
        m_col = sb(s_edges, "m_col", [P, LH, NT])
        shift = sb(s_edges, "shift", [P, LAYERS, NT, 2 * GH])
        count = sb(s_edges, "count", [P, NT, N], U16)
        s0 = ExitStack()
        xnT = [sb(s0, f"xnT_{p}", [128, KD, N], BF16) for p in ("hi", "lo")]
        s1 = ExitStack()
        xs = area.take([P, NT, D])
        area.clear()
        x1T = [area.take([128, KD, N], BF16) for p in range(2)]
        area.clear(NT * D)
        wide = D + 8
        w_ring = Ring([[area.take([128, KD, wide], BF16) for p in range(2)] for i in range(2)])
        stage = Ring([sb(s1, f"stage{i}", [128, wide]) for i in range(3)])
        all_banks = Ring(bank[0:8])

        cols = [sb(s1, f"edge_cols{i}", [P, CHUNKS], I32) for i in range(2)]
        rows = [sb(s1, f"edge_rows{i}", [P, CHUNKS], I32) for i in range(2)]
        key_c, key_r = sb(s1, "key_c", [P, CHUNKS]), sb(s1, "key_r", [P, CHUNKS])
        spread = [sb(s1, f"spread{i}", [P, CP * P]) for i in range(2)]
        same = [sb(s1, f"same{i}", [P, P]) for i in range(2)]
        later = sb(s1, "later", [P, P])
        amount = sb(s1, "amount", [P, CHUNKS])
        spare_i = sb(s1, "spare_i", [P, 1], I32)
        spare = sb(s1, "spare", [P, 1])
        moved = sb(s1, "moved", [P, CHUNKS])
        place = sb(s1, "place", [P, CHUNKS], U32)

        def edges():
            got_r = [L.load(rows[i][:, :], d.rearrange("(a b) -> a b", a=P), (), "edge_rows_in")
                     for i, d in enumerate((src_rows, dst_rows))]
            got_c = [L.load(cols[i][:, :], d, (), "edge_cols_in") for i, d in enumerate((src_cols, dst_cols))]
            kr = L.dve(partial(V.scalar_tensor_tensor, key_r[:, :], rows[0][:, :], float(N), rows[1][:, :],
                               ALU.mult, ALU.add), got_r[1:], "keys")
            L.dve(partial(V.scalar_tensor_tensor, key_c[:, :], cols[0][:, :], float(N), cols[1][:, :],
                               ALU.mult, ALU.add), got_c[1:], "keys")
            kept = L.store(key_rows.rearrange("(a b) -> a b", a=P), key_r[:, :], (kr,), "key_rows_out")
            t = L.pool(partial(G.memset, later[:, :], 1.0), (), "consts")
            t = L.pool(partial(G.affine_select, out=later[:, :], in_=later[:, :], compare_op=ALU.is_ge, fill=LATER,
                               base=0, pattern=[[1, P]], channel_multiplier=-1),
                       (t,), "consts")
            t = L.pool(partial(G.iota, spare_i[:, :], pattern=[[0, 1]], base=N * N, channel_multiplier=1),
                       (t,), "consts")
            t_sp = L.dve(partial(V.tensor_copy, spare[:, :], spare_i[:, :]), (t,), "keys")
            read = [(), ()]

            def spread_in(q):
                return L.load(spread[q % 2][:, :], key_rows[q * CP * P:(q + 1) * CP * P].partition_broadcast(P),
                              (kept, *read[q % 2]), f"spread_in{q % 2}")

            following = spread_in(0)
            yield
            for q in range(PIECES):
                got = following
                if q + 1 < PIECES:
                    following = spread_in(q + 1)
                for j in range(CP):
                    c = q * CP + j
                    a = L.dve(partial(V.scalar_tensor_tensor, same[c % 2][:, :], spread[q % 2][:, j * P:(j + 1) * P],
                                      key_c[:, c:c + 1], later[:, :],
                                      ALU.is_equal, ALU.mult, accum_out=amount[:, c:c + 1]),
                              (got, t_sp, ("same_key", c - 1) if c >= 2 else None), "same_key")
                read[q % 2] = (a,)
                cs = slice(q * CP, (q + 1) * CP)
                b = L.dve(partial(V.tensor_scalar, moved[:, cs], key_c[:, cs], spare[:, 0:1], None,
                                  ALU.subtract), (a,), "keys")
                b = L.dve(partial(V.scalar_tensor_tensor, moved[:, cs], amount[:, cs], LATER, moved[:, cs],
                                  ALU.is_lt, ALU.mult), (b,), "keys")
                b = L.dve(partial(V.tensor_scalar, place[:, cs], moved[:, cs], spare[:, 0:1], None,
                                  ALU.add), (b,), "keys")
                for c in range(q * CP, (q + 1) * CP):
                    i = c % TABLES
                    before = (f"scatter{i}", 16 * (c // TABLES)) if c >= TABLES else None
                    L.put(POOL, partial(G.indirect_dma_start, tables[i], bass.IndirectOffsetOnAxis(place[:, c:c + 1], axis=0),
                                        amount[:, c:c + 1], None,
                                        compute_op=ALU.add), (b, L.stores["table_zero"], before), f"scatter{i}", 16)
                yield

        def nodes():
            xn = [sb(s1, f"xn{i}", [P, D]) for i in range(2)]
            stats = sb(s1, "stats1", [P, NT, 16])
            b_col = sb(s1, "b_col", [128, KD])
            x1f = [sb(s1, f"x1f{i}", [128, 500]) for i in range(2)]
            b_got = L.load(b_col[:, :], b_ah, (), "bias_in")
            wi, w_ah, _ = w_ring.take()
            ln_done, turned, xn_done = {}, {}, {}
            BATCH = 5
            for t in range(NT):
                L.load(xs[:, t, :], x[t * P:(t + 1) * P, :], (), f"x_in{t // BATCH}")

            def clear_table(t):
                table, part = tables[t % TABLES], t // TABLES
                n = N * N // (NT // TABLES)
                rows = part * n
                L.store(table[rows:rows + n, :].rearrange("(t p n) o -> p t (n o)", p=P, n=N // 2),
                        zero[0:P, 0:N // 2].unsqueeze(1).broadcast_to([P, n // (P * (N // 2)), N // 2]),
                        (t_zero,), "table_zero", SCAL)
                if part == 0:
                    L.store(table[N * N:, :], zero[0:P, 0:1], (t_zero,), "table_zero", SCAL)

            def statistics(t0):
                for t in range(t0, t0 + BATCH):
                    a = row_stats(xs[:, t, :], stats[:, t, :], ((f"x_in{t // BATCH}", 16 * BATCH),))
                ln_done[t0] = inverse_root(stats[:, t0:t0 + BATCH, :], (a,))

            def norm(t):
                ln_done["x", t] = normalise(xs[:, t, :], xn[t % 2][:, :], stats[:, t, :],
                                            (ln_done[t - t % BATCH], turned.get(t - 2)))

            def turn(t):
                ts = slice(t * P, (t + 1) * P)
                xn_done[t], turned[t] = transposed(xn[t % 2], KD, xnT[0][:, :, ts], xnT[1][:, :, ts],
                                                   all_banks, (ln_done["x", t],))
            w_done = []
            for t in range(NT + 1):
                if t % BATCH == 0 and t < NT:
                    statistics(t)
                if t < NT:
                    norm(t)
                    clear_table(t)
                if t < KD:
                    w_done += load_split(stage, [(W_ah[t * 128:(t + 1) * 128, :], w_ah[0][:, t, 0:D],
                                                  w_ah[1][:, t, 0:D])])
                if t:
                    turn(t - 1)
                yield
            a_row = [[sb(s1, f"a_row{i}{j}", [128, D]) for j in range(2)] for i in range(2)]
            wa_tmp = [sb(s1, f"wa_tmp{i}", [128, D]) for i in range(2)]
            h_out = Ring([sb(s1, f"h_out{i}", [P, GH, HW], BF16) for i in range(3)])
            for i, b in enumerate(h_out.buffers):
                t = L.dve(partial(V.memset, b[:, :, :], 0.0), (), "h_out_set")
                t = L.dve(partial(V.memset, b[:, :, GC:GC + 1], 1.0), (t,), "h_out_set")
                h_out.free[i] = (t,)
            asd_done = {}
            h_mm_last = [None] * LAYERS
            layer_w = {}
            products = [None] * (2 * KD * LAYERS)

            rows_ahead = []

            def attention_vectors(l):
                i, w, w_free = w_ring.take()
                got = [L.load(a_row[l % 2][j][:, :], d[l].rearrange("h c -> (h c)").partition_broadcast(128),
                              (h_mm_last[l - 2],) if l >= 2 else (), f"a_in{l % 2}")
                       for j, d in enumerate((a_src, a_dst))]
                layer_w[l] = (i, w, w_free, got[1], [])

            def weights_part(l, k):
                i, w, w_free, got, done = layer_w[l]
                n = KD * l + k
                while len(rows_ahead) < min(n + 3, KD * LAYERS):
                    l_, k_ = divmod(len(rows_ahead), KD)
                    si, buf, free = stage.take()
                    g = L.load(buf[:, 0:D], Wg[l_][k_ * 128:(k_ + 1) * 128, :], free, f"w_in{si}")
                    rows_ahead.append((si, buf, free, g))
                si, buf, free, g = rows_ahead[n]
                for j in range(2):
                    n = 2 * (KD * l + k) + j
                    for h in range(GH):
                        hs = slice(h * GC, (h + 1) * GC)
                        r = L.dve(partial(V.tensor_tensor_reduce, out=wa_tmp[n % 2][:, hs], in0=buf[:, hs],
                                          in1=a_row[l % 2][j][:, hs], scale=1.0, scalar=0.0, op0=ALU.mult,
                                          op1=ALU.add, accum_out=buf[:, D + 4 * j + h:D + 4 * j + h + 1]),
                                  (g, got, *free, products[n - 2] if n >= 2 else None),
                                  "wa_sum" if h == GH - 1 else None)
                    products[n] = r
                d = split(buf[:, :], w[0][:, k, :], w[1][:, k, :], (g, r), w_free)
                stage.give(si, d)
                done.append(d)

            x1_done = []
            for m in range(KD):
                if m == 0:
                    attention_vectors(0)
                weights_part(0, m)
                ms = slice(m * 128, (m + 1) * 128)
                for c, (c0, c1) in enumerate(COLS):
                    i, b, free = all_banks.take()
                    for k in range(KD):
                        mm = product(b[:, 0:c1 - c0], [w[:, k, ms] for w in w_ah], [v[:, k, c0:c1] for v in xnT],
                                     k == 0, k == KD - 1, (*free, w_done[k], xn_done[NT - 1]),
                                     "x1_mm" if k == KD - 1 else None)
                    n = 3 * m + c
                    f = x1f[n % 2][:, 0:c1 - c0]
                    a = L.act(partial(A.activation, f, b[:, 0:(c1 - c0)], ACT.Relu, bias=b_col[:, m:m + 1]),
                              (mm, b_got, x1_done[n - 2] if n >= 2 else None), "x1_relu")
                    all_banks.give(i, a)
                    x1_done.append(split(f, x1T[0][:, m, c0:c1], x1T[1][:, m, c0:c1], (a,)))
                yield
            w_ring.give(wi, mm)

            for l in range(LAYERS):
                wi, w, _, _, w_done = layer_w.pop(l)
                for t in range(NT):
                    if t == 0 and l + 1 < LAYERS:
                        attention_vectors(l + 1)
                    if 0 <= t - 2 < KD and l + 1 < LAYERS:
                        weights_part(l + 1, t - 2)
                    ts = slice(t * P, (t + 1) * P)
                    oi, o, o_free = h_out.take()
                    los = []
                    for half in range(2):
                        c0, width = half * (D // 2), D // 2 + 8 * half
                        bi, b, free = all_banks.take()
                        for k in range(KD):
                            mm = product(b[0:P, 0:width], [v[:, k, ts] for v in x1T],
                                         [v[:, k, c0:c0 + width] for v in w], k == 0, k == KD - 1,
                                         (*free, w_done[k], x1_done[-1]), "h_mm" if k == KD - 1 else None)
                        v = b[0:P, 0:D // 2].rearrange("p (h c) -> p h c", h=2)
                        hi, lo = (o[:, 2 * half:2 * half + 2, s:s + GC] for s in (0, HW // 2))
                        d = split(v, hi, lo, (mm, *o_free))
                        los.append(d)
                        if half:
                            d2 = L.dve(partial(V.tensor_copy, asd[:, t, 8 * l:8 * l + 8], b[0:P, D // 2:D // 2 + 8]),
                                       (mm,), "asd_copy")
                            asd_done[l, t] = d2
                            d = d2
                        all_banks.give(bi, d)
                    s = L.store(h_rows[l, ts, :, :], o[:, :, :], (los[0], los[1]), f"h_out{oi}")
                    h_out.give(oi, s)
                    yield
                h_mm_last[l] = mm
                w_ring.give(wi, mm)
            as_row_sb = count[0:8 * LAYERS, :, :].rearrange("p t n -> p (t n)").bitcast(F32)[:, 0:N]
            last = None
            for t in range(NT):
                bi, b, free = all_banks.take()
                tt = L.pe(partial(T.transpose, b[0:8 * LAYERS, 0:P], asd[:, t, :], identP),
                          (*free, asd_done[LAYERS - 1, t]), "turned")
                last = L.dve(partial(V.tensor_copy, as_row_sb[:, t * P:(t + 1) * P],
                                     b[0:8 * LAYERS, 0:P]),
                             (tt, ln_done["x", NT - 1]), "asd_row")
                all_banks.give(bi, last)
            L.store(as_rows, as_row_sb, (last,), "as_rows_out")
            for l in range(LAYERS):
                L.dve(partial(V.tensor_scalar, as_low[:, :, 4 * l:4 * l + 4], asd[:, :, 8 * l:8 * l + 4],
                              SLOPE, None, ALU.mult), (asd_done[LAYERS - 1, NT - 1],),
                      "as_low")
            yield

        of_nodes = nodes()
        of_edges = edges()
        next(of_edges)
        for _ in range(NT + 1):
            next(of_nodes)
        run((of_nodes, NODE_RATE), (of_edges, 1))
        s1.close()
        t_as_rows = L.stores["as_rows_out"]
        end1 = fence()
        nodes_end = fence([f"scatter{i}" for i in range(TABLES)])

        def projections(banks, end):
            st = Ring([area.take([128, D]) for i in range(3)], end)
            pf = area.take([128, 2 * FEATS])
            z = L.dve(partial(V.memset, pf[:, :], 0.0), end, "proj_zero")
            L.load(pf[0:HD, 0:FEATS], projT, (z,), "proj_in")
            g1 = L.load(pf[HD:128, FEATS:2 * FEATS], projT, (z,), "proj_in")
            p_done = split(pf[:, :], feats[0][:, :], feats[1][:, :], (g1,))
            wv = [area.take([128, KD, D], BF16) for p in range(2)]
            wq = Ring([[area.take([128, KD, 128], BF16) for p in range(2)] for i in range(2)], end)
            sq = Ring([area.take([128, 500]) for i in range(3)], end)
            v_out = Ring([area.take([P, PAIRS, 2, HD + 1]) for i in range(2)])
            qk_out = Ring([area.take([128, 2, N], BF16) for i in range(2)], end)
            kmax = area.take([P, PAIRS * NT])
            top = area.take([128, 4])
            for i, b in enumerate(v_out.buffers):
                v_out.free[i] = (L.dve(partial(V.memset, b[:, :, :, HD:HD + 1], 1.0), end, "v_ones"),)
            order = [(which, pair) for pair in range(PAIRS) for which in (1, 0)]
            loaded, parted = {}, {}

            def weights_in(n):
                if n < len(order):
                    which, pair = order[n]
                    c = which * D + pair * 128
                    si, buf, free = st.take()
                    bv = buf[:, :].rearrange("p (k c) -> p k c", k=KD)
                    g = L.load(bv, wT_qkv[:, c:c + 128].rearrange("(k p) c -> p k c", p=128), free, f"w_in{si}")
                    loaded[n] = si, bv, g

            def weights_split(n):
                if n < len(order):
                    si, bv, g = loaded.pop(n)
                    wi, w, w_free = wq.take()
                    wd = split(bv, w[0][:, :, :], w[1][:, :, :], (g,), w_free)
                    st.give(si, wd)
                    parted[n] = wi, w, wd

            norms = []

            def squared_norms():
                which, pair, c0, c1, qi, sqv, squared = norms.pop(0)
                bi, b, free = banks.take()
                nt = (c1 - c0) // P
                for j in range(nt):
                    nm = L.pe(partial(T.matmul, b[0:P, 2 * j:2 * j + 2], sqv[:, j * P:(j + 1) * P], halves[:, :],
                                      start=True, stop=True),
                              (*free, squared, t_halves), "norm_mm" if j == nt - 1 else None)
                sq.give(qi, nm)
                t0 = c0 // P
                dd = L.dve(partial(V.tensor_scalar, diag[:, which, t0:t0 + nt, 2 * pair:2 * pair + 2],
                                   b[0:P, 0:2 * nt].rearrange("p (t h) -> p t h", h=2), 0.5 * NORM * NORM, None,
                                   ALU.mult), (nm,), "diag")
                banks.give(bi, dd)

            def heads_T(n, dst, dst_free):
                which, pair = order[n]
                wi, w, wd = parted.pop(n)
                weights_in(n + 2)
                for (c0, c1) in COLS:
                    bi, b, free = banks.take()
                    for k in range(KD):
                        mm = product(b[:, 0:c1 - c0], [u[:, k, :] for u in w], [v[:, k, c0:c1] for v in xnT],
                                     k == 0, k == KD - 1, (*free, wd), "qk_mm" if k == KD - 1 else None)
                    bb = b[:, 0:c1 - c0]
                    qi, sq_buf, sq_free = sq.take()
                    sqv = sq_buf[:, 0:c1 - c0]
                    a0 = L.act(partial(A.activation, sqv, bb, ACT.Square), (mm, *sq_free), "qk_square")
                    a1 = L.act(partial(A.activation, dst[:, 0, c0:c1], bb, ACT.Copy, scale=NORM), dst_free, "qk_hi")
                    d = L.dve(partial(V.scalar_tensor_tensor, dst[:, 1, c0:c1], bb, NORM, dst[:, 0, c0:c1],
                                      ALU.mult, ALU.subtract), (a1,), "qk_lo")
                    banks.give(bi, d)
                    norms.append((which, pair, c0, c1, qi, sqv, a0))
                    if len(norms) > 1:
                        squared_norms()
                    yield
                    if c0 == 0:
                        weights_split(n + 1)
                wq.give(wi, mm)
                ready[which, pair] = d

            vw = []
            for k in range(KD):
                vw += load_split(st, [(wT_qkv[k * 128:(k + 1) * 128, 2 * D:3 * D], wv[0][:, k, :], wv[1][:, k, :])])
            yield
            for t in range(NT):
                ts = slice(t * P, (t + 1) * P)
                oi, o, o_free = v_out.take()
                for half in range(2):
                    cs = slice(half * (D // 2), (half + 1) * (D // 2))
                    bi, b, free = banks.take()
                    for k in range(KD):
                        mm = product(b[0:P, 0:D // 2], [v[:, k, ts] for v in xnT], [w[:, k, cs] for w in wv],
                                     k == 0, k == KD - 1, (*free, vw[k]), "v_mm" if k == KD - 1 else None)
                    ps = slice(half * PAIRS // 2, (half + 1) * PAIRS // 2)
                    d = L.act(partial(A.activation, o[:, ps, :, 0:HD],
                                      b[0:P, 0:D // 2].rearrange("p (a h c) -> p a h c", h=2, c=HD), ACT.Copy),
                              (mm, *o_free), "v_copy")
                    banks.give(bi, d)
                    yield
                if t >= NT - 2:
                    weights_in(t - NT + 2)
                s = L.store(v_rows[:, ts, :].rearrange("a p c -> p a c"),
                            o[:, :, :, :].rearrange("p a h c -> p a (h c)"), (d,), f"v_out{oi}")
                v_out.give(oi, s)

            ready = {}
            weights_split(0)
            for n, (which, pair) in enumerate(order):
                    oi, o, o_free = qk_out.take()
                    yield from heads_T(n, o, o_free)
                    done = ready[which, pair]
                    s = L.store(qk_rows[which, pair], o[:, :, :], (done,), f"qk_out{oi}")
                    if which:
                        for t in range(NT):
                            bi, v, mm = dash(o, slice(t * P, (t + 1) * P), banks, (done, p_done))
                            c = pair * NT + t
                            m = L.dve(partial(V.tensor_reduce, kmax[:, c:c + 1], v, AX.XY, ALU.max), (mm,), "k_max")
                            banks.give(bi, m)
                            if t % 2:
                                yield
                        s = (s, mm)
                    else:
                        s = (s,)
                    qk_out.give(oi, *s)
            squared_norms()
            a = L.dve(partial(V.tensor_reduce, top[0:P, 0:1], kmax[:, :], AX.X, ALU.max), (m,), "k_top")
            bi, b, free = banks.take()
            mm = L.pe(partial(T.transpose, b[0:1, 0:P], top[0:P, 0:1], identP), (*free, a), "turned")
            a = L.dve(partial(V.tensor_reduce, top[0:1, 1:2], b[0:1, 0:P], AX.X, ALU.max), (mm,), "k_top")
            mm = L.pe(partial(T.matmul, b[0:P, 0:1], ones[0:1, 0:P], top[0:1, 1:2], start=True, stop=True),
                      (a, t_ones), "turned")
            a = L.dve(partial(V.tensor_copy, top[0:P, 2:3], b[0:P, 0:1]), (mm,), "k_top")
            banks.give(bi, a)
            L.dve(partial(V.tensor_scalar, k_shift[:, :, :], diag[:, 1, :, :], top[0:P, 2:3], -1.0,
                          ALU.add, ALU.mult), (a,), "k_top")
            yield

        def linear_attention(banks, cb, end):
            STEPS, DRAIN = NT // 2, 3
            ef = Ring([area.take([P, 2, FEATS]) for i in range(4)], end)
            qf = Ring([area.take([128, 2 * MT, P]) for i in range(4)], end)
            context = area.take([128, MT, 2, HD + 1])
            kT = Ring([area.take([128, 2, N], BF16) for i in range(2)], end)
            qT = Ring([area.take([128, 2, N], BF16) for i in range(2)], end)
            vs = Ring([area.take([P, NT, 2, HD + 1]) for i in range(2)], end)
            q_max, q_shift = area.take([P, NT, 2]), area.take([P, NT, 2])
            inv = area.take([P, 2, 2])
            att = Ring([area.take([P, NT, 128]) for i in range(2)], end)
            spilled = [L.stores[f"{what}_out{i}"] for what in ("qk", "v") for i in range(2)]
            order = [(pair, kind, b) for pair in range(PAIRS)
                     for kind, n in (("k", STEPS), ("q", STEPS), (None, DRAIN)) for b in range(n)]
            cv = cb[:, 0:MT * 2 * (HD + 1)].rearrange("p (m h d) -> p m h d", m=MT, h=2)
            ov = cb[0:P, 0:4 * (HD + 1)].rearrange("p (u h d) -> p u h d", u=2, h=2)
            loaded, step = {}, {"cb": end}

            def pair_in(pair):
                ki, kb, k_free = kT.take()
                k_got = L.load(kb[:, :, :], qk_rows[1, pair], (*k_free, *spilled), f"k_in{ki}")
                vi, vb, v_free = vs.take()
                v_got = L.load(vb[:, :, :, :].rearrange("p t h c -> p t (h c)"),
                               v_rows[pair].rearrange("(t p) c -> p t c", p=P), (*v_free, *spilled), f"v_in{vi}")
                qi, qb, q_free = qT.take()
                q_got = L.load(qb[:, :, :], qk_rows[0, pair], (*q_free, *spilled), f"q_in{qi}")
                loaded[pair] = {"k": (ki, kb, k_got), "v": (vi, vb, v_got), "q": (qi, qb, q_got)}

            def features(n):
                pair, kind, b = order[n]
                if kind is None:
                    return
                if pair == 0 and kind == "k" and b == 0:
                    pair_in(0)
                if kind == "k" and b == 2 and pair + 1 < PAIRS:
                    pair_in(pair + 1)
                i, buf, got = loaded[pair][kind]
                step["dash", n] = [dash(buf, slice(t * P, (t + 1) * P), banks, (got,)) for t in (2 * b, 2 * b + 1)]
                if b == STEPS - 1:
                    (kT if kind == "k" else qT).give(i, step["dash", n][1][2])

            def exponentials(n):
                pair, kind, b = order[n]
                if kind is None:
                    return
                hs = slice(2 * pair, 2 * pair + 2)
                tiles = step.pop(("dash", n))
                done = []
                if kind == "q":
                    for u, (bi, v, mm) in enumerate(tiles):
                        m = L.dve(partial(V.tensor_reduce, q_max[:, 2 * b + u, :], v, AX.X, ALU.max), (mm,), "q_max")
                    ts = slice(2 * b, 2 * b + 2)
                    m = L.dve(partial(V.scalar_tensor_tensor, q_shift[:, ts, :], q_max[:, ts, :], -1.0,
                                      diag[:, 0, ts, hs], ALU.mult, ALU.subtract), (m, step.get("q_exp")), "q_max")
                for u, (bi, v, mm) in enumerate(tiles):
                    t = 2 * b + u
                    ei, e, e_free = ef.take()
                    for h in range(2):
                        bias = k_shift[:, t, 2 * pair + h:2 * pair + h + 1] if kind == "k" else q_shift[:, t, h:h + 1]
                        a = L.act(partial(A.activation, e[:, h, :], v[:, h, :], ACT.Exp, bias=bias),
                                  (mm if kind == "k" else m, *e_free), kind + "_exp")
                    banks.give(bi, a)
                    if kind == "k":
                        a = L.dve(partial(V.tensor_scalar, e[:, :, :], e[:, :, :], EPS, None, ALU.add), (a,),
                                  "k_feat")
                    else:
                        step["q_exp"] = a
                    done.append((ei, e, a))
                step["exp", n] = done

            def sum_or_turn(n):
                pair, kind, b = order[n]
                if kind is None:
                    return
                tiles = step.pop(("exp", n))
                turned = []
                for u, (ei, e, ready) in enumerate(tiles):
                    t = 2 * b + u
                    if kind == "k":
                        vi, vb, v_got = loaded[pair]["v"]
                        for m in range(MT):
                            for h in range(2):
                                mm = L.pe(partial(T.matmul, cv[:, m, h, :], e[:, h, m * 128:(m + 1) * 128],
                                                  vb[:, t, h, :], start=t == 0 and m == 0 and h == 0,
                                                  stop=t == NT - 1, skip_group_check=True),
                                          (ready, v_got, *step["cb"]), "ctx_mm" if m == MT - 1 and h else None)
                        step["ctx"] = mm
                    else:
                        bi, bk, free = banks.take()
                        for k in range(2 * MT):
                            h, m = divmod(k, MT)
                            mm = L.pe(partial(T.transpose, bk[:, k * P:(k + 1) * P], e[:, h, m * 128:(m + 1) * 128],
                                              identP), (*free, ready), "turned" if k == 2 * MT - 1 else None)
                        turned.append((bi, bk, mm))
                    ef.give(ei, mm)
                if kind == "k" and b == STEPS - 1:
                    vs.give(vi, mm)
                step["turn", n] = turned

            def turned_features(n):
                pair, kind, b = order[n]
                if kind is None:
                    return
                tiles = step.pop(("turn", n))
                if kind == "k" and b == STEPS - 1:
                    a = L.act(partial(A.activation, context[:, :, :, :], cv, ACT.Copy, scale=RATIO * RATIO),
                              (step["ctx"], step.get("out"), *end), "ctx_copy")
                    step["cb"], step["context"] = (a,), a
                step["qf", n] = done = []
                for bi, bk, mm in tiles:
                    qi, q, q_free = qf.take()
                    a = L.dve(partial(V.tensor_scalar, q[:, :, :],
                                      bk[:, 0:2 * MT * P].rearrange("p (n c) -> p n c", n=2 * MT), EPS, None,
                                      ALU.add), (mm, *q_free), "q_feat")
                    banks.give(bi, a)
                    done.append((qi, q, a))

            def outputs(n):
                pair, kind, b = order[n]
                if kind is None:
                    return
                for u, (qi, q, ready) in enumerate(step.pop(("qf", n))):
                    for h in range(2):
                        for m in range(MT):
                            mm = L.pe(partial(T.matmul, ov[:, u, h, :], q[:, h * MT + m, :], context[:, m, h, :],
                                              start=u == 0 and h == 0 and m == 0, stop=m == MT - 1,
                                              skip_group_check=True),
                                      (ready, step["context"], *step["cb"]), "out_mm" if h and m == MT - 1 else None)
                    qf.give(qi, mm)
                    step["out"] = mm

            def divided(n):
                pair, kind, b = order[n]
                if kind != "q":
                    return
                if b == 0:
                    step["att"] = att.take()
                ai, att_buf, att_free = step["att"]
                r = L.dve(partial(V.reciprocal, inv[:, :, :], ov[:, :, :, HD:HD + 1].rearrange(
                    "p u h o -> p u (h o)")), (step["out"], step.get("att_done")), "att_inv")
                for u in range(2):
                    for h in range(2):
                        a = L.act(partial(A.activation, att_buf[:, 2 * b + u, h * HD:(h + 1) * HD],
                                          ov[:, u, h, 0:HD], ACT.Copy, scale=inv[:, u, h:h + 1]),
                                  (r, *att_free), "att_scaled")
                step["cb"], step["att_done"] = (a,), a
                if b == STEPS - 1:
                    o = L.store(attn_rows[:, pair * 128:(pair + 1) * 128].rearrange("(t p) c -> p t c", p=P),
                                att_buf[:, :, :], (a,), f"att_out{ai}")
                    att.give(ai, o)

            yield from in_step([(5, divided), (1, exponentials), (3, turned_features),
                                (2, sum_or_turn), (0, features), (4, outputs)], len(order))

        def mix_projection(banks, end):
            st = Ring([area.take([128, D]) for i in range(3)], end)
            wp = [area.take([128, KD, D], BF16) for p in range(2)]
            bp = area.take([P, D])
            ar = Ring([area.take([P, D]) for i in range(2)], end)
            aT = Ring([[area.take([128, KD, P], BF16) for p in range(2)] for i in range(2)], end)
            xr = Ring([area.take([P, D]) for i in range(2)], end)
            att_out = (L.stores["att_out0"], L.stores["att_out1"])
            b_got = L.load(bp[:, :], b_proj.partition_broadcast(P), end, "bias_in")
            pw = yield from load_split_spread(
                st, [(wT_proj[k * 128:(k + 1) * 128, :], wp[0][:, k, :], wp[1][:, k, :]) for k in range(KD)], end)
            yield
            step = {}

            def rows_in(t):
                ri, r, free = ar.take()
                step["rows", t] = ri, r, L.load(r[:, :], attn_rows[t * P:(t + 1) * P, :], (*free, *att_out),
                                                f"rows_in{ri}")

            def turn_rows(t):
                ri, r, got = step.pop(("rows", t))
                ti, a, t_free = aT.take()
                d, tt = transposed(r, KD, a[0], a[1], banks, (got, *t_free))
                ar.give(ri, tt)
                xi, xb, x_free = xr.take()
                xg = L.load(xb[:, :], x[t * P:(t + 1) * P, :], x_free, f"x_again{xi}")
                step[t] = (ti, a, d, xi, xb, xg)

            def project(t):
                ti, a, d, xi, xb, xg = step.pop(t)
                xg = L.dve(partial(V.tensor_tensor, xb[:, :], xb[:, :], bp[:, :], ALU.add), (xg, b_got),
                           "x_bias")
                for half in range(2):
                    cs = slice(half * (D // 2), (half + 1) * (D // 2))
                    bi, b, free = banks.take()
                    for k in range(KD):
                        mm = product(b[0:P, 0:D // 2], [v[:, k, :] for v in a], [w[:, k, cs] for w in wp],
                                     k == 0, k == KD - 1, (*free, pw[k], d), "proj_mm" if k == KD - 1 else None)
                    s = L.dve(partial(V.tensor_tensor, xb[:, cs], b[0:P, 0:D // 2], xb[:, cs],
                                      ALU.add), (mm, xg), "mixed")
                    banks.give(bi, s)
                    yield
                aT.give(ti, mm)
                o = L.store(mixed_rows[t * P:(t + 1) * P, :], xb[:, :], (s,), f"mixed_out{xi}")
                xr.give(xi, o)

            yield from in_step([(0, rows_in), (1, turn_rows), (2, project)], NT)

        def counts(banks, sp, end):
            absent = sb(sp, "absent", [P, NT, N], BF16)
            tab = Ring([[sb(sp, f"tab{i}{j}", [P, N]) for j in range(TABLES)] for i in range(2)])
            for i in range(2):
                tab.give(i, *end)
            scattered = tuple((f"scatter{i}", L.count[f"scatter{i}"]) for i in range(TABLES))
            for _ in range(COUNT_DELAY):
                yield
            for t in range(NT):
                ti, tb, free = tab.take()
                got = [L.load(tb[j][:, :], tables[j][t * P * N:(t + 1) * P * N, :].rearrange(
                    "(p n) o -> p (n o)", p=P), (*free, *scattered), f"tab_in{ti}") for j in range(TABLES)]
                a = L.pool(partial(G.tensor_tensor, tb[0][:, :], tb[0][:, :], tb[1][:, :], ALU.add),
                           got[1:], "counted")
                a = L.pool(partial(G.tensor_tensor, tb[0][:, t * P:(t + 1) * P], tb[0][:, t * P:(t + 1) * P],
                                   identP, ALU.add), (a, t_ident), "counted")
                c = L.act(partial(A.activation, count[:, t, :], tb[0][:, :], ACT.Copy), (a,), "count_copy")
                for u0 in range(0, NT, 4):
                    nu = min(4, NT - u0)
                    bi, b, free = banks.take()
                    for j in range(nu):
                        mm = L.pe(partial(T.transpose, b[0:P, j * P:(j + 1) * P],
                                          tb[0][:, (u0 + j) * P:((u0 + j) + 1) * P], identP),
                                  (*free, a), "turned" if j == nu - 1 else None)
                    d = L.dve(partial(V.tensor_scalar, absent[:, u0:u0 + nu, t * P:(t + 1) * P],
                                      b[0:P, 0:nu * P].rearrange("p (u s) -> p u s", u=nu), 0.0, -BIG, ALU.is_equal, ALU.mult),
                              (mm,), "absent")
                    banks.give(bi, d)
                tab.give(ti, mm, c)
                yield
            ab = Ring([sb(sp, f"ab{i}", [P, N]) for i in range(2)])
            junk = [sb(sp, f"junk{i}", [P, N]) for i in range(2)]
            for i in range(2):
                ab.give(i, *end)
            mz = sb(sp, "mz", [P, NT, GH])
            ms = sb(sp, "ms", [P, NT, GH])
            srow = sb(sp, "srow", [2 * GH, N])

            def source_terms(lh):
                l, h = divmod(lh, GH)
                ai, a_buf, free = ab.take()
                return ai, a_buf, L.load(a_buf[:, :], as_rows[8 * l + h, :].partition_broadcast(P),
                                         (*free, t_as_rows), f"spread_in{ai}")

            def shifts(l, m):
                ls = slice(GH * l, GH * (l + 1))
                ad = asd[:, :, 8 * l + 4:8 * l + 8]
                a = L.dve(partial(V.tensor_tensor, mz[:, :, :], m_col[:, ls, :].rearrange("p h t -> p t h"), ad,
                                  ALU.add), (m, *end), "shifts")
                a = L.dve(partial(V.scalar_tensor_tensor, ms[:, :, :], mz[:, :, :], SLOPE, mz[:, :, :],
                                  ALU.mult, ALU.max), (a,), "shifts")
                L.dve(partial(V.tensor_tensor, shift[:, l, :, 0:GH], ad, ms[:, :, :], ALU.subtract), (a,), "shifts")
                a = L.dve(partial(V.scalar_tensor_tensor, shift[:, l, :, GH:2 * GH], ad, SLOPE, ms[:, :, :],
                                  ALU.mult, ALU.subtract), (a,), "shifts")
                for c0, c1 in COLS:
                    bi, b, free = banks.take()
                    for t in range(c0 // P, c1 // P):
                        tt = L.pe(partial(T.transpose, b[0:2 * GH, t * P - c0:(t + 1) * P - c0], shift[:, l, t, :],
                                          identP), (*free, a), "turned" if (t + 1) * P == c1 else None)
                    last = L.dve(partial(V.tensor_copy, srow[:, c0:c1], b[0:2 * GH, 0:c1 - c0]),
                                 (tt, L.stores.get(f"shift_rows_out{l - 1}"), *end), "shift_row")
                    banks.give(bi, last)
                L.store(shift_rows[l], srow[:, :], (last,), f"shift_rows_out{l}")

            n = 0
            following = source_terms(0)
            for lh in range(LH):
                ai, a_buf, got = following
                if lh + 1 < LH:
                    following = source_terms(lh + 1)
                for t in range(NT):
                    m = L.dve(partial(V.tensor_tensor_reduce, out=junk[n % 2][:, :], in0=a_buf[:, :],
                                      in1=absent[:, t, :], scale=1.0, scalar=-BIG, op0=ALU.add, op1=ALU.max,
                                      accum_out=m_col[:, lh, t:t + 1]),
                              (got, d, ("edge_max", n - 1) if n >= 2 else None), "edge_max")
                    n += 1
                    yield
                ab.give(ai, m)
                if lh % GH == GH - 1:
                    shifts(lh // GH, m)
                    yield

        sc = ExitStack()
        area.clear()
        run((projections(Ring(bank[0:6]), nodes_end), 1), (counts(Ring(bank[6:8]), sc, end1), COUNT_RATE))
        sc.close()
        s0.close()
        end2 = fence()

        HALF = NT // 2
        HN = HALF * P
        layers_queued = [0]

        def graph_attention(acc, sp, end):
            rb = Ring([[sb(sp, f"shift_b{i}{j}", [P, N]) for j in range(2)] for i in range(2)], end)
            hb = Ring([sb(sp, f"hb{i}", [P, NT, HW], BF16) for i in range(2)], end)
            eb = Ring([[sb(sp, f"eb{i}{j}", [P, 2, HN]) for j in range(2)] for i in range(4)], end)
            pb = Ring([[sb(sp, f"pp{i}_{p}", [P, 2, HN], BF16) for p in ("hi", "lo")] for i in range(3)], end)
            bgr = sb(sp, "bgr", [P, LAYERS * D])
            rinv = sb(sp, "rinv", [P, 2, HALF])
            node = Ring([sb(sp, f"node{i}", [P, HALF, GC]) for i in range(2)], end)
            heads, step = {}, {}
            acc_free = [end] * len(acc)
            SPLITS = NT // 2
            ITEMS = 2 * SPLITS

            def head_in(lh):
                l, h = divmod(lh, GH)
                ri, r, free = rb.take()
                got = [L.load(r[j][:, :], shift_rows[l, j * GH + h, :].partition_broadcast(P),
                              (*free, L.stores[f"shift_rows_out{l}"]), f"shift_in{ri}") for j in range(2)]
                hi, hv, h_free = hb.take()
                got_h = L.load(hv[:, :, :], h_rows[l, :, h, :].rearrange("(t p) c -> p t c", p=P),
                               (*h_free, *[L.stores[f"h_out{i}"] for i in range(3)]), f"h_in{hi}")
                heads[lh] = (ri, r, got, hi, hv, got_h)

            def edge_exp(i):
                lh, j = divmod(i, ITEMS)
                half, pair = divmod(j, SPLITS)
                l, h = divmod(lh, GH)
                ns = slice(half * HN, (half + 1) * HN)
                if i == 0:
                    head_in(0)
                if i == 1:
                    for k in range(LAYERS):
                        step["bias"] = L.load(bgr[:, k * D:(k + 1) * D], bg[k].partition_broadcast(P), end, "bg_in")
                if j == 4 and lh + 1 < LH:
                    head_in(lh + 1)
                ri, r, got, *_ = heads[lh]
                ei, eb2, free = eb.take()
                for u in range(2):
                    t = 2 * pair + u
                    L.act(partial(A.activation, eb2[0][:, u, :], r[0][:, ns], ACT.Exp,
                                  bias=asd[:, t, 8 * l + h:8 * l + h + 1]), (got[1], *free))
                    a1 = L.act(partial(A.activation, eb2[1][:, u, :], r[1][:, ns], ACT.Exp,
                                       bias=as_low[:, t, lh:lh + 1]), (), "edge_exp" if u else None)
                if j == ITEMS - 1:
                    rb.give(ri, a1)
                step["e", i] = (ei, eb2, a1)

            def weigh(i):
                j = i % ITEMS
                half, pair = divmod(j, SPLITS)
                ns = slice(half * HN, (half + 1) * HN)
                ei, eb2, a1 = step.pop(("e", i))
                d = L.dve(partial(V.tensor_tensor, eb2[0][:, :, :], eb2[0][:, :, :], eb2[1][:, :, :], ALU.max),
                          (a1,), "edge_w")
                d = L.dve(partial(V.scalar_tensor_tensor, eb2[0][:, :, :], eb2[0][:, :, :], 1.0,
                                  count[:, 2 * pair:2 * pair + 2, ns], ALU.min, ALU.mult), (d,), "edge_w")
                pi, pp, p_free = pb.take()
                a = L.dve(partial(V.tensor_copy, pp[0][:, :, :], eb2[0][:, :, :]), (d, *p_free), "edge_w")
                s = L.pool(partial(G.tensor_tensor, pp[1][:, :, :], eb2[0][:, :, :], pp[0][:, :, :],
                                   ALU.subtract), (a,), "edge_w_lo")
                eb.give(ei, s)
                step["p", i] = (pi, pp, s)

            def gather(i):
                lh, j = divmod(i, ITEMS)
                half, pair = divmod(j, SPLITS)
                ri, r, got, hi_, hv, got_h = heads[lh]
                pi, pp, ready = step.pop(("p", i))
                for u in range(2):
                    t = 2 * pair + u
                    first, last = pair == 0 and u == 0, pair == SPLITS - 1 and u == 1
                    for v in range(HALF):
                        c0 = (v % 2) * (GC + 2)
                        o = acc[v // 2][0:P, c0:c0 + GC + 1]
                        vs = slice(v * P, (v + 1) * P)
                        after = (ready, got_h, *acc_free[v // 2]) if first else (ready,)
                        L.pe(partial(T.matmul, o, pp[0][:, u, vs], hv[:, t, 0:GC + 1], start=first and v % 2 == 0,
                                     stop=False, skip_group_check=True), after)
                        L.pe(partial(T.matmul, o[:, 0:GC], pp[0][:, u, vs], hv[:, t, HW // 2:HW // 2 + GC],
                                     start=False, stop=False, skip_group_check=True))
                        ends = v % 2 == 1 or v == HALF - 1
                        mm = L.pe(partial(T.matmul, o, pp[1][:, u, vs], hv[:, t, 0:GC + 1], start=False,
                                          stop=last, skip_group_check=True),
                                  (), "gather_mm" if (last and ends) or (u == 1 and v == HALF - 1) else None)
                        if last and ends:
                            step["acc", v // 2] = mm
                pb.give(pi, mm)
                if j == ITEMS - 1:
                    hb.give(hi_, mm)

            def finish(i):
                lh, j = divmod(i, ITEMS)
                half, pair = divmod(j, SPLITS)
                if pair < SPLITS - 1:
                    return
                ni, nb, free = node.take()
                for k, b in enumerate(acc):
                    n = min(2, HALF - 2 * k)
                    v = b[0:P, 0:n * (GC + 2)].rearrange("p (u c) -> p u c", u=n)
                    q = rinv[:, half, 2 * k:2 * k + n]
                    a = L.dve(partial(V.tensor_scalar, q, v[:, :, GC:GC + 1].rearrange("p u o -> p (u o)"),
                                      SOFTMAX_EPS, None, ALU.add), (step.pop(("acc", k)), step.get(("scaled", half))), "node_inv")
                    a = L.dve(partial(V.reciprocal, q, q), (a,), "node_inv")
                    for u in range(n):
                        a = L.act(partial(A.activation, nb[:, 2 * k + u, :], v[:, u, 0:GC], ACT.Copy,
                                          scale=rinv[:, half, 2 * k + u:2 * k + u + 1]),
                                  (a, *free) if u == 0 else (), "node_scaled")
                    acc_free[k] = (a,)
                step["scaled", half] = a
                a = L.pool(partial(G.tensor_tensor, nb[:, :, :], nb[:, :, :],
                                   bgr[:, lh * GC:(lh + 1) * GC].unsqueeze(1).broadcast_to([P, HALF, GC]), ALU.add),
                           (a, step["bias"]), "node_bias")
                o = L.store(node_rows[half * HN:(half + 1) * HN, lh * GC:(lh + 1) * GC].rearrange(
                    "(t p) c -> p t c", p=P), nb[:, :, :], (a,), f"node_out{ni}")
                node.give(ni, o)
                if half and lh % GH == GH - 1:
                    layers_queued[0] += 1

            yield from in_step([(0, edge_exp), (1, weigh), (4, finish), (3, gather)], LH * ITEMS)

        def weights_out(l, stage, dst, after, signal="w_in"):
            return (yield from load_split_spread(
                stage, [(W_out[r0:r0 + 128, :], dst[0][:, k, :], dst[1][:, k, :])
                        for k, r0 in enumerate(range(l * D, (l + 1) * D, 128))], after, signal))

        def node_projection(end, wacc):
            w = [area.take([128, KD, D], BF16) for p in range(2)]
            st = Ring([area.take([128, D]) for i in range(2)], end)
            nr = Ring([area.take([P, D]) for i in range(2)], end)
            nT = Ring([[area.take([128, KD, P], BF16) for p in range(2)] for i in range(2)], end)
            state = {"w_free": end, "summed": end}

            def layer(l, banks, between=(), then=(), given=None):
                wl, wd = given or (w, (yield from weights_out(l, st, w, state["w_free"])))
                while layers_queued[0] <= l:
                    yield
                stored = (L.stores["node_out0"], L.stores["node_out1"])
                summed = state["summed"]
                step = {}

                def rows_in(t):
                    ri, r, free = nr.take()
                    step["rows", t] = ri, r, L.load(r[:, :], node_rows[t * P:(t + 1) * P, l * D:(l + 1) * D],
                                                    (*free, *stored), f"rows_in{ri}")

                def turn_rows(t):
                    ri, r, got = step.pop(("rows", t))
                    ti, a, t_free = nT.take()
                    d, tt = transposed(r, KD, a[0], a[1], banks, (got, *t_free), relu=True)
                    nr.give(ri, tt)
                    step[t] = (ti, a, d)

                def times(t):
                    ti, a, d = step.pop(t)
                    for half in range(2):
                        cs = slice(half * (D // 2), (half + 1) * (D // 2))
                        bi, b, free = banks.take()
                        for k in range(KD):
                            mm = product(b[0:P, 0:D // 2], [v[:, k, :] for v in a], [v[:, k, cs] for v in wl],
                                         k == 0, k == KD - 1, (*free, wd[k], d), "wout_mm" if k == KD - 1 else None)
                        if l == 0:
                            s = L.dve(partial(V.tensor_copy, wacc[:, t, cs], b[0:P, 0:D // 2]), (mm, *end), "wacc")
                        else:
                            s = L.dve(partial(V.tensor_tensor, wacc[:, t, cs], b[0:P, 0:D // 2], wacc[:, t, cs],
                                              ALU.add), (mm, *summed), "wacc")
                        banks.give(bi, s)
                        step["sum"] = s
                        yield
                    nT.give(ti, mm)

                yield from in_step([(0, rows_in), (1, turn_rows), *between, (2, times), *then], NT)
                state["w_free"], state["summed"] = (("wout_mm", L.count["wout_mm"]),), (step["sum"],)

            return layer

        def mix_then_nodes(end):
            yield from linear_attention(Ring(bank[3:7], end), bank[7], end)
            L.store(slot_rows[0:SLOTS, :].rearrange("(t p) c -> p t c", p=SP),
                    zero[0:SP, 0:D].unsqueeze(1).broadcast_to([SP, ST, D]), (), "slot_zero")
            area.clear()
            end = fence()
            yield from mix_projection(Ring(bank[3:8], end), end)
            area.clear(NT * D)
            end = fence()
            layer = node_projection(end, wacc)
            banks = Ring(bank[3:8], end)
            for l in range(LAYERS - 1):
                yield from layer(l, banks)
            last_layer.append(layer)

        area.clear()
        wacc = area.take([P, NT, D])
        area.clear()
        last_layer = []

        x2 = wacc

        def experts(sp, end):
            xf = sb(sp, "xf", [P, NT, D])
            pm = sb(sp, "pm", [P, 8, NT])
            slot = sb(sp, "slot", [P, 2, NT], U32)
            b1c = sb(sp, "b1c", [128, EXPERTS, KF])
            g_b1 = L.load(b1c[:, :, :], b1_cols, end, "b1_in")
            w1s = Ring([sb(sp, f"w1_{i}", [128, KD, F]) for i in range(3)], end)
            w2s = Ring([sb(sp, f"w2_{i}", [128, KF, D]) for i in range(3)], end)
            b2r = Ring([sb(sp, f"b2r{i}", [128, D]) for i in range(3)], end)
            hT = Ring([sb(sp, f"hT{i}", [128, KF, CAP]) for i in range(2)], end)
            orow = Ring([sb(sp, f"orow{i}", [128, D]) for i in range(2)], end)
            rt = ExitStack()
            bo = sb(rt, "bo", [P, D])
            mi = Ring([sb(rt, f"mi{i}", [P, D]) for i in range(2)], end)
            stats = sb(rt, "stats3", [P, NT, 16])
            sw = sb(rt, "sw", [128, KD, EXPERTS])
            sbias = sb(rt, "sbias", [P, EXPERTS])
            fT = Ring([sb(rt, f"fT{i}", [128, KD, P]) for i in range(2)], end)
            iota8i, iota8 = sb(rt, "iota8i", [P, EXPERTS], I32), sb(rt, "iota8", [P, EXPERTS])
            idx_i, idx = sb(rt, "idx_i", [P, NT], I32), sb(rt, "idx", [P, NT])
            lg = sb(rt, "lg", [P, NT, EXPERTS])
            ex = sb(rt, "ex", [P, NT, EXPERTS])
            b_got = L.load(bo[:, :], b_out.partition_broadcast(P), end, "bias_in")
            sw_got = L.load(sw[:, :, :], switch_w.rearrange("(k p) e -> p k e", p=128), end, "switch_in")
            g_bias = L.load(sbias[:, :], switch_b.partition_broadcast(P), end, "switch_b_in")
            t = L.pool(partial(G.iota, iota8i[:, :], pattern=[[1, EXPERTS]], base=0, channel_multiplier=0),
                       end, "consts")
            t = L.pool(partial(G.iota, idx_i[:, :], pattern=[[P, NT]], base=SLOTS, channel_multiplier=1),
                       (), "consts")
            i8 = L.dve(partial(V.tensor_copy, iota8[:, :], iota8i[:, :]), (t, *end), "route")
            i8 = L.dve(partial(V.tensor_copy, idx[:, :], idx_i[:, :]), (t,), "route")
            w_last = [ring.buffers[2][:, :, :].rearrange("p k f -> p (k f)").bitcast(BF16).rearrange(
                "p (k c) -> p k c", k=KD) for ring in (w1s, w2s)]
            w_last_done = yield from weights_out(LAYERS - 1, orow, w_last, end, "w1_in")
            yield "loaded"
            end = fence()
            banks = Ring(bank[0:8], end)
            done, ws, hs = {}, {}, {}
            BATCH = 2

            def weights_in(e):
                i1, b1_, f1 = w1s.take()
                g1 = L.load(b1_[:, :, :], w1[e].rearrange("(k p) f -> p k f", p=128), f1, f"w1_in{i1}")
                i2, b2_, f2 = w2s.take()
                g2 = L.load(b2_[:, :, :], w2[e].rearrange("(k p) d -> p k d", p=128), f2, f"w2_in{i2}")
                i3, br, f3 = b2r.take()
                g3 = L.load(br[:, :], b2[e].partition_broadcast(128), f3, f"b2_in{i3}")
                ws[e] = (i1, b1_, g1), (i2, b2_, g2), (i3, br, g3)

            def new_x(t):
                if t >= NT - 2:
                    weights_in(t - NT + 2)
                mi_i, m, m_free = mi.take()
                got = L.load(m[:, :], mixed_rows[t * P:(t + 1) * P, :],
                             (*m_free, L.stores["mixed_out0"], L.stores["mixed_out1"]), f"mixed_in{mi_i}")
                summed = ("wacc", 2 * (NT * (LAYERS - 1) + t + 1))
                a = L.dve(partial(V.tensor_tensor, x2[:, t, :], wacc[:, t, :], bo[:, :], ALU.add),
                          (b_got, summed), "x2")
                a = L.dve(partial(V.scalar_tensor_tensor, x2[:, t, :], x2[:, t, :], 0.0, m[:, :],
                                  ALU.max, ALU.add), (a, got), "x2")
                mi.give(mi_i, a)
                a = row_stats(x2[:, t, :], stats[:, t, :], (a,))
                if t % BATCH == BATCH - 1:
                    tiles = range(t - BATCH + 1, t + 1)
                    a = inverse_root(stats[:, t - BATCH + 1:t + 1, :], (a,))
                    for u in tiles:
                        done["xf", u] = normalise(x2[:, u, :], xf[:, u, :], stats[:, u, :], (a, *end))

            def turn(t):
                ti, f, f_free = fT.take()
                for g in range(2):
                    bi, b, free = banks.take()
                    for k in range(3):
                        kk = 3 * g + k
                        tt = L.pe(partial(T.transpose, b[:, k * P:(k + 1) * P], xf[:, t, kk * 128:(kk + 1) * 128],
                                          identP), (*free, done["xf", t]), "turned" if k == 2 else None)
                    ps = b[:, 0:3 * P].rearrange("p (k n) -> p k n", k=3)
                    if g:
                        d = L.dve(partial(V.tensor_copy, f[:, 3:6, :], ps), (tt, *f_free), "xf_turned")
                    else:
                        d = a = L.act(partial(A.activation, f[:, 0:3, :], ps, ACT.Copy), (tt, *f_free),
                                      "xf_turned_act")
                    banks.give(bi, d)
                done["turned", t] = ti, f, a, d

            def logits(t):
                ti, f, a, d = done["turned", t]
                bi, b, free = banks.take()
                for k in range(KD):
                    mm = L.pe(partial(T.matmul, b[0:P, 0:EXPERTS], f[:, k, :], sw[:, k, :], start=k == 0,
                                      stop=k == KD - 1), (*free, a, d, sw_got), "logit_mm" if k == KD - 1 else None)
                fT.give(ti, mm)
                a = L.dve(partial(V.tensor_tensor, lg[:, t, :], b[0:P, 0:EXPERTS], sbias[:, :], ALU.add),
                          (mm, g_bias, *end), "route")
                banks.give(bi, a)
                done["logits"] = a

            yield from last_layer[0](LAYERS - 1, banks, [(5, turn)], [(5, logits), (3, new_x)],
                                     (w_last, w_last_done))
            for ring in (w1s, w2s):
                ring.free[2] = (("wout_mm", L.count["wout_mm"]),)
            by_expert = [P, NT, EXPERTS]
            a = L.dve(partial(V.tensor_reduce, pm[:, 0, :], lg[:, :, :], AX.X, ALU.max), (done["logits"],), "route")
            shifted = L.dve(partial(V.tensor_tensor, lg[:, :, :], lg[:, :, :],
                                    pm[:, 0, :].unsqueeze(2).broadcast_to(by_expert), ALU.subtract), (a,), "route")
            e = L.act(partial(A.activation, ex[:, :, :], lg[:, :, :], ACT.Exp), (shifted,), "route_exp")
            a = L.dve(partial(V.tensor_scalar, lg[:, :, :], lg[:, :, :], 0.0, float(EXPERTS), ALU.is_lt,
                              ALU.mult), (e,), "route")
            a = L.dve(partial(V.tensor_tensor, lg[:, :, :], lg[:, :, :],
                              iota8[:, :].unsqueeze(1).broadcast_to(by_expert), ALU.add), (a, i8), "route")
            L.dve(partial(V.tensor_reduce, pm[:, 2, :], lg[:, :, :], AX.X, ALU.min), (a,), "route")
            a = L.dve(partial(V.tensor_reduce, pm[:, 7, :], ex[:, :, :], AX.X, ALU.add), (e,), "route")
            done["route"] = L.dve(partial(V.reciprocal, pm[:, 1, :], pm[:, 7, :]), (a,), "route")
            area.clear(NT * D)
            end = fence()
            rr = area.take([2 * NT, P])
            bi, b, free = banks.take()
            tt = L.pe(partial(T.transpose, b[0:2 * NT, 0:P], pm[:, 1:3, :].rearrange("p a t -> p (a t)"), identP),
                      (*free, done["route"]), "turned")
            a = L.dve(partial(V.tensor_copy, rr[:, :], b[0:2 * NT, 0:P]), (tt, *end), "route_row")
            banks.give(bi, a)
            s = L.store(route_rows.rearrange("a (t p) -> (a t) p", p=P), rr[:, :], (a,), "route_rows_out")
            pr, ro = area.take([P, N]), area.take([P, N])
            g0 = L.load(pr[:, :], route_rows[0, :].partition_broadcast(P), (s, *end), "route_in")
            g1 = L.load(ro[:, :], route_rows[1, :].partition_broadcast(P), (s, *end), "route_in")
            earlier = area.take([P, P])
            t = L.pool(partial(G.memset, earlier[:, :], 1.0), end, "consts")
            t_e = L.pool(partial(G.affine_select, out=earlier[:, :], in_=earlier[:, :], compare_op=ALU.is_gt,
                                 fill=0.0, base=0, pattern=[[-1, P]], channel_multiplier=1),
                         (t,), "consts")
            mates = Ring([area.take([P, N]) for i in range(3)], end)
            won = area.take([P, N], BF16)
            cnt = area.take([P, 4, NT])
            c = L.dve(partial(V.memset, cnt[:, :, :], 0.0), end, "ranks")
            for t in range(NT):
                mate_i, mt, m_free = mates.take()
                lo, hi = t * P, (t + 1) * P
                prob, route = pm[:, 1, t:t + 1], pm[:, 2, t:t + 1]
                put, eng, done_sem = (L.dve, V, "ranks") if t % MATE_TURN == MATE_TURN - 1 else (L.pool, G, "mates")
                a = put(partial(eng.tensor_scalar, mt[:, :], ro[:, :], route, None, ALU.is_equal), (g1, *m_free),
                        done_sem)
                parts = [(0, lo, ALU.is_ge, 0), (lo, hi, ALU.is_gt, 1), (hi, N, ALU.is_gt, 2)]
                for p0, p1, op, j in parts:
                    if p1 > p0:
                        c = L.dve(partial(V.scalar_tensor_tensor, won[:, p0:p1], pr[:, p0:p1], prob, mt[:, p0:p1],
                                          op, ALU.mult,
                                          accum_out=cnt[:, j, t:t + 1]), (a, c), "ranks")
                c = L.dve(partial(V.scalar_tensor_tensor, mt[:, lo:hi], pr[:, lo:hi], prob,
                                  mt[:, lo:hi], ALU.is_equal, ALU.mult), (c,), "ranks")
                c = L.dve(partial(V.scalar_tensor_tensor, won[:, lo:hi], mt[:, lo:hi], 1.0, earlier[:, :],
                                  ALU.mult, ALU.mult,
                                  accum_out=cnt[:, 3, t:t + 1]), (c, t_e), "ranks")
                mates.give(mate_i, c)
            c = L.dve(partial(V.tensor_reduce, pm[:, 3, :], cnt[:, :, :].rearrange("p a t -> p t a"), AX.X,
                              ALU.add), (c,), "ranks")
            keep = L.dve(partial(V.tensor_scalar, pm[:, 4, :], pm[:, 3, :], float(CAP), None, ALU.is_lt),
                         (c,), "ranks")
            a = L.dve(partial(V.scalar_tensor_tensor, pm[:, 5, :], pm[:, 2, :], float(CAP), pm[:, 3, :], ALU.mult,
                              ALU.add), (keep,), "ranks")
            a = L.dve(partial(V.tensor_tensor, pm[:, 6, :], pm[:, 5, :], idx[:, :], ALU.subtract), (a,), "ranks")
            a = L.dve(partial(V.tensor_tensor, pm[:, 6, :], pm[:, 6, :], pm[:, 4, :], ALU.mult), (a,), "ranks")
            a = L.dve(partial(V.tensor_tensor, slot[:, 0, :], pm[:, 6, :], idx[:, :], ALU.add), (a,), "ranks")
            a = L.dve(partial(V.tensor_tensor, slot[:, 1, :], pm[:, 5, :], pm[:, 4, :], ALU.mult), (a,), "ranks")
            a = L.dve(partial(V.tensor_tensor, pm[:, 5, :], pm[:, 4, :], pm[:, 1, :], ALU.mult), (a,), "ranks")
            ranked = L.dve(partial(V.tensor_tensor, pm[:, 6, :], pm[:, 1, :], pm[:, 5, :], ALU.subtract), (a,),
                           "ranks")
            yield
            for t in range(NT):
                L.put(POOL, partial(G.indirect_dma_start, slot_rows,
                                    bass.IndirectOffsetOnAxis(slot[:, 0, t:t + 1], axis=0), xf[:, t, :], None),
                      (ranked, L.stores["slot_zero"]), "to_slots", 16)
                own = L.dve(partial(V.scalar_tensor_tensor, x2[:, t, :], xf[:, t, :], pm[:, 6, t:t + 1],
                                    x2[:, t, :], ALU.mult, ALU.add), (ranked,), "own")
            placed = ("to_slots", L.count["to_slots"])
            rt.close()
            routed = fence()
            area.clear(NT * D)
            sT = area.take([128, KD, SLOTS])
            sr = Ring([sb(sp, f"sr{i}", [P, D]) for i in range(FETCHES)], routed)
            weights_in(2)
            for t in range(ST):
                ri, r, free = sr.take()
                got = L.load(r[0:SP, :], slot_rows[t * SP:(t + 1) * SP, :], (*free, placed), f"rows_in{ri}")
                for g in range(KD // 3):
                    bi, b, free = banks.take()
                    for k in range(3):
                        kk = 3 * g + k
                        tt = L.pe(partial(T.transpose, b[:, k * SP:(k + 1) * SP], r[0:SP, kk * 128:(kk + 1) * 128],
                                          ident[0:SP, 0:SP]), (*free, got), "turned" if k == 2 else None)
                    bv = b[:, 0:3 * SP].rearrange("p (k n) -> p k n", k=3)
                    dst = sT[:, 3 * g:3 * g + 3, t * SP:(t + 1) * SP]
                    if g:
                        d = L.dve(partial(V.tensor_copy, dst, bv), (tt, *routed), "xf_turned")
                    else:
                        d = L.act(partial(A.activation, dst, bv, ACT.Copy), (tt, *routed), "xf_turned_act")
                    banks.give(bi, d)
                sr.give(ri, tt)
            sT_done = ("xf_turned", L.count["xf_turned"]), ("xf_turned_act", L.count["xf_turned_act"])

            def hidden(e):
                i1, w1b, g1 = ws[e][0]
                hi_, h, h_free = hT.take()
                for f in range(KF):
                    bi, b, free = banks.take()
                    for k in range(KD):
                        mm = L.pe(partial(T.matmul, b[:, 0:CAP], w1b[:, k, f * 128:(f + 1) * 128],
                                          sT[:, k, e * CAP:(e + 1) * CAP], start=k == 0, stop=k == KD - 1),
                                  (*free, g1, *sT_done), "w1_mm" if k == KD - 1 else None)
                    a = L.act(partial(A.activation, h[:, f, :], b[:, 0:CAP], ACT.Gelu, bias=b1c[:, e, f:f + 1]),
                              (mm, g_b1, *h_free), "gelu")
                    banks.give(bi, a)
                w1s.give(i1, mm)
                hs[e] = (hi_, h, a)

            def expert_out(e):
                _, (i2, w2b, g2), (i3, br, g3) = ws.pop(e)
                hi_, h, ready = hs.pop(e)
                for r0, r1 in ((0, (CAP + 1) // 2), ((CAP + 1) // 2, CAP)):
                    oi, ob, o_free = orow.take()
                    for half in range(2):
                        cs = slice(half * (D // 2), (half + 1) * (D // 2))
                        bi, b, free = banks.take()
                        for f in range(KF):
                            mm = L.pe(partial(T.matmul, b[0:r1 - r0, 0:D // 2], h[:, f, r0:r1], w2b[:, f, cs],
                                              start=f == 0, stop=f == KF - 1), (*free, ready, g2),
                                      "w2_mm" if f == KF - 1 else None)
                        a = L.dve(partial(V.tensor_tensor, ob[0:r1 - r0, cs], b[0:r1 - r0, 0:D // 2],
                                          br[0:r1 - r0, cs], ALU.add), (mm, g3, *o_free), "expert_row")
                        banks.give(bi, a)
                    o = L.store(expert_rows[e * CAP + r0:e * CAP + r1, :], ob[0:r1 - r0, :], (a,),
                                f"expert_out{oi}")
                    orow.give(oi, o)
                hT.give(hi_, mm)
                w2s.give(i2, mm)
                b2r.give(i3, a)
                if e + 3 < EXPERTS:
                    weights_in(e + 3)

            yield from in_step([(0, hidden), (1, expert_out)], EXPERTS)
            stored = (L.stores["expert_out0"], L.stores["expert_out1"])
            for t in range(NT):
                fi, f, free = sr.take()
                got = L.put(POOL, partial(G.indirect_dma_start, f[:, :], None, expert_rows,
                                          bass.IndirectOffsetOnAxis(slot[:, 1, t:t + 1], axis=0)),
                            (*free, *stored, ranked), f"fetch{fi}", 16)
                a = L.dve(partial(V.scalar_tensor_tensor, f[:, :], f[:, :], pm[:, 5, t:t + 1],
                                  x2[:, t, :], ALU.mult, ALU.add),
                          (got, own), "result")
                o = L.store(out[t * P:(t + 1) * P, :], f[:, :], (a,), f"result_out{fi}")
                sr.give(fi, o)
                yield

        sg, sx = ExitStack(), ExitStack()
        of_experts = []

        def attention_then_loads():
            yield from graph_attention(bank[0:3], sg, end2)
            sg.close()
            s_edges.close()
            for _ in range(LOAD_DELAY):
                yield
            of_experts.append(experts(sx, fence()))
            while next(of_experts[0]) != "loaded":
                yield

        run((attention_then_loads(), 1), (mix_then_nodes(end2), MIX_RATE))
        run((of_experts[0], 1))
        sx.close()
        for token in L.stores.values():
            L.put(SYNC, None, (token,))
        block = ctx.enter_context(nc.Block())
        L.emit(block)


_SHAPE = (N, D)


def kernel(**inputs):
    import numpy as _np
    import concourse.bacc as _bacc
    from concourse import mybir as _mybir
    from concourse.bass_utils import run_bass_kernel_spmd as _run

    g = {k: _np.asarray(v) for k, v in inputs.items()}
    laid = {
        "x": g["x"], "src_rows": g["src"], "dst_rows": g["dst"],
        "src_cols": g["src"].reshape(CHUNKS, P).T, "dst_cols": g["dst"].reshape(CHUNKS, P).T,
        "W_ah": g["L0_gnn_W_ah"], "b_ah": g["L0_gnn_b_ah"].reshape(KD, 128).T,
        "W0": g["L0_gnn_W0"], "W1": g["L0_gnn_W1"], "W2": g["L0_gnn_W2"],
        "a_src": _np.stack([g[f"L0_gnn_a_src{i}"] for i in range(LAYERS)]),
        "a_dst": _np.stack([g[f"L0_gnn_a_dst{i}"] for i in range(LAYERS)]),
        "bg": _np.stack([g[f"L0_gnn_b{i}"] for i in range(LAYERS)]),
        "W_out": g["L0_gnn_W_out"], "b_out": g["L0_gnn_b_out"],
        "wT_qkv": g["L0_mix_w_qkv"].T, "wT_proj": g["L0_mix_w_proj"].T, "b_proj": g["L0_mix_b_proj"],
        "projT": g["L0_mix_proj_mat"].T, "switch_w": g["L0_ffn_switch_w"], "switch_b": g["L0_ffn_switch_b"],
        "w1": g["L0_ffn_w1"], "b1_cols": g["L0_ffn_b1"].reshape(EXPERTS, KF, 128).transpose(2, 0, 1),
        "w2": g["L0_ffn_w2"], "b2": g["L0_ffn_b2"],
    }
    nc = _bacc.Bacc("TRN2", target_bir_lowering=False, num_devices=1)
    arrays, ap = {}, {}
    for name, a in laid.items():
        a = _np.ascontiguousarray(a)
        arrays[f"in_{name}"] = a
        ap[name] = nc.dram_tensor(f"in_{name}", a.shape, _mybir.dt.from_np(a.dtype), kind="ExternalInput").ap()
    out = nc.dram_tensor("out_x", _SHAPE, _mybir.dt.float32, kind="ExternalOutput").ap()
    program(nc, ap["x"], ap["src_rows"], ap["dst_rows"], ap["src_cols"], ap["dst_cols"], ap["W_ah"], ap["b_ah"],
            [ap["W0"], ap["W1"], ap["W2"]], ap["a_src"], ap["a_dst"], ap["bg"], ap["W_out"], ap["b_out"],
            ap["wT_qkv"], ap["wT_proj"], ap["b_proj"], ap["projT"], ap["switch_w"], ap["switch_b"], ap["w1"],
            ap["b1_cols"], ap["w2"], ap["b2"], out)
    r = _run(nc, [arrays], core_ids=[0])
    return r.results[0]["out_x"]
```
